# Optimizing a Trainium2 kernel written in Bass

```python
import numpy as np
import jax
import jax.numpy as jnp

def _softmax(x, axis=-1):
    return jax.nn.softmax(x, axis=axis)

def _gelu(x):
    return jax.nn.gelu(x, approximate=True)

def _silu(x):
    return jax.nn.silu(x)

def _sigmoid(x):
    return jax.nn.sigmoid(x)

def _layernorm(x, axis=-1, eps=1e-05):
    m = jnp.mean(x, axis=axis, keepdims=True)
    v = jnp.var(x, axis=axis, keepdims=True)
    return (x - m) / jnp.sqrt(v + eps)

def _scatter_add(tgt, idx, src, axis=0):
    return tgt.at[idx].add(src)

def _segment_sum(src, seg, n):
    return jax.ops.segment_sum(src, seg, n)
kernel_name = 'mk_decoder_postln_d2_seqx_r4_41d80c'

def setup_inputs(seed: int=0):
    np.random.seed(seed)
    _w = jnp.asarray

    def _rec_inputs():
        import jax
        import jax.numpy as jnp
        _rk = jax.random.key(seed)
        x = 7.22e-05 + 1 * jax.random.normal(jax.random.fold_in(_rk, 1), (16, 100, 256), jnp.float32)
        _lenS = 100 - jax.random.randint(jax.random.fold_in(_rk, 7), (16,), 0, max(1, 100 // 4) + 1, jnp.int32)
        _lenS2 = 361 - jax.random.randint(jax.random.fold_in(_rk, 8), (16,), 0, max(1, 361 // 4) + 1, jnp.int32)
        _ctx_1024P = jax.random.normal(jax.random.fold_in(_rk, 11), (16, 16, 256), jnp.float32)
        _ctx_1024c = jax.random.dirichlet(jax.random.fold_in(_rk, 511), 0.3 * jnp.ones((16,), jnp.float32), (16, 361))
        _ctx_1024t = jnp.einsum('bsk,bkd->bsd', _ctx_1024c, _ctx_1024P)
        _ctx_1024t = _ctx_1024t * jax.lax.rsqrt(jnp.mean(jnp.square(_ctx_1024t)) + 1e-12) * 0.953939
        ctx_1024 = 4.13588e-05 + 0.999923 * (_ctx_1024t + 0.3 * jax.random.normal(jax.random.fold_in(_rk, 611), (16, 361, 256), jnp.float32))
        _validS = jnp.arange(100)[None, :] < _lenS[:, None]
        _validS2 = jnp.arange(361)[None, :] < _lenS2[:, None]
        _causal = jnp.tril(jnp.ones((100, 100), dtype=bool))
        mask_Bx1xSxS2_ik1 = jnp.where(jnp.broadcast_to(_validS2[:, None, None, :], (16, 1, 100, 361)), 1, 0).astype(jnp.int32)
        return (x, ctx_1024, mask_Bx1xSxS2_ik1)
    x, ctx_1024, mask_Bx1xSxS2_ik1 = _rec_inputs()

    def _L0_attn_setup():
        import jax, jax.numpy as jnp
        import numpy as np
        B, M, D, H = (2, 512, 256, 16)

        def _rope(x):
            b, m, d = x.shape
            i = jnp.arange(d // 2, dtype=jnp.float32)
            theta = 10000.0 ** (-2.0 * (i - 1.0) / d)
            ang = jnp.arange(m, dtype=jnp.float32)[:, None] * theta[None, :]
            c, s = (jnp.cos(ang), jnp.sin(ang))
            xe, xo = (x[..., 0::2], x[..., 1::2])
            ye = xe * c + xo * s
            yo = -xe * s + xo * c
            return jnp.stack([ye, yo], axis=-1).reshape(b, m, d)
        key = jax.random.key(seed)
        ks = jax.random.split(key, 8)
        w = lambda k, shape: jax.random.normal(k, shape, jnp.float32) * 0.02
        return {'x': jax.random.normal(ks[0], (B, M, D), jnp.float32), 'wq': w(ks[1], (D, D)), 'wk': w(ks[2], (D, D)), 'wv': w(ks[3], (D, D)), 'in_proj_w': w(ks[4], (3 * D, D)), 'in_proj_b': w(ks[5], (3 * D,)), 'out_w': w(ks[6], (D, D)), 'out_b': w(ks[7], (D,))}
    _L0_attn_all = _L0_attn_setup()
    _L0_attn_in = {k: v for k, v in _L0_attn_all.items() if k in ('wq', 'wk', 'wv', 'in_proj_w', 'in_proj_b', 'out_w', 'out_b')}
    del _L0_attn_all

    def _L0_xattn_setup():
        import jax, jax.numpy as jnp
        import numpy as np
        D_MODEL = 256
        NUM_HEADS = 16
        DEPTH = D_MODEL // NUM_HEADS

        def _split_heads(x, B):
            return x.reshape(B, -1, NUM_HEADS, DEPTH).transpose(0, 2, 1, 3)
        key = jax.random.key(seed)
        ks = jax.random.split(key, 11)
        B, S = (4, 512)
        scale = 1.0 / np.sqrt(D_MODEL)
        inp = {'query': jax.random.normal(ks[0], (B, S, D_MODEL), jnp.float32), 'key': jax.random.normal(ks[1], (B, S, D_MODEL), jnp.float32), 'value': jax.random.normal(ks[2], (B, S, D_MODEL), jnp.float32), 'wq_w': jax.random.normal(ks[3], (D_MODEL, D_MODEL), jnp.float32) * scale, 'wq_b': jnp.zeros((D_MODEL,), jnp.float32), 'wk_w': jax.random.normal(ks[4], (D_MODEL, D_MODEL), jnp.float32) * scale, 'wk_b': jnp.zeros((D_MODEL,), jnp.float32), 'wv_w': jax.random.normal(ks[5], (D_MODEL, D_MODEL), jnp.float32) * scale, 'wv_b': jnp.zeros((D_MODEL,), jnp.float32), 'dense_w': jax.random.normal(ks[6], (D_MODEL, D_MODEL), jnp.float32) * scale, 'dense_b': jnp.zeros((D_MODEL,), jnp.float32)}
        return inp
    _L0_xattn_all = _L0_xattn_setup()
    _L0_xattn_in = {k: v for k, v in _L0_xattn_all.items() if k in ('wq_w', 'wq_b', 'wk_w', 'wk_b', 'wv_w', 'wv_b', 'dense_w', 'dense_b')}
    del _L0_xattn_all

    def _L0_ffn_setup():
        import jax, jax.numpy as jnp
        import numpy as np
        B, L, D, E, K, DFF = (2, 512, 256, 8, 2, 1024)
        key = jax.random.key(seed)
        kx, kr, kg, ku, kd = jax.random.split(key, 5)
        scale = 0.02
        return {'x': jax.random.normal(kx, (B, L, D), dtype=jnp.float32), 'Wr': jax.random.normal(kr, (E, D), dtype=jnp.float32) * scale, 'Wg': jax.random.normal(kg, (E, DFF, D), dtype=jnp.float32) * scale, 'Wu': jax.random.normal(ku, (E, DFF, D), dtype=jnp.float32) * scale, 'Wd': jax.random.normal(kd, (E, D, DFF), dtype=jnp.float32) * scale}
    _L0_ffn_all = _L0_ffn_setup()
    _L0_ffn_in = {k: v for k, v in _L0_ffn_all.items() if k in ('Wr', 'Wg', 'Wu', 'Wd')}
    del _L0_ffn_all

    def _L1_attn_setup():
        import jax, jax.numpy as jnp
        import numpy as np
        B, S, D = (4, 1024, 256)
        key = jax.random.key(seed)
        ks = jax.random.split(key, 7)
        scale = 1.0 / np.sqrt(D)
        return {'x': jax.random.normal(ks[0], (B, S, D), dtype=jnp.float32), 'W_in': jax.random.normal(ks[1], (D, D), dtype=jnp.float32) * scale, 'W_select': jax.random.normal(ks[2], (D, D), dtype=jnp.float32) * scale, 'W_gate': jax.random.normal(ks[3], (D, D), dtype=jnp.float32) * scale, 'W_out': jax.random.normal(ks[4], (D, D), dtype=jnp.float32) * scale, 'W_delta': jax.random.normal(ks[5], (D, D), dtype=jnp.float32) * scale, 'log_a': jax.random.normal(ks[6], (D,), dtype=jnp.float32) * 0.1}
    _L1_attn_all = _L1_attn_setup()
    _L1_attn_in = {k: v for k, v in _L1_attn_all.items() if k in ('W_in', 'W_select', 'W_gate', 'W_out', 'W_delta', 'log_a')}
    del _L1_attn_all

    def _L1_xattn_setup():
        import jax, jax.numpy as jnp
        import numpy as np
        D_MODEL = 256
        NUM_HEAD = 16
        D_K = D_MODEL // NUM_HEAD

        def _split_heads(x):
            b, s, _ = x.shape
            return x.reshape(b, s, NUM_HEAD, D_K).transpose(0, 2, 1, 3)
        key = jax.random.key(seed)
        ks = jax.random.split(key, 13)
        B, S = (2, 512)
        s = 1.0 / np.sqrt(D_MODEL)
        return {'q': jax.random.normal(ks[0], (B, S, D_MODEL), jnp.float32), 'k': jax.random.normal(ks[1], (B, S, D_MODEL), jnp.float32), 'v': jax.random.normal(ks[2], (B, S, D_MODEL), jnp.float32), 'mask': jax.random.randint(ks[3], (B, 1, S, S), 0, 2, jnp.int32), 'wq': jax.random.normal(ks[4], (D_MODEL, D_MODEL), jnp.float32) * s, 'bq': jax.random.normal(ks[5], (D_MODEL,), jnp.float32) * 0.02, 'wk': jax.random.normal(ks[6], (D_MODEL, D_MODEL), jnp.float32) * s, 'bk': jax.random.normal(ks[7], (D_MODEL,), jnp.float32) * 0.02, 'wv': jax.random.normal(ks[8], (D_MODEL, D_MODEL), jnp.float32) * s, 'bv': jax.random.normal(ks[9], (D_MODEL,), jnp.float32) * 0.02, 'wo': jax.random.normal(ks[10], (D_MODEL, D_MODEL), jnp.float32) * s, 'bo': jax.random.normal(ks[11], (D_MODEL,), jnp.float32) * 0.02}
    _L1_xattn_all = _L1_xattn_setup()
    _L1_xattn_in = {k: v for k, v in _L1_xattn_all.items() if k in ('wq', 'bq', 'wk', 'bk', 'wv', 'bv', 'wo', 'bo')}
    del _L1_xattn_all

    def _L1_ffn_setup():
        import jax, jax.numpy as jnp
        import numpy as np
        IN_DIM = 256
        HIDDEN = 256
        OUT_DIM = 256
        NUM_EXPERTS = 16
        TOP_K = 2
        ROUTER_TEMP = 1.0
        LN_EPS = 1e-05

        def _layernorm(h, g, b):
            mu = jnp.mean(h, axis=-1, keepdims=True)
            var = jnp.mean(jnp.square(h - mu), axis=-1, keepdims=True)
            return (h - mu) * jax.lax.rsqrt(var + LN_EPS) * g + b
        key = jax.random.key(seed)
        ks = jax.random.split(key, 8)
        s_in = 1.0 / np.sqrt(IN_DIM)
        s_h = 1.0 / np.sqrt(HIDDEN)
        x = jax.random.normal(ks[0], (4, 512, IN_DIM), dtype=jnp.float32)
        Wr = jax.random.uniform(ks[1], (IN_DIM, NUM_EXPERTS), jnp.float32, -s_in, s_in)
        br = jax.random.uniform(ks[2], (NUM_EXPERTS,), jnp.float32, -s_in, s_in)
        W1 = jax.random.uniform(ks[3], (NUM_EXPERTS, IN_DIM, HIDDEN), jnp.float32, -s_in, s_in)
        b1 = jax.random.uniform(ks[4], (NUM_EXPERTS, HIDDEN), jnp.float32, -s_in, s_in)
        g1 = jnp.ones((NUM_EXPERTS, HIDDEN), jnp.float32)
        be1 = jnp.zeros((NUM_EXPERTS, HIDDEN), jnp.float32)
        W2 = jax.random.uniform(ks[5], (NUM_EXPERTS, HIDDEN, OUT_DIM), jnp.float32, -s_h, s_h)
        b2 = jax.random.uniform(ks[6], (NUM_EXPERTS, OUT_DIM), jnp.float32, -s_h, s_h)
        return {'x': x, 'Wr': Wr, 'br': br, 'W1': W1, 'b1': b1, 'g1': g1, 'be1': be1, 'W2': W2, 'b2': b2}
    _L1_ffn_all = _L1_ffn_setup()
    _L1_ffn_in = {k: v for k, v in _L1_ffn_all.items() if k in ('Wr', 'br', 'W1', 'b1', 'g1', 'be1', 'W2', 'b2')}
    del _L1_ffn_all
    return {'x': x, 'ctx_1024': ctx_1024, 'mask_Bx1xSxS2_ik1': mask_Bx1xSxS2_ik1, 'L0_attn_wq': _L0_attn_in['wq'], 'L0_attn_wk': _L0_attn_in['wk'], 'L0_attn_wv': _L0_attn_in['wv'], 'L0_attn_in_proj_w': _L0_attn_in['in_proj_w'], 'L0_attn_in_proj_b': _L0_attn_in['in_proj_b'], 'L0_attn_out_w': _L0_attn_in['out_w'], 'L0_attn_out_b': _L0_attn_in['out_b'], 'L0_xattn_wq_w': _L0_xattn_in['wq_w'], 'L0_xattn_wq_b': _L0_xattn_in['wq_b'], 'L0_xattn_wk_w': _L0_xattn_in['wk_w'], 'L0_xattn_wk_b': _L0_xattn_in['wk_b'], 'L0_xattn_wv_w': _L0_xattn_in['wv_w'], 'L0_xattn_wv_b': _L0_xattn_in['wv_b'], 'L0_xattn_dense_w': _L0_xattn_in['dense_w'], 'L0_xattn_dense_b': _L0_xattn_in['dense_b'], 'L0_ffn_Wr': _L0_ffn_in['Wr'], 'L0_ffn_Wg': _L0_ffn_in['Wg'], 'L0_ffn_Wu': _L0_ffn_in['Wu'], 'L0_ffn_Wd': _L0_ffn_in['Wd'], 'L1_attn_W_in': _L1_attn_in['W_in'], 'L1_attn_W_select': _L1_attn_in['W_select'], 'L1_attn_W_gate': _L1_attn_in['W_gate'], 'L1_attn_W_out': _L1_attn_in['W_out'], 'L1_attn_W_delta': _L1_attn_in['W_delta'], 'L1_attn_log_a': _L1_attn_in['log_a'], 'L1_xattn_wq': _L1_xattn_in['wq'], 'L1_xattn_bq': _L1_xattn_in['bq'], 'L1_xattn_wk': _L1_xattn_in['wk'], 'L1_xattn_bk': _L1_xattn_in['bk'], 'L1_xattn_wv': _L1_xattn_in['wv'], 'L1_xattn_bv': _L1_xattn_in['bv'], 'L1_xattn_wo': _L1_xattn_in['wo'], 'L1_xattn_bo': _L1_xattn_in['bo'], 'L1_ffn_Wr': _L1_ffn_in['Wr'], 'L1_ffn_br': _L1_ffn_in['br'], 'L1_ffn_W1': _L1_ffn_in['W1'], 'L1_ffn_b1': _L1_ffn_in['b1'], 'L1_ffn_g1': _L1_ffn_in['g1'], 'L1_ffn_be1': _L1_ffn_in['be1'], 'L1_ffn_W2': _L1_ffn_in['W2'], 'L1_ffn_b2': _L1_ffn_in['b2']}

def reference(x, ctx_1024, mask_Bx1xSxS2_ik1, L0_attn_wq, L0_attn_wk, L0_attn_wv, L0_attn_in_proj_w, L0_attn_in_proj_b, L0_attn_out_w, L0_attn_out_b, L0_xattn_wq_w, L0_xattn_wq_b, L0_xattn_wk_w, L0_xattn_wk_b, L0_xattn_wv_w, L0_xattn_wv_b, L0_xattn_dense_w, L0_xattn_dense_b, L0_ffn_Wr, L0_ffn_Wg, L0_ffn_Wu, L0_ffn_Wd, L1_attn_W_in, L1_attn_W_select, L1_attn_W_gate, L1_attn_W_out, L1_attn_W_delta, L1_attn_log_a, L1_xattn_wq, L1_xattn_bq, L1_xattn_wk, L1_xattn_bk, L1_xattn_wv, L1_xattn_bv, L1_xattn_wo, L1_xattn_bo, L1_ffn_Wr, L1_ffn_br, L1_ffn_W1, L1_ffn_b1, L1_ffn_g1, L1_ffn_be1, L1_ffn_W2, L1_ffn_b2):
    import jax
    import jax.numpy as jnp

    def _L0_attn_ref(x, wq, wk, wv, in_proj_w, in_proj_b, out_w, out_b):
        import jax, jax.numpy as jnp
        import numpy as np
        B, M, D, H = (2, 512, 256, 16)

        def _rope(x):
            b, m, d = x.shape
            i = jnp.arange(d // 2, dtype=jnp.float32)
            theta = 10000.0 ** (-2.0 * (i - 1.0) / d)
            ang = jnp.arange(m, dtype=jnp.float32)[:, None] * theta[None, :]
            c, s = (jnp.cos(ang), jnp.sin(ang))
            xe, xo = (x[..., 0::2], x[..., 1::2])
            ye = xe * c + xo * s
            yo = -xe * s + xo * c
            return jnp.stack([ye, yo], axis=-1).reshape(b, m, d)
        b, m, d = x.shape
        h = H
        hd = d // h
        q = _rope(x @ wq.T)
        k = _rope(x @ wk.T)
        v = _rope(x @ wv.T)
        wqi, wki, wvi = jnp.split(in_proj_w, 3, axis=0)
        bqi, bki, bvi = jnp.split(in_proj_b, 3, axis=0)
        qh = (q @ wqi.T + bqi).reshape(b, m, h, hd)
        kh = (k @ wki.T + bki).reshape(b, m, h, hd)
        vh = (v @ wvi.T + bvi).reshape(b, m, h, hd)
        scores = jnp.einsum('bqhd,bkhd->bhqk', qh, kh) / jnp.sqrt(jnp.float32(hd))
        causal = jnp.tril(jnp.ones((m, m), dtype=bool))
        scores = jnp.where(causal, scores, jnp.float32(-jnp.inf))
        attn = jax.nn.softmax(scores, axis=-1)
        o = jnp.einsum('bhqk,bkhd->bqhd', attn, vh).reshape(b, m, d)
        return o @ out_w.T + out_b

    def _L0_xattn_ref(query, key, value, wq_w, wq_b, wk_w, wk_b, wv_w, wv_b, dense_w, dense_b):
        import jax, jax.numpy as jnp
        import numpy as np
        D_MODEL = 256
        NUM_HEADS = 16
        DEPTH = D_MODEL // NUM_HEADS

        def _split_heads(x, B):
            return x.reshape(B, -1, NUM_HEADS, DEPTH).transpose(0, 2, 1, 3)
        B = query.shape[0]
        q = _split_heads(query @ wq_w.T + wq_b, B)
        k = _split_heads(key @ wk_w.T + wk_b, B)
        v = _split_heads(value @ wv_w.T + wv_b, B)
        scores = jnp.einsum('bhqd,bhkd->bhqk', q, k) / jnp.sqrt(jnp.float32(DEPTH)).astype(q.dtype)
        attn = jax.nn.softmax(scores, axis=-1)
        out = jnp.einsum('bhqk,bhkd->bhqd', attn, v)
        out = out.transpose(0, 2, 1, 3).reshape(B, -1, D_MODEL)
        return out @ dense_w.T + dense_b

    def _L0_ffn_ref(x, Wr, Wg, Wu, Wd):
        import jax, jax.numpy as jnp
        import numpy as np
        B, L, D, E, K, DFF = (2, 512, 256, 8, 2, 1024)
        Bb, Ll, Dd = x.shape
        T = Bb * Ll
        xt = x.reshape(T, Dd)
        logits = jnp.einsum('td,ed->te', xt, Wr)
        scores = jax.nn.softmax(logits, axis=-1)
        k_scores, k_ids = jax.lax.top_k(scores, K)
        eps = jnp.finfo(x.dtype).eps
        k_w = k_scores / (k_scores.sum(axis=-1, keepdims=True) + eps)
        combine = jnp.sum(jax.nn.one_hot(k_ids, E, dtype=x.dtype) * k_w[..., None], axis=1)
        g = jnp.einsum('td,efd->etf', xt, Wg)
        u = jnp.einsum('td,efd->etf', xt, Wu)
        h = jax.nn.relu(g) * u
        out_e = jnp.einsum('etf,edf->etd', h, Wd)
        out = jnp.einsum('te,etd->td', combine, out_e)
        return out.reshape(Bb, Ll, Dd)

    def _L1_attn_ref(x, W_in, W_select, W_gate, W_out, W_delta, log_a):
        import jax, jax.numpy as jnp
        import numpy as np
        B, S, D = (4, 1024, 256)
        a_base = jax.nn.sigmoid(log_a).astype(x.dtype)
        delta = jnp.maximum(jax.nn.softplus(jnp.einsum('bsd,ed->bse', x, W_delta)), 0.0001)
        decay = jnp.exp(-delta * a_base)
        update = jax.nn.sigmoid(jnp.einsum('bsd,ed->bse', x, W_select)) * jnp.tanh(jnp.einsum('bsd,ed->bse', x, W_in))
        gate = jax.nn.sigmoid(jnp.einsum('bsd,ed->bse', x, W_gate))

        def step(state, inputs):
            dec_t, upd_t = inputs
            state = dec_t * state + upd_t
            return (state, state)
        init = jnp.zeros((x.shape[0], x.shape[2]), dtype=x.dtype)
        _, states = jax.lax.scan(step, init, (decay.transpose(1, 0, 2), update.transpose(1, 0, 2)))
        states = states.transpose(1, 0, 2)
        out = gate * states
        y = jnp.einsum('bsd,ed->bse', out, W_out)
        return y

    def _L1_xattn_ref(q, k, v, mask, wq, bq, wk, bk, wv, bv, wo, bo):
        import jax, jax.numpy as jnp
        import numpy as np
        D_MODEL = 256
        NUM_HEAD = 16
        D_K = D_MODEL // NUM_HEAD

        def _split_heads(x):
            b, s, _ = x.shape
            return x.reshape(b, s, NUM_HEAD, D_K).transpose(0, 2, 1, 3)
        query = _split_heads(q @ wq + bq)
        key = _split_heads(k @ wk + bk)
        value = _split_heads(v @ wv + bv)
        scale = 1.0 / np.sqrt(D_K).astype(np.float32)
        scores = jnp.einsum('bhqd,bhkd->bhqk', query, key) * scale
        scores = jnp.where(mask == 0, -jnp.inf, scores)
        attn = jax.nn.softmax(scores, axis=-1)
        out = jnp.einsum('bhqk,bhkd->bhqd', attn, value)
        b, h, s, d = out.shape
        out = out.transpose(0, 2, 1, 3).reshape(b, s, h * d)
        return out @ wo + bo

    def _L1_ffn_ref(x, Wr, br, W1, b1, g1, be1, W2, b2):
        import jax, jax.numpy as jnp
        import numpy as np
        IN_DIM = 256
        HIDDEN = 256
        OUT_DIM = 256
        NUM_EXPERTS = 16
        TOP_K = 2
        ROUTER_TEMP = 1.0
        LN_EPS = 1e-05

        def _layernorm(h, g, b):
            mu = jnp.mean(h, axis=-1, keepdims=True)
            var = jnp.mean(jnp.square(h - mu), axis=-1, keepdims=True)
            return (h - mu) * jax.lax.rsqrt(var + LN_EPS) * g + b
        orig_shape = x.shape[:-1]
        x_flat = x.reshape(-1, x.shape[-1])
        logits = (x_flat @ Wr + br) / max(ROUTER_TEMP, 1e-06)
        probs = jax.nn.softmax(logits, axis=-1)
        topk_w, topk_idx = jax.lax.top_k(probs, TOP_K)
        topk_w = topk_w / jnp.clip(jnp.sum(topk_w, axis=-1, keepdims=True), 1e-09)
        h = jnp.einsum('nc,ech->neh', x_flat, W1) + b1
        h = _layernorm(h, g1, be1)
        h = jax.nn.gelu(h, approximate=False)
        expert_out = jnp.einsum('neh,eho->neo', h, W2) + b2
        sel = jnp.take_along_axis(expert_out, topk_idx[:, :, None], axis=1)
        y_flat = jnp.sum(sel * topk_w[:, :, None], axis=1)
        return y_flat.reshape(*orig_shape, y_flat.shape[-1])
    x = _layernorm(x + _L0_attn_ref(x, L0_attn_wq, L0_attn_wk, L0_attn_wv, L0_attn_in_proj_w, L0_attn_in_proj_b, L0_attn_out_w, L0_attn_out_b), axis=-1)
    x = _layernorm(x + _L0_xattn_ref(x, ctx_1024, ctx_1024, L0_xattn_wq_w, L0_xattn_wq_b, L0_xattn_wk_w, L0_xattn_wk_b, L0_xattn_wv_w, L0_xattn_wv_b, L0_xattn_dense_w, L0_xattn_dense_b), axis=-1)
    x = _layernorm(x + _L0_ffn_ref(x, L0_ffn_Wr, L0_ffn_Wg, L0_ffn_Wu, L0_ffn_Wd), axis=-1)
    x = _layernorm(x + _L1_attn_ref(x, L1_attn_W_in, L1_attn_W_select, L1_attn_W_gate, L1_attn_W_out, L1_attn_W_delta, L1_attn_log_a), axis=-1)
    x = _layernorm(x + _L1_xattn_ref(x, ctx_1024, ctx_1024, mask_Bx1xSxS2_ik1, L1_xattn_wq, L1_xattn_bq, L1_xattn_wk, L1_xattn_bk, L1_xattn_wv, L1_xattn_bv, L1_xattn_wo, L1_xattn_bo), axis=-1)
    x = _layernorm(x + _L1_ffn_ref(x, L1_ffn_Wr, L1_ffn_br, L1_ffn_W1, L1_ffn_b1, L1_ffn_g1, L1_ffn_be1, L1_ffn_W2, L1_ffn_b2), axis=-1)
    return x

_drawn_inputs = setup_inputs


def setup_inputs(seed=0):
    import zlib

    import numpy as np

    out = dict(_drawn_inputs(seed))
    spreads = {'L0_xattn_wq_b': (0.0, 0.1),
     'L0_xattn_wk_b': (0.0, 0.8),
     'L0_xattn_wv_b': (0.0, 0.1),
     'L0_xattn_dense_b': (0.0, 0.1),
     'L1_ffn_g1': (1.0, 0.2),
     'L1_ffn_be1': (0.0, 0.301)}
    factors = {'L0_attn_wq': 8.0,
     'L0_attn_wk': 8.0,
     'L0_attn_wv': 3.006,
     'L0_attn_in_proj_w': 3.108,
     'L0_attn_in_proj_b': 3.491,
     'L1_xattn_bq': 3.931,
     'L1_xattn_bk': 8.0,
     'L1_ffn_b1': 3.201}
    for name, (base, spread) in spreads.items():
        noise = np.random.default_rng([zlib.crc32(name.encode()), seed]).standard_normal(out[name].shape)
        drawn = base * np.exp(spread * noise) if base else spread * noise
        out[name] = jnp.asarray(drawn.astype(out[name].dtype))
    for name, factor in factors.items():
        out[name] = (out[name] * factor).astype(out[name].dtype)
    return out
```

```python
from contextlib import ExitStack

import numpy as np

import concourse.bass as bass
from concourse import mybir

F32 = mybir.dt.float32
BF16 = mybir.dt.bfloat16
I32 = mybir.dt.int32
U32 = mybir.dt.uint32
ALU = mybir.AluOpType
ACT = mybir.ActivationFunctionType
AX = mybir.AxisListType

P = 128
SEQS = 16
ROWS = 100
D = 256
KC = D // P
HEADS = 16
HD = D // HEADS
HPC = P // HD
KEYS = 361
KT = [(0, 121), (121, 120), (241, 120)]
KTW = 121
BANK = 512
VW = 32
MASKED = -1e30
LN_EPS = 1e-5
E0, F0 = 8, 1024
E1, F1 = 16, 256
PAIRS = SEQS * ROWS * 2
FFN0_TILES = (PAIRS + E0 * (P - 1)) // P
FFN1_TILES = (PAIRS + E1 * (P - 1)) // P
F32_EPS = float(np.finfo(np.float32).eps)


def need(eng, sem, count):
    if isinstance(count, int) and count <= 0:
        return
    eng.wait_ge(sem, count)


def steps(eng, body):
    body(-1, -1, 1, True, False, False)
    body(0, 0, 0, True, True, False)
    with eng.Fori(0, (SEQS - 2) // 2) as it:
        body(2 * it + 1, it, 1, True, True, True)
        body(2 * it + 2, it + 1, 0, True, True, True)
    body(SEQS - 1, SEQS // 2 - 1, 1, False, True, True)
    body(SEQS, SEQS // 2, 0, False, False, True)


def landed(half):
    return 16 * (half + 1)


class Stage:

    def __init__(self, nc, name):
        self.nc, self.name, self.stack, self.sems = nc, name, ExitStack(), []

    def sb(self, name, shape, dt=F32):
        return self.stack.enter_context(self.nc.sbuf_tensor(f"{self.name}_{name}", shape, dt))

    def ps(self, name, shape, dt=F32):
        return self.stack.enter_context(self.nc.psum_tensor(f"{self.name}_{name}", shape, dt))

    def sem(self, name):
        self.sems.append(self.nc.alloc_semaphore(f"{self.name}_{name}"))
        return self.sems[-1]

    def block(self):
        return self.nc.Block()

    def end(self):
        self.nc.clear_and_free_semaphores(self.sems)
        self.nc.all_engine_barrier()
        self.stack.close()


def self_attention(nc, dram, x_in, x_out):
    st = Stage(nc, "sa")
    x = [st.sb(f"x{k}", [ROWS, D]) for k in (0, 1)]
    xb = st.sb("xb", [ROWS, D])
    xT = st.sb("xT", [P, KC, ROWS])
    w1 = st.sb("w1", [P, 3, KC, D])
    w2 = st.sb("w2", [P, 3, KC, D])
    wo = st.sb("wo", [P, KC, D])
    bqk = st.sb("bqk", [P, 2, KC])
    bv = st.sb("bv", [P, D])
    bo = st.sb("bo", [P, D])
    ident = st.sb("ident", [P, P])
    identb = st.sb("identb", [P, P], BF16)
    causal = st.sb("causal", [ROWS, ROWS])
    causalb = st.sb("causalb", [ROWS, 4, ROWS], BF16)
    cs = st.sb("cs", [P, 2, ROWS])
    hm = st.sb("hm", [P, HPC])
    pc = st.sb("pc", [P, 3, 2, ROWS])
    psn = st.sb("psn", [P, 3, 2, ROWS])
    rot = st.sb("rot", [P, 3, KC, ROWS])
    qT = st.sb("qT", [P, KC, ROWS])
    kT = st.sb("kT", [P, KC, ROWS])
    qm = st.sb("qm", [P, KC, HPC, ROWS])
    va = st.sb("va", [ROWS, HEADS, VW])
    mx = st.sb("mx", [ROWS, HEADS])
    sh = st.sb("sh", [ROWS, HEADS, ROWS])
    pr = st.sb("pr", [ROWS, HEADS, ROWS])
    pT = st.sb("pT", [ROWS, HEADS, ROWS])
    oT = st.sb("oT", [P, 4, ROWS])
    rden = st.sb("rden", [ROWS, HEADS])
    o = st.sb("o", [ROWS, D])
    oT2 = st.sb("oT2", [P, KC, ROWS])
    y = st.sb("y", [ROWS, D])
    stat = st.sb("stat", [ROWS, 6])
    mv = st.sb("mv", [ROWS, 2])
    ve = st.sb("ve", [ROWS, 1])
    rstd = st.sb("rstd", [ROWS, 1])
    tick = st.sb("tick", [ROWS, 1])
    minus_half = st.sb("minus_half", [P, 1])
    xo = [st.sb(f"xo{k}", [ROWS, D]) for k in (0, 1)]

    ps_s = st.ps("ps_s", [P, 4, BANK])
    ps_t = st.ps("ps_t", [P, 2, BANK])
    ps_p = st.ps("ps_p", [P, 2, BANK])
    prj = ps_p[:, :, :].rearrange("p a b -> p (a b)")[:, 0:3 * D].rearrange("p (w n) -> p w n", w=3)[:, :, 0:KC * ROWS]

    s = {n: st.sem(n) for n in (
        "w_in", "const", "zeros", "xT_ps", "xT_sb", "prj1", "rope_mul", "rope", "qk_ps", "v_ps", "q_sb",
        "k_sb", "v_sb", "qm", "xb", "scores", "max", "shifted", "probs", "pt_ps", "pt_even", "pt_odd", "o_ps", "oT_sb",
        "otr_ps", "rden", "o_sb", "oT2_ps", "oT2_sb", "y_ps", "y_sb", "stat", "mv", "ve", "rstd", "xo")}
    x_landed = [st.sem(f"x_landed{k}") for k in (0, 1)]
    stored = [st.sem(f"stored{k}") for k in (0, 1)]

    with st.block() as block:
        @block.sync
        def _(sp):
            def load(t, a):
                sp.dma_start(t, a).then_inc(s["w_in"], 16)
            load(w1[:, :, :, :], dram["sa_w1"])
            load(ident[:, :], dram["ident"])
            load(cs[:, :, :], dram["rope"])
            load(w2[:, :, :, :], dram["sa_w2"])
            load(hm[:, :], dram["head_mask"])
            load(bqk[:, :, :], dram["sa_bqk"])
            load(bv[:, :], dram["sa_bv"])
            load(bo[:, :], dram["sa_bo"])
            load(wo[:, :, :], dram["sa_wo"])
            load(causal[:, :], dram["causal"])

            def body(i, half, par, pre, main, post):
                if pre:
                    need(sp, s["xb"], i)
                    sp.dma_start(x[1 - par][:, :], x_in[i + 1]).then_inc(x_landed[1 - par], 16)
                if post:
                    need(sp, s["xo"], i)
                    sp.dma_start(x_out[i - 1], xo[1 - par][:, :]).then_inc(stored[1 - par], 16)
            steps(sp, body)
            for par in (0, 1):
                sp.wait_ge(stored[par], landed(SEQS // 2 - 1))

        @block.gpsimd
        def _(pool):
            pool.memset(minus_half[:, :], -0.5).then_inc(s["zeros"], 1)
            pool.memset(va[:, :, :], 0.0).then_inc(s["zeros"], 1)
            pool.wait_ge(s["zeros"], 2)
            pool.memset(va[:, :, HD:HD + 1], 1.0).then_inc(s["zeros"], 1)
            pool.wait_ge(s["w_in"], 160)
            pool.tensor_copy(identb[:, :], ident[:, :]).then_inc(s["const"], 1)
            pool.tensor_copy(causalb[:, :, :], causal[:, :].unsqueeze(1).to_broadcast([ROWS, 4, ROWS])).then_inc(s["const"], 1)
            pool.wait_ge(s["zeros"], 3)

            def body(i, half, par, pre, main, post):
                if pre:
                    need(pool, s["rope_mul"], i + 2)
                    need(pool, s["v_ps"], i + 1)
                    pool.tensor_tensor(rot[:, :, 0, :], pc[:, :, 0, :], psn[:, :, 1, :], ALU.add)
                    pool.tensor_tensor(rot[:, :, 1, :], pc[:, :, 1, :], psn[:, :, 0, :], ALU.subtract).then_inc(s["rope"], 1)
                    need(pool, s["q_sb"], i + 2)
                    need(pool, s["scores"], i + 1)
                    for c in range(KC):
                        done = pool.tensor_tensor(qm[:, c, :, :], qT[:, c, :].unsqueeze(1).to_broadcast([P, HPC, ROWS]),
                                                  hm[:, :].unsqueeze(2).to_broadcast([P, HPC, ROWS]), ALU.mult)
                    done.then_inc(s["qm"], 1)
                if main:
                    need(pool, x_landed[par], landed(half))
                    need(pool, s["y_sb"], i)
                    pool.tensor_tensor(xb[:, :], x[par][:, :], bo[0:ROWS, :], ALU.add).then_inc(s["xb"], 1)
                    need(pool, s["ve"], i + 1)
                    need(pool, s["xo"], i)
                    pool.tensor_tensor(rstd[:, :], ve[:, :], minus_half[0:ROWS, :], ALU.pow).then_inc(s["rstd"], 1)
            steps(pool, body)

        @block.tensor
        def _(pe):
            pe.wait_ge(s["w_in"], 160)
            pe.wait_ge(s["const"], 2)

            def body(i, half, par, pre, main, post):
                if main:
                    need(pe, s["qm"], i + 1)
                    need(pe, s["k_sb"], i + 1)
                    need(pe, s["shifted"], i)
                    for j in range(4):
                        pe.matmul(ps_s[0:ROWS, j, 0:4 * ROWS], identb[0:ROWS, 0:ROWS], causalb[:, :, :], start=True, stop=False)
                        for g in range(4):
                            h = 4 * j + g
                            done = pe.matmul(ps_s[0:ROWS, j, g * ROWS:(g + 1) * ROWS], qm[:, h // HPC, h % HPC, :],
                                             kT[:, h // HPC, :], start=False, stop=g == 3)
                    done.then_inc(s["scores"], 1)
                if pre:
                    need(pe, x_landed[1 - par], landed(half + par))
                    need(pe, s["q_sb"], i + 1)
                    need(pe, s["k_sb"], i + 1)
                    for c in range(KC):
                        done = pe.transpose(ps_p[:, 0, c * ROWS:(c + 1) * ROWS], x[1 - par][:, c * P:(c + 1) * P], ident[0:ROWS, 0:ROWS])
                    done.then_inc(s["xT_ps"], 1)
                    need(pe, s["xT_sb"], i + 2)
                    need(pe, s["v_sb"], i + 1)
                    for w in range(3):
                        for m in range(KC):
                            for c in range(KC):
                                done = pe.matmul(prj[:, w, m * ROWS:(m + 1) * ROWS], w1[:, w, c, m * P:(m + 1) * P], xT[:, c, :],
                                                 start=c == 0, stop=c == KC - 1)
                    done.then_inc(s["prj1"], 1)
                if main:
                    for j in range(4):
                        if j == 0:
                            need(pe, s["probs"], i + 1)
                            need(pe, s["oT2_sb"], i)
                        if j == 1:
                            need(pe, s["y_sb"], i)
                        if j == 2:
                            need(pe, s["pt_even"], 2 * i + 1)
                        if j == 3:
                            need(pe, s["pt_odd"], 2 * i + 1)
                        for g in range(4):
                            done = pe.transpose(ps_t[0:ROWS, j % 2, g * ROWS:(g + 1) * ROWS], pr[:, 4 * j + g, :], ident[0:ROWS, 0:ROWS])
                        done.then_inc(s["pt_ps"], 1)
                    need(pe, s["pt_even"], 2 * i + 2)
                    need(pe, s["pt_odd"], 2 * i + 2)
                    need(pe, s["v_sb"], i + 1)
                    for j in range(4):
                        for g in range(4):
                            h = 4 * j + g
                            done = pe.matmul(ps_t[g * VW:(g + 1) * VW, 0, j * ROWS:(j + 1) * ROWS], va[:, h, :], pT[:, h, :],
                                             start=True, stop=True, tile_position=(0, g * VW))
                    done.then_inc(s["o_ps"], 1)
                if pre:
                    need(pe, s["rope"], i + 2)
                    for w in range(2):
                        for m in range(KC):
                            for c in range(KC):
                                done = pe.matmul(ps_p[:, 0, (KC * w + m) * ROWS:(KC * w + m + 1) * ROWS], w2[:, w, c, m * P:(m + 1) * P],
                                                 rot[:, w, c, :], start=c == 0, stop=c == KC - 1)
                    done.then_inc(s["qk_ps"], 1)
                    for c in range(KC):
                        done = pe.matmul(ps_p[0:ROWS, 1, 0:D], rot[:, 2, c, :], w2[:, 2, c, :], start=c == 0, stop=c == KC - 1)
                    done.then_inc(s["v_ps"], 1)
                if main:
                    need(pe, s["oT_sb"], i + 1)
                    for j in range(4):
                        done = pe.transpose(ps_t[0:ROWS, 1, j * P:(j + 1) * P], oT[:, j, :], ident[:, :])
                    done.then_inc(s["otr_ps"], 1)
                    need(pe, s["o_sb"], i + 1)
                    for c in range(KC):
                        done = pe.transpose(ps_t[:, 0, c * ROWS:(c + 1) * ROWS], o[:, c * P:(c + 1) * P], ident[0:ROWS, 0:ROWS])
                    done.then_inc(s["oT2_ps"], 1)
                    need(pe, s["oT2_sb"], i + 1)
                    for c in range(KC):
                        done = pe.matmul(ps_t[0:ROWS, 1, 0:D], oT2[:, c, :], wo[:, c, :], start=c == 0, stop=c == KC - 1)
                    done.then_inc(s["y_ps"], 1)
            steps(pe, body)

        @block.scalar
        def _(act):
            act.wait_ge(s["w_in"], 160)

            def body(i, half, par, pre, main, post):
                if main:
                    need(act, s["shifted"], i + 1)
                    need(act, s["pt_ps"], 4 * i)
                    act.activation(pr[:, :, :], sh[:, :, :], ACT.Exp).then_inc(s["probs"], 1)
                    for j in (1, 3):
                        need(act, s["pt_ps"], 4 * i + j + 1)
                        if j == 1:
                            need(act, s["o_ps"], i)
                        act.activation(pT[:, 4 * j:4 * j + 4, :], ps_t[0:ROWS, 1, 0:4 * ROWS].rearrange("p (g n) -> p g n", g=4),
                                       ACT.Copy).then_inc(s["pt_odd"], 1)
                    need(act, s["o_ps"], i + 1)
                    need(act, s["otr_ps"], i)
                    act.activation(oT[:, :, :], ps_t[:, 0, 0:4 * ROWS].rearrange("p (g n) -> p g n", g=4), ACT.Copy).then_inc(s["oT_sb"], 1)
                if pre:
                    need(act, s["q_sb"], i + 2)
                    need(act, s["scores"], i + 1)
                    for c in range(KC):
                        done = act.activation(kT[:, c, :], ps_p[:, 0, (KC + c) * ROWS:(KC + c + 1) * ROWS], ACT.Identity, bias=bqk[:, 1, c:c + 1])
                    done.then_inc(s["k_sb"], 1)
                if main:
                    need(act, s["oT2_ps"], i + 1)
                    need(act, s["y_ps"], i)
                    act.activation(oT2[:, :, :], ps_t[:, 0, 0:KC * ROWS].rearrange("p (g n) -> p g n", g=KC), ACT.Copy).then_inc(s["oT2_sb"], 1)
            steps(act, body)

        @block.vector
        def _(dve):
            dve.wait_ge(s["w_in"], 160)
            dve.wait_ge(s["zeros"], 3)

            def body(i, half, par, pre, main, post):
                if main:
                    need(dve, s["scores"], i + 1)
                    grp = ps_s[0:ROWS, :, 0:4 * ROWS].rearrange("p j (g n) -> p j g n", g=4)
                    dve.tensor_reduce(mx[:, :].rearrange("p (j g) -> p j g", j=4), grp, AX.X, ALU.max).then_inc(s["max"], 1)
                    need(dve, s["max"], i + 1)
                    need(dve, s["probs"], i)
                    for j in range(4):
                        done = dve.tensor_tensor(sh[:, 4 * j:4 * j + 4, :], grp[:, j, :, :],
                                                 mx[:, 4 * j:4 * j + 4].unsqueeze(2).to_broadcast([ROWS, 4, ROWS]), ALU.subtract)
                    done.then_inc(s["shifted"], 1)
                if pre:
                    need(dve, s["xT_ps"], i + 2)
                    dve.tensor_copy(xT[:, :, :], ps_p[:, 0, 0:KC * ROWS].rearrange("p (c n) -> p c n", c=KC)).then_inc(s["xT_sb"], 1)
                    need(dve, s["prj1"], i + 2)
                    need(dve, s["rope"], i + 1)
                    for t, n in ((pc, 0), (psn, 1)):
                        for w in range(3):
                            done = dve.tensor_tensor(t[:, w, :, :], prj[:, w, :].rearrange("p (c n) -> p c n", c=KC),
                                                     cs[:, n, :].unsqueeze(1).to_broadcast([P, KC, ROWS]), ALU.mult)
                    done.then_inc(s["rope_mul"], 1)
                if main:
                    for j in (0, 2):
                        need(dve, s["pt_ps"], 4 * i + j + 1)
                        if j == 0:
                            need(dve, s["o_ps"], i)
                        dve.tensor_copy(pT[:, 4 * j:4 * j + 4, :], ps_t[0:ROWS, 0, 0:4 * ROWS].rearrange("p (g n) -> p g n", g=4)).then_inc(s["pt_even"], 1)
                if pre:
                    need(dve, s["qk_ps"], i + 2)
                    need(dve, s["qm"], i + 1)
                    for c in range(KC):
                        done = dve.tensor_scalar(qT[:, c, :], ps_p[:, 0, c * ROWS:(c + 1) * ROWS], bqk[:, 0, c:c + 1], HD ** -0.5, ALU.add, ALU.mult)
                    done.then_inc(s["q_sb"], 1)
                    need(dve, s["v_ps"], i + 2)
                    need(dve, s["o_ps"], i + 1)
                    dve.tensor_tensor(va[:, :, 0:HD], ps_p[0:ROWS, 1, 0:D].rearrange("p (h d) -> p h d", h=HEADS),
                                      bv[0:ROWS, :].rearrange("p (h d) -> p h d", h=HEADS), ALU.add).then_inc(s["v_sb"], 1)
                if main:
                    need(dve, s["otr_ps"], i + 1)
                    heads = ps_t[0:ROWS, 1, :].rearrange("p (h w) -> p h w", w=VW)
                    dve.reciprocal(rden[:, :], heads[:, :, HD]).then_inc(s["rden"], 1)
                    need(dve, s["rden"], i + 1)
                    need(dve, s["oT2_ps"], i)
                    dve.tensor_tensor(o[:, :].rearrange("p (h d) -> p h d", h=HEADS), heads[:, :, 0:HD],
                                      rden[:, :].unsqueeze(2).to_broadcast([ROWS, HEADS, HD]), ALU.mult).then_inc(s["o_sb"], 1)
                    need(dve, s["y_ps"], i + 1)
                    need(dve, s["xb"], i + 1)
                    dve.tensor_tensor(y[:, :], ps_t[0:ROWS, 1, 0:D], xb[:, :], ALU.add).then_inc(s["y_sb"], 1)
                    need(dve, s["y_sb"], i + 1)
                    dve.bn_stats(stat[:, :], y[:, :]).then_inc(s["stat"], 1)
                    need(dve, s["stat"], i + 1)
                    dve.memset(tick[:, :], 0.0)
                    dve.bn_aggr(mv[:, :], stat[:, :]).then_inc(s["mv"], 1)
                    need(dve, s["mv"], i + 1)
                    dve.tensor_scalar(ve[:, :], mv[:, 1:2], LN_EPS, None, ALU.add).then_inc(s["ve"], 1)
                    need(dve, s["rstd"], i + 1)
                    need(dve, stored[par], landed(half - 1))
                    dve.tensor_scalar(xo[par][:, :], y[:, :], mv[:, 0:1], rstd[:, 0:1], ALU.subtract, ALU.mult).then_inc(s["xo"], 1)
            steps(dve, body)
    st.end()


def cross_attention(nc, dram, name, x_in, x_out, mask=None):
    st = Stage(nc, name)
    NPAIR = HEADS // 2
    ready = 8 if mask is not None else 7
    both = (0, 1)
    x = [st.sb(f"x{k}", [ROWS, D]) for k in both]
    ctx = [st.sb(f"ctx{k}", [P, KC, KEYS]) for k in both]
    wq, wk, wv, wo = (st.sb(n, [P, KC, D]) for n in ("wq", "wk", "wv", "wo"))
    bqk = st.sb("bqk", [P, 2, KC])
    bv = st.sb("bv", [P, D])
    bo = st.sb("bo", [P, D])
    ident = st.sb("ident", [P, P])
    hm = st.sb("hm", [P, HPC])
    xb = st.sb("xb", [ROWS, D])
    xT = st.sb("xT", [P, KC, ROWS])
    qT = st.sb("qT", [P, KC, ROWS])
    qm = [st.sb(f"qm{k}", [P, KC, HPC, ROWS]) for k in both]
    kT = [st.sb(f"kT{k}", [P, KC, KEYS]) for k in both]
    va = [st.sb(f"va{k}", [KTW, 3, HEADS, VW]) for k in both]
    nmx = [st.sb(f"nmx{k}", [ROWS, HEADS]) for k in both]
    pr = [st.sb(f"pr{k}", [ROWS, 2, 3 * KTW]) for k in both]
    pT = [st.sb(f"pT{k}", [KTW, HEADS, 3, ROWS]) for k in both]
    oT = st.sb("oT", [P, 4, ROWS])
    rden = st.sb("rden", [ROWS, HEADS])
    o = st.sb("o", [ROWS, D])
    oT2 = st.sb("oT2", [P, KC, ROWS])
    y = st.sb("y", [ROWS, D])
    stat = st.sb("stat", [ROWS, 6])
    mv = st.sb("mv", [ROWS, 2])
    ve = st.sb("ve", [ROWS, 1])
    rstd = st.sb("rstd", [ROWS, 1])
    tick = st.sb("tick", [ROWS, 1])
    minus_half = st.sb("minus_half", [P, 1])
    xo = [st.sb(f"xo{k}", [ROWS, D]) for k in both]
    if mask is not None:
        maskid = st.sb("maskid", [P, P], BF16)
        mk = [st.sb(f"mk{k}", [ROWS, KEYS], I32) for k in both]
        mb = [st.sb(f"mb{k}", [ROWS, KEYS], BF16) for k in both]

    ps_s = st.ps("ps_s", [P, 4, BANK])
    ps_t = st.ps("ps_t", [P, 2, BANK])
    ps_p = st.ps("ps_p", [P, BANK])
    ps_o = st.ps("ps_o", [P, BANK])

    s = {n: st.sem(n) for n in (
        "w_in", "zeros", "xT_ps", "xT_sb", "q_ps", "q_sb", "qm", "xb", "mb",
        "o_ps", "oT_sb", "otr_ps", "rden", "o_sb", "oT2_ps", "oT2_sb", "y_ps", "y_sb", "stat", "mv", "ve", "rstd", "xo")}
    k_ps, k_sb = ([st.sem(f"{n}{m}") for m in range(KC)] for n in ("k_ps", "k_sb"))
    v_ps, v_sb = ([st.sem(f"{n}{m}") for m in range(3)] for n in ("v_ps", "v_sb"))
    scores, nmax, probs = ([st.sem(f"{n}{p}") for p in range(NPAIR)] for n in ("scores", "nmax", "probs"))
    pt, pt_sb = ([[st.sem(f"{n}{p}_{g}") for g in both] for p in range(NPAIR)] for n in ("pt", "pt_sb"))
    x_landed, c_landed, m_landed, stored = ([st.sem(f"{n}{k}") for k in both] for n in ("x_landed", "c_landed", "m_landed", "stored"))

    with st.block() as block:
        @block.sync
        def _(sp):
            weights = [(wq, "wq"), (ident, "ident"), (hm, "head_mask"), (bqk, "bqk"), (wk, "wk"), (wv, "wv"), (bv, "bv"), (bo, "bo"), (wo, "wo")]
            for t, n in weights:
                key = n if n in ("ident", "head_mask") else f"{name}_{n}"
                sp.dma_start(t.ap(), dram[key]).then_inc(s["w_in"], 16)

            def body(i, half, par, pre, main, post):
                if pre:
                    nxt, nhalf = 1 - par, half + par
                    need(sp, s["xb"], i)
                    sp.dma_start(x[nxt][:, :], x_in[i + 1]).then_inc(x_landed[nxt], 16)
                    need(sp, v_ps[2], i)
                    sp.dma_start(ctx[nxt][:, :, :], dram["ctxT"][i + 1]).then_inc(c_landed[nxt], 16)
                    if mask is not None:
                        need(sp, s["mb"], i)
                        sp.dma_start(mk[nxt][:, :], mask[i + 1]).then_inc(m_landed[nxt], 16)
                if post:
                    need(sp, s["xo"], i)
                    sp.dma_start(x_out[i - 1], xo[1 - par][:, :]).then_inc(stored[1 - par], 16)
            steps(sp, body)
            for k in both:
                sp.wait_ge(stored[k], landed(SEQS // 2 - 1))

        @block.gpsimd
        def _(pool):
            pool.memset(minus_half[:, :], -0.5).then_inc(s["zeros"], 1)
            for k in both:
                pool.memset(va[k][:, :, :, :], 0.0).then_inc(s["zeros"], 1)
                pool.memset(pr[k][:, :, :], 0.0).then_inc(s["zeros"], 1)
            pool.wait_ge(s["zeros"], 5)
            for k in both:
                pool.memset(va[k][:, :, :, HD:HD + 1], 1.0).then_inc(s["zeros"], 1)
            pool.wait_ge(s["w_in"], 144)
            if mask is not None:
                pool.tensor_scalar(maskid[:, :], ident[:, :], MASKED, None, ALU.mult).then_inc(s["zeros"], 1)
            pool.wait_ge(s["zeros"], ready)

            def body(i, half, par, pre, main, post):
                if pre:
                    nxt = 1 - par
                    need(pool, s["q_sb"], i + 2)
                    need(pool, scores[NPAIR - 1], i)
                    for c in range(KC):
                        done = pool.tensor_tensor(qm[nxt][:, c, :, :], qT[:, c, :].unsqueeze(1).to_broadcast([P, HPC, ROWS]),
                                                  hm[:, :].unsqueeze(2).to_broadcast([P, HPC, ROWS]), ALU.mult)
                    done.then_inc(s["qm"], 1)
                if post:
                    need(pool, s["ve"], i)
                    need(pool, s["xo"], i - 1)
                    pool.tensor_tensor(rstd[:, :], ve[:, :], minus_half[0:ROWS, :], ALU.pow).then_inc(s["rstd"], 1)
                if main:
                    need(pool, x_landed[par], landed(half))
                    need(pool, s["y_sb"], i)
                    pool.tensor_tensor(xb[:, :], x[par][:, :], bo[0:ROWS, :], ALU.add).then_inc(s["xb"], 1)
            steps(pool, body)

        @block.tensor
        def _(pe):
            pe.wait_ge(s["w_in"], 144)
            pe.wait_ge(s["zeros"], ready)

            def pair_scores(p, i, par):
                if p == 0:
                    need(pe, s["qm"], i + 1)
                    for c in range(KC):
                        need(pe, k_sb[c], i + 1)
                    if mask is not None:
                        need(pe, s["mb"], i + 1)
                need(pe, probs[(p - 2) % NPAIR], i + 1 if p >= 2 else i)
                for g in both:
                    h = 2 * p + g
                    bank = ps_s[0:ROWS, 2 * (p % 2) + g, 0:KEYS]
                    if mask is not None:
                        pe.matmul(bank, maskid[0:ROWS, 0:ROWS], mb[par][:, :], start=True, stop=False)
                    done = pe.matmul(bank, qm[par][:, h // HPC, h % HPC, :], kT[par][:, h // HPC, :], start=mask is None, stop=True)
                done.then_inc(scores[p], 1)

            def pair_transposes(p, i):
                need(pe, probs[p], i + 1)
                for g in both:
                    need(pe, pt_sb[(p - 1) % NPAIR][g], i + 1 if p >= 1 else i)
                    for k in range(3):
                        done = pe.transpose(ps_t[0:KTW, g, k * ROWS:(k + 1) * ROWS], pr[p % 2][:, g, k * KTW:(k + 1) * KTW], ident[0:ROWS, 0:ROWS])
                    done.then_inc(pt[p][g], 1)

            def pre_step(p, i, half, par):
                nxt, nhalf = 1 - par, half + par
                if p == 0:
                    need(pe, x_landed[nxt], landed(nhalf))
                    need(pe, v_sb[2], i + 1)
                    for c in range(KC):
                        done = pe.transpose(ps_p[:, c * ROWS:(c + 1) * ROWS], x[nxt][:, c * P:(c + 1) * P], ident[0:ROWS, 0:ROWS])
                    done.then_inc(s["xT_ps"], 1)
                if p == 1:
                    need(pe, s["xT_sb"], i + 2)
                    for m in range(KC):
                        for c in range(KC):
                            done = pe.matmul(ps_p[:, m * ROWS:(m + 1) * ROWS], wq[:, c, m * P:(m + 1) * P], xT[:, c, :], start=c == 0, stop=c == KC - 1)
                    done.then_inc(s["q_ps"], 1)
                if p in (2, 3):
                    m = p - 2
                    if m == 0:
                        need(pe, c_landed[nxt], landed(nhalf))
                        need(pe, s["q_sb"], i + 2)
                    else:
                        need(pe, k_sb[0], i + 2)
                    for c in range(KC):
                        done = pe.matmul(ps_p[:, 0:KEYS], wk[:, c, m * P:(m + 1) * P], ctx[nxt][:, c, :], start=c == 0, stop=c == KC - 1)
                    done.then_inc(k_ps[m], 1)
                if p in (4, 5, 6):
                    k = p - 4
                    k0, kn = k * KTW, min(KTW, KEYS - k * KTW)
                    need(pe, k_sb[1] if k == 0 else v_sb[k - 1], i + 2)
                    for c in range(KC):
                        done = pe.matmul(ps_p[0:kn, 0:D], ctx[nxt][:, c, k0:k0 + kn], wv[:, c, :], start=c == 0, stop=c == KC - 1)
                    done.then_inc(v_ps[k], 1)

            def post_step(p, i, par):
                prv = 1 - par
                if p == 1:
                    for g in both:
                        need(pe, pt_sb[NPAIR - 1][g], i)
                    need(pe, s["y_sb"], i - 1)
                    for j in range(4):
                        for k in range(3):
                            for g in range(4):
                                h = 4 * j + g
                                done = pe.matmul(ps_o[g * VW:(g + 1) * VW, j * ROWS:(j + 1) * ROWS], va[prv][:, k, h, :], pT[prv][:, h, k, :],
                                                 start=k == 0, stop=k == 2, tile_position=(0, g * VW))
                    done.then_inc(s["o_ps"], 1)
                if p == 2:
                    need(pe, s["oT_sb"], i)
                    for j in range(4):
                        done = pe.transpose(ps_o[0:ROWS, j * P:(j + 1) * P], oT[:, j, :], ident[:, :])
                    done.then_inc(s["otr_ps"], 1)
                if p == 3:
                    need(pe, s["o_sb"], i)
                    for c in range(KC):
                        done = pe.transpose(ps_o[:, c * ROWS:(c + 1) * ROWS], o[:, c * P:(c + 1) * P], ident[0:ROWS, 0:ROWS])
                    done.then_inc(s["oT2_ps"], 1)
                if p == 4:
                    need(pe, s["oT2_sb"], i)
                    for c in range(KC):
                        done = pe.matmul(ps_o[0:ROWS, 0:D], oT2[:, c, :], wo[:, c, :], start=c == 0, stop=c == KC - 1)
                    done.then_inc(s["y_ps"], 1)

            def body(i, half, par, pre, main, post):
                for p in range(NPAIR):
                    if main:
                        pair_scores(p, i, par)
                    if pre:
                        pre_step(p, i, half, par)
                    if p == 0 and post:
                        pair_transposes(NPAIR - 1, i - 1)
                    if post:
                        post_step(p, i, par)
                    if p >= 1 and main:
                        pair_transposes(p - 1, i)
            steps(pe, body)

        @block.scalar
        def _(act):
            act.wait_ge(s["w_in"], 144)
            act.wait_ge(s["zeros"], 7)

            def copy_odd(p, i, par):
                need(act, pt[p][1], i + 1)
                if p == 0:
                    need(act, s["o_ps"], i - 1)
                act.activation(pT[par][:, 2 * p + 1, :, :], ps_t[0:KTW, 1, 0:3 * ROWS].rearrange("p (k n) -> p k n", k=3), ACT.Copy).then_inc(pt_sb[p][1], 1)

            def body(i, half, par, pre, main, post):
                for p in range(NPAIR):
                    if main:
                        need(act, nmax[p], i + 1)
                        need(act, pt[(p - 2) % NPAIR][1], i + 1 if p >= 2 else i)
                        for g in both:
                            h = 2 * p + g
                            done = act.activation(pr[p % 2][:, g, 0:KEYS], ps_s[0:ROWS, 2 * (p % 2) + g, 0:KEYS], ACT.Exp, bias=nmx[par][:, h:h + 1])
                        done.then_inc(probs[p], 1)
                    if pre and p in (2, 3):
                        m = p - 2
                        need(act, k_ps[m], i + 2)
                        need(act, scores[NPAIR - 1], i)
                        act.activation(kT[1 - par][:, m, :], ps_p[:, 0:KEYS], ACT.Identity, bias=bqk[:, 1, m:m + 1]).then_inc(k_sb[m], 1)
                    if p == 0 and post:
                        copy_odd(NPAIR - 1, i - 1, 1 - par)
                    if p >= 1 and main:
                        copy_odd(p - 1, i, par)
                    if p == 1 and post:
                        need(act, s["o_ps"], i)
                        need(act, s["otr_ps"], i - 1)
                        act.activation(oT[:, :, :], ps_o[:, 0:4 * ROWS].rearrange("p (g n) -> p g n", g=4), ACT.Copy).then_inc(s["oT_sb"], 1)
                    if p == 3 and post:
                        need(act, s["oT2_ps"], i)
                        need(act, s["y_ps"], i - 1)
                        act.activation(oT2[:, :, :], ps_o[:, 0:KC * ROWS].rearrange("p (g n) -> p g n", g=KC), ACT.Copy).then_inc(s["oT2_sb"], 1)
            steps(act, body)

        @block.vector
        def _(dve):
            dve.wait_ge(s["w_in"], 144)
            dve.wait_ge(s["zeros"], 7)

            def copy_even(p, i, par):
                need(dve, pt[p][0], i + 1)
                if p == 0:
                    need(dve, s["o_ps"], i - 1)
                dve.tensor_copy(pT[par][:, 2 * p, :, :], ps_t[0:KTW, 0, 0:3 * ROWS].rearrange("p (k n) -> p k n", k=3)).then_inc(pt_sb[p][0], 1)

            def pre_step(p, i, half, par):
                if p == 7 and mask is not None:
                    need(dve, m_landed[1 - par], landed(half + par))
                    need(dve, scores[NPAIR - 1], i)
                    dve.tensor_scalar(mb[1 - par][:, :], mk[1 - par][:, :], 0.0, None, ALU.is_equal).then_inc(s["mb"], 1)
                if p == 0:
                    need(dve, s["xT_ps"], i + 2)
                    dve.tensor_copy(xT[:, :, :], ps_p[:, 0:KC * ROWS].rearrange("p (c n) -> p c n", c=KC)).then_inc(s["xT_sb"], 1)
                if p == 1:
                    need(dve, s["q_ps"], i + 2)
                    need(dve, s["qm"], i + 1)
                    for c in range(KC):
                        done = dve.tensor_scalar(qT[:, c, :], ps_p[:, c * ROWS:(c + 1) * ROWS], bqk[:, 0, c:c + 1], HD ** -0.5, ALU.add, ALU.mult)
                    done.then_inc(s["q_sb"], 1)
                if p in (4, 5, 6):
                    k = p - 4
                    kn = min(KTW, KEYS - k * KTW)
                    need(dve, v_ps[k], i + 2)
                    need(dve, s["o_ps"], i)
                    dve.tensor_tensor(va[1 - par][0:kn, k, :, 0:HD], ps_p[0:kn, 0:D].rearrange("p (h d) -> p h d", h=HEADS),
                                      bv[0:kn, :].rearrange("p (h d) -> p h d", h=HEADS), ALU.add).then_inc(v_sb[k], 1)

            def post_step(p, i, half, par):
                prv, phalf = 1 - par, half + par - 1
                if p == 2:
                    need(dve, s["otr_ps"], i)
                    heads = ps_o[0:ROWS, :].rearrange("p (h w) -> p h w", w=VW)
                    dve.reciprocal(rden[:, :], heads[:, :, HD]).then_inc(s["rden"], 1)
                    need(dve, s["rden"], i)
                    dve.tensor_tensor(o[:, :].rearrange("p (h d) -> p h d", h=HEADS), heads[:, :, 0:HD],
                                      rden[:, :].unsqueeze(2).to_broadcast([ROWS, HEADS, HD]), ALU.mult).then_inc(s["o_sb"], 1)
                if p == 4:
                    need(dve, s["y_ps"], i)
                    need(dve, s["xb"], i)
                    dve.tensor_tensor(y[:, :], ps_o[0:ROWS, 0:D], xb[:, :], ALU.add).then_inc(s["y_sb"], 1)
                if p == 5:
                    need(dve, s["y_sb"], i)
                    dve.bn_stats(stat[:, :], y[:, :]).then_inc(s["stat"], 1)
                    need(dve, s["stat"], i)
                    dve.memset(tick[:, :], 0.0)
                    dve.bn_aggr(mv[:, :], stat[:, :]).then_inc(s["mv"], 1)
                    need(dve, s["mv"], i)
                    dve.tensor_scalar(ve[:, :], mv[:, 1:2], LN_EPS, None, ALU.add).then_inc(s["ve"], 1)
                if p == 6:
                    need(dve, s["rstd"], i)
                    need(dve, stored[prv], landed(phalf - 1))
                    dve.tensor_scalar(xo[prv][:, :], y[:, :], mv[:, 0:1], rstd[:, 0:1], ALU.subtract, ALU.mult).then_inc(s["xo"], 1)

            def body(i, half, par, pre, main, post):
                for p in range(NPAIR):
                    if main:
                        need(dve, scores[p], i + 1)
                        if p == 0:
                            need(dve, probs[NPAIR - 1], i - 1)
                        dve.tensor_reduce(nmx[par][:, 2 * p:2 * p + 2], ps_s[0:ROWS, 2 * (p % 2):2 * (p % 2) + 2, 0:KEYS], AX.X, ALU.max,
                                          negate=True).then_inc(nmax[p], 1)
                    if p == 0 and post:
                        copy_even(NPAIR - 1, i - 1, 1 - par)
                    if pre:
                        pre_step(p, i, half, par)
                    if p >= 1 and main:
                        copy_even(p - 1, i, par)
                    if post:
                        post_step(p, i, half, par)
            steps(dve, body)
    st.end()


class Routes:

    def __init__(self, nc, stack, name, experts, tiles):
        def sb(n, shape, dt):
            return stack.enter_context(nc.sbuf_tensor(f"{name}_{n}", shape, dt))
        self.name, self.experts, self.tiles = name, experts, tiles
        self.slot = sb("slot", [ROWS, 2, SEQS], I32)
        self.weight = sb("weight", [ROWS, 2, SEQS], F32)
        self.expert = sb("expert", [P, tiles], I32)
        self.ring = sb("ring", [P, tiles], I32)
        self.end = sb("end", [P, experts], I32)


RING = 3


def router(nc, dram, routes, x_in, xs, norm_eps, norm_min, bias):
    E, T = routes.experts, routes.tiles
    st = Stage(nc, routes.name)
    xa = st.sb("xa", [ROWS, SEQS, D])
    wr = st.sb("wr", [P, KC, E])
    br = st.sb("br", [P, E])
    ident = st.sb("ident", [P, P])
    before = st.sb("before", [ROWS, ROWS])
    ones = st.sb("ones", [ROWS, ROWS])
    iota = st.sb("iota", [P, P])
    chain = st.sb("chain", [P, E, SEQS])
    xT = [st.sb(f"xT{k}", [P, KC, ROWS]) for k in (0, 1)]
    lg = st.sb("lg", [ROWS, SEQS, E])
    top = st.sb("top", [ROWS, SEQS, 8])
    idx = st.sb("idx", [ROWS, SEQS, 8], U32)
    idf = st.sb("idf", [ROWS, SEQS, 8])
    hot = [st.sb(f"hot{k}", [ROWS, SEQS, E]) for k in (0, 1)]
    hots = st.sb("hots", [ROWS, SEQS, E])
    less = st.sb("less", [ROWS, SEQS, E])
    ex = st.sb("ex", [ROWS, SEQS, E])
    less2 = st.sb("less2", [ROWS, SEQS])
    sc = st.sb("sc", [ROWS, 2, SEQS])
    ex2 = st.sb("ex2", [ROWS, SEQS])
    z = st.sb("z", [ROWS, SEQS])
    rz = st.sb("rz", [ROWS, SEQS])
    sm = st.sb("sm", [ROWS, SEQS])
    sm2 = st.sb("sm2", [ROWS, SEQS])
    rs = st.sb("rs", [ROWS, SEQS])
    tot = st.sb("tot", [ROWS, E, SEQS])
    upto = st.sb("upto", [ROWS, E, SEQS])
    prior = st.sb("prior", [ROWS, E, SEQS])
    nt = st.sb("nt", [ROWS, E], I32)
    nt2 = st.sb("nt2", [ROWS, E], I32)
    ntf = st.sb("ntf", [ROWS, E])
    endf = st.sb("endf", [ROWS, E])
    base = st.sb("base", [ROWS, E])
    base2 = st.sb("base2", [ROWS, E])
    pos = st.sb("pos", [ROWS, SEQS, E])
    pos2 = st.sb("pos2", [ROWS, SEQS, E])
    pk = [st.sb(f"pk{k}", [ROWS, SEQS, E]) for k in (0, 1)]
    slotf = st.sb("slotf", [ROWS, 2, SEQS])
    past = st.sb("past", [ROWS, T, E])
    ef = st.sb("ef", [ROWS, T])
    ef2 = st.sb("ef2", [ROWS, T])
    wrap = [st.sb(f"wrap{k}", [ROWS, T]) for k in range(E // RING)]
    ringf = [st.sb(f"ringf{k}", [ROWS, T]) for k in range(E // RING)]
    ps_x = [st.ps(f"ps_x{k}", [P, BANK]) for k in (0, 1)]
    ps_l = st.ps("ps_l", [P, BANK])
    ps_r = st.ps("ps_r", [P, BANK])
    ps_c = st.ps("ps_c", [P, BANK])
    s = {n: st.sem(n) for n in ("w_in", "x_in", "xT_ps", "xT_sb", "lg_ps", "hots", "rank_ps", "ones", "less", "ex", "slot", "dve", "sent")}

    with st.block() as block:
        @block.sync
        def _(sp):
            for t, n in ((wr.ap(), f"{routes.name}_wr"), (br.ap(), f"{routes.name}_br"), (ident.ap(), "ident"), (before.ap(), "before"),
                         (iota.ap(), "iota"), (chain.ap(), f"{routes.name}_chain")):
                sp.dma_start(t, dram[n]).then_inc(s["w_in"], 16)
            sp.dma_start(xa[:, :, :], x_in.rearrange("s r d -> r s d")).then_inc(s["x_in"], 16)

        @block.gpsimd
        def _(pool):
            pool.memset(ones[:, :], 1.0).then_inc(s["ones"], 1)
            pool.wait_ge(s["x_in"], 16)
            pool.wait_ge(s["slot"], 1)
            for b in range(SEQS):
                for k in (0, 1):
                    pool.indirect_dma_start(xs, bass.IndirectOffsetOnAxis(ap=routes.slot[:, k, b:b + 1], axis=0), xa[:, b, :], None).then_inc(s["sent"], 16)
            pool.wait_ge(s["sent"], 16 * 2 * SEQS)

        @block.tensor
        def _(pe):
            pe.wait_ge(s["w_in"], 96)
            pe.wait_ge(s["x_in"], 16)

            def logits(b):
                pe.wait_ge(s["xT_sb"], b + 1)
                for c in range(KC):
                    done = pe.matmul(ps_l[0:ROWS, b * E:(b + 1) * E], xT[b % 2][:, c, :], wr[:, c, :], start=c == 0, stop=c == KC - 1)
                done.then_inc(s["lg_ps"], 1)

            for b in range(SEQS):
                if b >= 2:
                    pe.wait_ge(s["xT_sb"], b - 1)
                for c in range(KC):
                    done = pe.transpose(ps_x[b % 2][:, c * ROWS:(c + 1) * ROWS], xa[:, b, c * P:(c + 1) * P], ident[0:ROWS, 0:ROWS])
                done.then_inc(s["xT_ps"], 1)
                if b >= 1:
                    logits(b - 1)
            logits(SEQS - 1)
            pe.wait_ge(s["hots"], 1)
            pe.wait_ge(s["ones"], 1)
            flat = hots[:, :, :].rearrange("p s e -> p (s e)")
            pe.matmul(ps_r[0:ROWS, 0:SEQS * E], before[:, :], flat, start=True, stop=True)
            pe.matmul(ps_c[0:ROWS, 0:SEQS * E], ones[:, :], flat, start=True, stop=True).then_inc(s["rank_ps"], 1)

        @block.scalar
        def _(act):
            for b in range(SEQS):
                act.wait_ge(s["xT_ps"], b + 1)
                if b >= 2:
                    act.wait_ge(s["lg_ps"], b - 1)
                act.activation(xT[b % 2][:, :, :], ps_x[b % 2][:, 0:KC * ROWS].rearrange("p (c n) -> p c n", c=KC), ACT.Copy).then_inc(s["xT_sb"], 1)
            act.wait_ge(s["less"], 2)
            act.activation(ex[:, :, :], less[:, :, :], ACT.Exp).then_inc(s["ex"], 1)
            act.activation(ex2[:, :], less2[:, :], ACT.Exp).then_inc(s["ex"], 1)

        @block.vector
        def _(dve):
            count = [0]

            def then(ins):
                count[0] += 1
                ins.then_inc(s["dve"], 1)
                dve.wait_ge(s["dve"], count[0])

            def over(a, n):
                return a.unsqueeze(2).to_broadcast([ROWS, a.shape[1], n])

            def by_seq(a):
                return a.unsqueeze(1).to_broadcast([ROWS, SEQS, E])

            dve.wait_ge(s["w_in"], 96)
            dve.wait_ge(s["ones"], 1)
            dve.wait_ge(s["lg_ps"], SEQS)
            logits = ps_l[0:ROWS, 0:SEQS * E].rearrange("p (s e) -> p s e", s=SEQS)
            if bias:
                then(dve.tensor_tensor(lg[:, :, :], logits, by_seq(br[0:ROWS, :]), ALU.add))
            else:
                then(dve.tensor_copy(lg[:, :, :], logits))
            for b in range(SEQS):
                last = dve.max(top[:, b, :], lg[:, b, :])
            then(last)
            for b in range(SEQS):
                last = dve.max_index(idx[:, b, :], top[:, b, :], lg[:, b, :])
            then(last)
            then(dve.tensor_copy(idf[:, :, :], idx[:, :, :]))
            row = iota[0:ROWS, 0:E].unsqueeze(1).to_broadcast([ROWS, SEQS, E])
            for k in (0, 1):
                last = dve.tensor_tensor(hot[k][:, :, :], row, over(idf[:, :, k], E), ALU.is_equal)
            then(last)
            dve.tensor_tensor(hots[:, :, :], hot[0][:, :, :], hot[1][:, :, :], ALU.add).then_inc(s["hots"], 1)
            dve.tensor_tensor(less[:, :, :], lg[:, :, :], over(top[:, :, 0], E), ALU.subtract).then_inc(s["less"], 1)
            dve.tensor_tensor(less2[:, :], top[:, :, 1], top[:, :, 0], ALU.subtract).then_inc(s["less"], 1)
            dve.wait_ge(s["ex"], 2)
            then(dve.tensor_reduce(z[:, :], ex[:, :, :], AX.X, ALU.add))
            then(dve.reciprocal(rz[:, :], z[:, :]))
            dve.tensor_copy(sc[:, 0, :], rz[:, :])
            then(dve.tensor_tensor(sc[:, 1, :], ex2[:, :], rz[:, :], ALU.mult))
            then(dve.tensor_tensor(sm[:, :], sc[:, 0, :], sc[:, 1, :], ALU.add))
            then(dve.tensor_scalar(sm2[:, :], sm[:, :], norm_eps, norm_min, ALU.add, ALU.max))
            then(dve.reciprocal(rs[:, :], sm2[:, :]))
            for k in (0, 1):
                dve.tensor_tensor(routes.weight[:, k, :], sc[:, k, :], rs[:, :], ALU.mult)
            dve.wait_ge(s["rank_ps"], 1)
            then(dve.tensor_copy(tot[:, :, :], ps_c[0:ROWS, 0:SEQS * E].rearrange("p (s e) -> p e s", s=SEQS)))
            flat = "p e s -> p (e s)"
            then(dve.tensor_tensor_scan(upto[:, :, :].rearrange(flat), chain[0:ROWS, :, :].rearrange(flat), tot[:, :, :].rearrange(flat), 0.0, ALU.mult, ALU.add))
            dve.tensor_tensor(prior[:, :, :], upto[:, :, :], tot[:, :, :], ALU.subtract)
            then(dve.tensor_scalar(nt[:, :], upto[:, :, SEQS - 1], float(P - 1), None, ALU.add))
            then(dve.tensor_scalar(nt2[:, :], nt[:, :], P.bit_length() - 1, None, ALU.logical_shift_right))
            then(dve.tensor_copy(ntf[:, :], nt2[:, :]))
            then(dve.tensor_tensor_scan(endf[:, :], ones[:, 0:E], ntf[:, :], 0.0, ALU.mult, ALU.add))
            dve.tensor_copy(routes.end[0:ROWS, :], endf[:, :])
            then(dve.tensor_tensor(base[:, :], endf[:, :], ntf[:, :], ALU.subtract))
            then(dve.tensor_scalar(base2[:, :], base[:, :], float(P), None, ALU.mult))
            then(dve.tensor_tensor(pos[:, :, :], ps_r[0:ROWS, 0:SEQS * E].rearrange("p (s e) -> p s e", s=SEQS), prior[:, :, :].rearrange("p e s -> p s e"), ALU.add))
            then(dve.tensor_tensor(pos2[:, :, :], pos[:, :, :], by_seq(base2[:, :]), ALU.add))
            for k in (0, 1):
                last = dve.tensor_tensor(pk[k][:, :, :], hot[k][:, :, :], pos2[:, :, :], ALU.mult)
            then(last)
            for k in (0, 1):
                last = dve.tensor_reduce(slotf[:, k, :], pk[k][:, :, :], AX.X, ALU.add)
            then(last)
            dve.tensor_copy(routes.slot[:, :, :], slotf[:, :, :]).then_inc(s["slot"], 1)
            then(dve.tensor_tensor(past[:, :, :], endf[:, :].unsqueeze(1).to_broadcast([ROWS, T, E]), over(iota[0:ROWS, 0:T], E), ALU.is_le))
            then(dve.tensor_reduce(ef[:, :], past[:, :, :], AX.X, ALU.add))
            then(dve.tensor_scalar(ef2[:, :], ef[:, :], float(E - 1), None, ALU.min))
            dve.tensor_copy(routes.expert[0:ROWS, :], ef2[:, :])
            for k in range(E // RING):
                last = dve.tensor_scalar(wrap[k][:, :], ef2[:, :], float(RING * (k + 1)), float(-RING), ALU.is_ge, ALU.mult)
            then(last)
            for k in range(E // RING):
                then(dve.tensor_tensor(ringf[k][:, :], ringf[k - 1][:, :] if k else ef2[:, :], wrap[k][:, :], ALU.add))
            then(dve.tensor_copy(routes.ring[0:ROWS, :], ringf[-1][:, :]))
    st.end()


def tile_steps(eng, tiles, body):
    body(-1, -1, 1, True, False, False)
    body(0, 0, 0, True, True, False)
    with eng.Fori(0, (tiles - 2) // 2) as it:
        body(2 * it + 1, it, 1, True, True, True)
        body(2 * it + 2, it + 1, 0, True, True, True)
    body(tiles - 1, tiles // 2 - 1, 1, False, True, True)
    body(tiles, tiles // 2, 0, False, False, True)


def relu_experts(nc, dram, routes, xs, ys):
    st = Stage(nc, "ff0")
    HALF = F0 // 2
    GU = 2 * KC * F0
    FC = F0 // P
    w = st.sb("w", [P, RING, GU + FC * D])
    gu = w[:, :, 0:GU].rearrange("p r (m c f) -> p r m c f", m=2, c=KC)
    down = w[:, :, GU:].rearrange("p r (k d) -> p r k d", k=FC)
    ident = st.sb("ident", [P, P])
    x = [st.sb(f"x{k}", [P, D]) for k in (0, 1)]
    xT = [st.sb(f"xT{k}", [P, KC, P]) for k in (0, 1)]
    rg = st.sb("rg", [P, 2, HALF])
    h = st.sb("h", [P, 2, HALF])
    hT = st.sb("hT", [P, FC, P])
    y = [st.sb(f"y{k}", [P, D]) for k in (0, 1)]
    ps_g = [st.ps(f"ps_g{k}", [P, BANK]) for k in (0, 1)]
    ps_u = [st.ps(f"ps_u{k}", [P, BANK]) for k in (0, 1)]
    ps_h = [st.ps(f"ps_h{k}", [P, BANK]) for k in (0, 1)]
    ps_x = st.ps("ps_x", [P, BANK])
    ps_y = st.ps("ps_y", [P, BANK])
    s = {n: st.sem(n) for n in ("w_in", "w_ready", "freed", "tiles_done", "xT_ps", "xT_sb", "y_ps", "y_sb")}
    g_ps, u_ps, rg_sb, h_sb, hT_ps, hT_sb = ([st.sem(f"{n}{k}") for k in (0, 1)] for n in ("g_ps", "u_ps", "rg_sb", "h_sb", "hT_ps", "hT_sb"))
    x_landed, stored = ([st.sem(f"{n}{k}") for k in (0, 1)] for n in ("x_landed", "stored"))
    w_landed = [st.sem(f"w_landed{k}") for k in range(RING)]

    with st.block() as block:
        @block.sync
        def _(sp):
            sp.dma_start(ident[:, :], dram["ident"]).then_inc(s["w_in"], 16)

            def body(i, half, par, pre, main, post):
                if pre:
                    need(sp, s["xT_ps"], i)
                    sp.dma_start(x[1 - par][:, :], xs[i + 1]).then_inc(x_landed[1 - par], 16)
                if post:
                    need(sp, s["y_sb"], i)
                    sp.dma_start(ys[i - 1], y[1 - par][:, :]).then_inc(stored[1 - par], 16)
            tile_steps(sp, routes.tiles, body)
            for k in (0, 1):
                sp.wait_ge(stored[k], landed(routes.tiles // 2 - 1))

        @block.gpsimd
        def _(pool):
            pool.sem_inc(s["tiles_done"], 1)

            def fetch(e):
                pool.dma_start(w[:, e % RING, :], dram["ff0_w"][e]).then_inc(w_landed[e % RING], 16)
            for e in range(RING):
                fetch(e)
            for e in range(E0):
                pool.wait_ge(w_landed[e % RING], 16 * (e // RING + 1))
                pool.sem_inc(s["w_ready"], 1)
                if e + RING < E0:
                    end = pool.value_load(routes.end[0:1, e:e + 1], min_val=0, max_val=routes.tiles)
                    pool.wait_ge(s["tiles_done"], end + 1)
                    pool.sem_inc(s["freed"], 1)
                    fetch(e + RING)

        @block.tensor
        def _(pe):
            pe.wait_ge(s["w_in"], 16)

            def body(i, half, par, pre, main, post):
                if main:
                    expert = pe.value_load(routes.expert[0:1, bass.ds(i, 1)], min_val=0, max_val=E0 - 1)
                    at = pe.value_load(routes.ring[0:1, bass.ds(i, 1)], min_val=0, max_val=RING - 1)
                    pe.wait_ge(s["w_ready"], expert + 1)
                    need(pe, s["xT_sb"], i + 1)
                    for k in (0, 1):
                        for m, bank, read, sem in ((0, ps_g[k], rg_sb[k], g_ps[k]), (1, ps_u[k], h_sb[k], u_ps[k])):
                            need(pe, read, i)
                            for c in range(KC):
                                done = pe.matmul(bank[:, :], xT[par][:, c, :], gu[:, at, m, c, k * HALF:(k + 1) * HALF], start=c == 0, stop=c == KC - 1)
                            done.then_inc(sem, 1)
                if pre:
                    need(pe, x_landed[1 - par], landed(half + par))
                    need(pe, s["xT_sb"], i + 1)
                    for c in range(KC):
                        done = pe.transpose(ps_x[:, c * P:(c + 1) * P], x[1 - par][:, c * P:(c + 1) * P], ident[:, :])
                    done.then_inc(s["xT_ps"], 1)
                if main:
                    for k in (0, 1):
                        need(pe, h_sb[k], i + 1)
                        need(pe, hT_sb[k], i)
                        for q in range(FC // 2):
                            done = pe.transpose(ps_h[k][:, q * P:(q + 1) * P], h[:, k, q * P:(q + 1) * P], ident[:, :])
                        done.then_inc(hT_ps[k], 1)
                    for k in (0, 1):
                        need(pe, hT_sb[k], i + 1)
                        if k == 0:
                            need(pe, s["y_sb"], i)
                        for q in range(k * FC // 2, (k + 1) * FC // 2):
                            done = pe.matmul(ps_y[:, 0:D], hT[:, q, :], down[:, at, q, :], start=q == 0, stop=q == FC - 1)
                    done.then_inc(s["y_ps"], 1)
            tile_steps(pe, routes.tiles, body)

        @block.scalar
        def _(act):
            def body(i, half, par, pre, main, post):
                if main:
                    for k in (0, 1):
                        need(act, g_ps[k], i + 1)
                        need(act, h_sb[k], i)
                        act.activation(rg[:, k, :], ps_g[k][:, :], ACT.Relu).then_inc(rg_sb[k], 1)
                if pre:
                    need(act, s["xT_ps"], i + 2)
                    need(act, u_ps[1], i)
                    act.activation(xT[1 - par][:, :, :], ps_x[:, 0:D].rearrange("p (c n) -> p c n", c=KC), ACT.Copy).then_inc(s["xT_sb"], 1)
                if main:
                    need(act, hT_ps[0], i + 1)
                    need(act, s["y_ps"], i)
                    act.activation(hT[:, 0:FC // 2, :], ps_h[0][:, :].rearrange("p (q n) -> p q n", n=P), ACT.Copy).then_inc(hT_sb[0], 1)
            tile_steps(act, routes.tiles, body)

        @block.vector
        def _(dve):
            def body(i, half, par, pre, main, post):
                if main:
                    for k in (0, 1):
                        need(dve, rg_sb[k], i + 1)
                        need(dve, u_ps[k], i + 1)
                        need(dve, hT_ps[k], i)
                        dve.tensor_tensor(h[:, k, :], ps_u[k][:, :], rg[:, k, :], ALU.mult).then_inc(h_sb[k], 1)
                    need(dve, hT_ps[1], i + 1)
                    need(dve, s["y_ps"], i)
                    dve.tensor_copy(hT[:, FC // 2:, :], ps_h[1][:, :].rearrange("p (q n) -> p q n", n=P)).then_inc(hT_sb[1], 1)
                    need(dve, s["y_ps"], i + 1)
                    need(dve, stored[par], landed(half - 1))
                    dve.tensor_copy(y[par][:, :], ps_y[:, 0:D]).then_inc(s["y_sb"], 1)
                    dve.sem_inc(s["tiles_done"], 1)
            tile_steps(dve, routes.tiles, body)
    st.end()


class Norm:

    def __init__(self, st, name, rows=ROWS, width=D):
        self.y = st.sb(f"{name}_y", [rows, width])
        self.stat = st.sb(f"{name}_stat", [rows, 6])
        self.mv = st.sb(f"{name}_mv", [rows, 2])
        self.ve = st.sb(f"{name}_ve", [rows, 1])
        self.rstd = st.sb(f"{name}_rstd", [rows, 1])
        self.tick = st.sb(f"{name}_tick", [rows, 1])
        self.y_sb, self.stat_done, self.mv_done, self.ve_done, self.rstd_done, self.normed = (
            st.sem(f"{name}_{n}") for n in ("y_sb", "stat", "mv", "ve", "rstd", "normed"))

    def vector_stats(self, dve, n):
        need(dve, self.y_sb, n)
        dve.bn_stats(self.stat[:, :], self.y[:, :]).then_inc(self.stat_done, 1)
        need(dve, self.stat_done, n)
        dve.memset(self.tick[:, :], 0.0)
        dve.bn_aggr(self.mv[:, :], self.stat[:, :]).then_inc(self.mv_done, 1)
        need(dve, self.mv_done, n)
        need(dve, self.rstd_done, n - 1)
        dve.tensor_scalar(self.ve[:, :], self.mv[:, 1:2], LN_EPS, None, ALU.add).then_inc(self.ve_done, 1)

    def pool_rstd(self, pool, n, minus_half):
        need(pool, self.ve_done, n)
        need(pool, self.normed, n - 1)
        pool.tensor_tensor(self.rstd[:, :], self.ve[:, :], minus_half, ALU.pow).then_inc(self.rstd_done, 1)

    def vector_scale(self, dve, n, out):
        need(dve, self.rstd_done, n)
        dve.tensor_scalar(out, self.y[:, :], self.mv[:, 0:1], self.rstd[:, 0:1], ALU.subtract, ALU.mult).then_inc(self.normed, 1)


def recurrence(nc, dram, routes, x_in, ys, x_out):
    st = Stage(nc, "rec")
    both = (0, 1)
    x = [st.sb(f"x{k}", [ROWS, D]) for k in both]
    pick = [[st.sb(f"pick{n}_{k}", [ROWS, D]) for k in both] for n in both]
    ident = st.sb("ident", [P, P])
    win = st.sb("win", [P, 4, KC, D])
    wout = st.sb("wout", [P, KC, D])
    la = st.sb("la", [P, KC])
    th = st.sb("th", [P, KC])
    minus_a = st.sb("minus_a", [P, KC])
    minus_half = st.sb("minus_half", [P, 1])
    part = st.sb("part", [ROWS, D])
    x3 = [st.sb(f"x3_{k}", [ROWS, D]) for k in both]
    x3T = st.sb("x3T", [P, KC, ROWS])
    az = st.sb("az", [P, KC, ROWS])
    ez = st.sb("ez", [P, KC, ROWS])
    lz = st.sb("lz", [P, KC, ROWS])
    sp_ = st.sb("sp", [P, KC, ROWS])
    delta = st.sb("delta", [P, KC, ROWS])
    decay = st.sb("decay", [P, KC, ROWS])
    tin = st.sb("tin", [P, KC, ROWS])
    tsel = st.sb("tsel", [P, KC, ROWS])
    tgate = st.sb("tgate", [P, KC, ROWS])
    upd = st.sb("upd", [P, KC, ROWS])
    state = st.sb("state", [P, KC, ROWS])
    gated = st.sb("gated", [P, KC, ROWS])
    xo = [st.sb(f"xo{k}", [ROWS, D]) for k in both]
    n3, n4 = Norm(st, "n3"), Norm(st, "n4")
    ps_x = st.ps("ps_x", [P, BANK])
    ps_z = [st.ps(f"ps_z{m}", [P, BANK]) for m in range(4)]
    ps_y = st.ps("ps_y", [P, BANK])
    s = {n: st.sem(n) for n in ("w_in", "half", "th", "a", "x_read", "part", "x3T_ps", "x3T_sb", "az", "ez", "lz", "sp", "delta", "decay",
                                "tin", "tsel", "tgate", "upd", "state", "gated", "y_ps")}
    z_ps = [st.sem(f"z_ps{m}") for m in range(4)]
    x_landed, stored = ([st.sem(f"{n}{k}") for k in both] for n in ("x_landed", "stored"))
    pick_landed = [[st.sem(f"pick_landed{n}_{k}") for k in both] for n in both]

    def chunks(t):
        return t.rearrange("p (c n) -> p c n", c=KC)

    with st.block() as block:
        @block.sync
        def _(sp):
            for t, n in ((ident, "ident"), (win, "rec_win"), (wout, "rec_wout"), (la, "rec_la")):
                sp.dma_start(t.ap(), dram[n]).then_inc(s["w_in"], 16)

            def body(i, half, par, pre, main, post):
                if pre:
                    need(sp, s["part"], i)
                    sp.dma_start(x[1 - par][:, :], x_in[i + 1]).then_inc(x_landed[1 - par], 16)
                if post:
                    need(sp, n4.normed, i)
                    sp.dma_start(x_out[i - 1], xo[1 - par][:, :]).then_inc(stored[1 - par], 16)
            steps(sp, body)
            for k in both:
                sp.wait_ge(stored[k], landed(SEQS // 2 - 1))

        @block.gpsimd
        def _(pool):
            pool.memset(minus_half[:, :], -0.5).then_inc(s["half"], 1)
            pool.wait_ge(s["half"], 1)

            def fetch(b):
                if b >= 2:
                    pool.wait_ge(n3.y_sb, b - 1)
                for n in both:
                    pool.indirect_dma_start(pick[n][b % 2][:, :], None, ys, bass.IndirectOffsetOnAxis(ap=routes.slot[:, n, b:b + 1], axis=0)).then_inc(pick_landed[n][b % 2], 16)
            fetch(0)
            for b in range(-1, SEQS + 1):
                if b + 2 < SEQS:
                    fetch(b + 2)
                if b >= 1:
                    n4.pool_rstd(pool, b, minus_half[0:ROWS, :])
                if b + 1 < SEQS:
                    n3.pool_rstd(pool, b + 2, minus_half[0:ROWS, :])

        @block.tensor
        def _(pe):
            pe.wait_ge(s["w_in"], 64)

            def body(i, half, par, pre, main, post):
                if post:
                    need(pe, s["gated"], i)
                    need(pe, n4.y_sb, i - 1)
                    for c in range(KC):
                        done = pe.matmul(ps_y[0:ROWS, 0:D], gated[:, c, :], wout[:, c, :], start=c == 0, stop=c == KC - 1)
                    done.then_inc(s["y_ps"], 1)
                if pre:
                    need(pe, n3.normed, i + 2)
                    need(pe, s["x3T_sb"], i + 1)
                    for c in range(KC):
                        done = pe.transpose(ps_x[:, c * ROWS:(c + 1) * ROWS], x3[1 - par][:, c * P:(c + 1) * P], ident[0:ROWS, 0:ROWS])
                    done.then_inc(s["x3T_ps"], 1)
                    need(pe, s["x3T_sb"], i + 2)
                    for m, read in enumerate((s["sp"], s["tin"], s["tsel"], s["tgate"])):
                        need(pe, read, i + 1)
                        for q in range(KC):
                            for c in range(KC):
                                done = pe.matmul(ps_z[m][:, q * ROWS:(q + 1) * ROWS], win[:, m, c, q * P:(q + 1) * P], x3T[:, c, :], start=c == 0, stop=c == KC - 1)
                        done.then_inc(z_ps[m], 1)
            steps(pe, body)

        @block.scalar
        def _(act):
            act.wait_ge(s["w_in"], 64)
            act.activation(th[:, :], la[:, :], ACT.Tanh, scale=0.5).then_inc(s["th"], 1)

            def body(i, half, par, pre, main, post):
                if main:
                    need(act, s["delta"], i + 1)
                    need(act, s["state"], i)
                    for c in range(KC):
                        done = act.activation(decay[:, c, :], delta[:, c, :], ACT.Exp, scale=minus_a[:, c:c + 1])
                    done.then_inc(s["decay"], 1)
                if pre:
                    need(act, s["x3T_ps"], i + 2)
                    need(act, z_ps[3], i + 1)
                    act.activation(x3T[:, :, :], chunks(ps_x[:, 0:KC * ROWS]), ACT.Copy).then_inc(s["x3T_sb"], 1)
                    need(act, z_ps[0], i + 2)
                    need(act, s["ez"], i + 1)
                    act.activation(az[:, :, :], chunks(ps_z[0][:, 0:KC * ROWS]), ACT.Abs).then_inc(s["az"], 1)
                    need(act, s["az"], i + 2)
                    need(act, s["lz"], i + 1)
                    act.activation(ez[:, :, :], az[:, :, :], ACT.Exp, scale=-1.0).then_inc(s["ez"], 1)
                    need(act, z_ps[1], i + 2)
                    need(act, s["upd"], i + 1)
                    act.activation(tin[:, :, :], chunks(ps_z[1][:, 0:KC * ROWS]), ACT.Tanh).then_inc(s["tin"], 1)
                    need(act, z_ps[2], i + 2)
                    act.activation(tsel[:, :, :], chunks(ps_z[2][:, 0:KC * ROWS]), ACT.Tanh, scale=0.5).then_inc(s["tsel"], 1)
                    need(act, z_ps[3], i + 2)
                    need(act, s["gated"], i + 1)
                    act.activation(tgate[:, :, :], chunks(ps_z[3][:, 0:KC * ROWS]), ACT.Tanh, scale=0.5).then_inc(s["tgate"], 1)
                    need(act, s["ez"], i + 2)
                    need(act, s["sp"], i + 1)
                    act.activation(lz[:, :, :], ez[:, :, :], ACT.Ln, bias=1.0).then_inc(s["lz"], 1)
            steps(act, body)

        @block.vector
        def _(dve):
            dve.wait_ge(s["th"], 1)
            dve.tensor_scalar(minus_a[:, :], th[:, :], -0.5, -0.5, ALU.mult, ALU.add).then_inc(s["a"], 1)
            dve.wait_ge(s["a"], 1)

            def body(i, half, par, pre, main, post):
                if main:
                    need(dve, s["decay"], i + 1)
                    need(dve, s["upd"], i + 1)
                    for c in range(KC):
                        done = dve.tensor_tensor_scan(state[:, c, :], decay[:, c, :], upd[:, c, :], 0.0, ALU.mult, ALU.add)
                    done.then_inc(s["state"], 1)
                    need(dve, s["state"], i + 1)
                    need(dve, s["tgate"], i + 1)
                    need(dve, s["y_ps"], i)
                    dve.scalar_tensor_tensor(gated[:, :, :], tgate[:, :, :], 1.0, state[:, :, :], ALU.add, ALU.mult).then_inc(s["gated"], 1)
                if post:
                    need(dve, s["y_ps"], i)
                    need(dve, n4.normed, i - 1)
                    dve.scalar_tensor_tensor(n4.y[:, :], ps_y[0:ROWS, 0:D], 0.25, x3[1 - par][:, :], ALU.mult, ALU.add).then_inc(n4.y_sb, 1)
                    n4.vector_stats(dve, i)
                    need(dve, stored[1 - par], landed(half + par - 2))
                    n4.vector_scale(dve, i, xo[1 - par][:, :])
                if pre:
                    nxt, nhalf = 1 - par, half + par
                    need(dve, x_landed[nxt], landed(nhalf))
                    need(dve, pick_landed[0][nxt], landed(nhalf))
                    dve.memset(n3.tick[:, :], 0.0)
                    dve.scalar_tensor_tensor(part[:, :], pick[0][nxt][:, :], routes.weight[:, 0, bass.ds(i + 1, 1)], x[nxt][:, :], ALU.mult, ALU.add).then_inc(s["part"], 1)
                    need(dve, s["part"], i + 2)
                    need(dve, pick_landed[1][nxt], landed(nhalf))
                    dve.memset(n3.tick[:, :], 0.0)
                    dve.scalar_tensor_tensor(n3.y[:, :], pick[1][nxt][:, :], routes.weight[:, 1, bass.ds(i + 1, 1)], part[:, :], ALU.mult, ALU.add).then_inc(n3.y_sb, 1)
                    n3.vector_stats(dve, i + 2)
                    need(dve, n4.y_sb, i)
                    n3.vector_scale(dve, i + 2, x3[nxt][:, :])
                if pre:
                    need(dve, s["lz"], i + 2)
                    need(dve, z_ps[0], i + 2)
                    dve.scalar_tensor_tensor(sp_[:, :, :], chunks(ps_z[0][:, 0:KC * ROWS]), 0.0, lz[:, :, :], ALU.max, ALU.add).then_inc(s["sp"], 1)
                    need(dve, s["sp"], i + 2)
                    dve.tensor_scalar(delta[:, :, :], sp_[:, :, :], 1e-4, None, ALU.max).then_inc(s["delta"], 1)
                    need(dve, s["tsel"], i + 2)
                    dve.scalar_tensor_tensor(upd[:, :, :], tsel[:, :, :], 1.0, tin[:, :, :], ALU.add, ALU.mult).then_inc(s["upd"], 1)
            steps(dve, body)
    st.end()


def gelu_experts(nc, dram, routes, xs, ys):
    st = Stage(nc, "ff1")
    both = (0, 1)
    w1 = st.sb("w1", [P, E1, KC, F1])
    w2 = st.sb("w2", [P, E1, KC, D])
    b1 = st.sb("b1", [1, E1, F1])
    b2 = st.sb("b2", [1, E1, D])
    gb = st.sb("gb", [P, 2, E1, F1])
    ones = st.sb("ones", [1, P])
    ident = st.sb("ident", [P, P])
    minus_half = st.sb("minus_half", [P, 1])
    x = [st.sb(f"x{k}", [P, D]) for k in both]
    xT = st.sb("xT", [P, KC, P])
    hn = st.sb("hn", [P, F1])
    hg = st.sb("hg", [P, F1])
    hb = st.sb("hb", [P, F1])
    ha = st.sb("ha", [P, F1])
    hT = st.sb("hT", [P, KC, P])
    y = [st.sb(f"y{k}", [P, D]) for k in both]
    nm = Norm(st, "nm", P, F1)
    ps_x = st.ps("ps_x", [P, BANK])
    ps_h = st.ps("ps_h", [P, BANK])
    ps_t = st.ps("ps_t", [P, BANK])
    ps_y = st.ps("ps_y", [P, BANK])
    s = {n: st.sem(n) for n in ("w_in", "half", "xT_ps", "xT_sb", "h_ps", "hg", "hb", "ha", "hT_ps", "hT_sb", "y_ps", "y_sb")}
    x_landed, stored = ([st.sem(f"{n}{k}") for k in both] for n in ("x_landed", "stored"))

    with st.block() as block:
        @block.sync
        def _(sp):
            for t, n in ((ident, "ident"), (w1, "ff1_w1"), (b1, "ff1_b1"), (gb, "ff1_gb"), (w2, "ff1_w2"), (b2, "ff1_b2")):
                sp.dma_start(t.ap(), dram[n]).then_inc(s["w_in"], 16)

            def body(i, half, par, pre, main, post):
                if pre:
                    need(sp, s["xT_ps"], i)
                    sp.dma_start(x[1 - par][:, :], xs[i + 1]).then_inc(x_landed[1 - par], 16)
                if post:
                    need(sp, s["y_sb"], i)
                    sp.dma_start(ys[i - 1], y[1 - par][:, :]).then_inc(stored[1 - par], 16)
            tile_steps(sp, routes.tiles, body)
            for k in both:
                sp.wait_ge(stored[k], landed(routes.tiles // 2 - 1))

        @block.gpsimd
        def _(pool):
            pool.memset(minus_half[:, :], -0.5).then_inc(s["half"], 1)
            pool.memset(ones[:, :], 1.0).then_inc(s["half"], 1)
            pool.wait_ge(s["half"], 2)

            def body(i, half, par, pre, main, post):
                if main:
                    nm.pool_rstd(pool, i + 1, minus_half[:, :])
            tile_steps(pool, routes.tiles, body)

        @block.tensor
        def _(pe):
            pe.wait_ge(s["w_in"], 96)
            pe.wait_ge(s["half"], 2)

            def body(i, half, par, pre, main, post):
                if main:
                    expert = pe.value_load(routes.expert[0:1, bass.ds(i, 1)], min_val=0, max_val=E1 - 1)
                    need(pe, s["xT_sb"], i + 1)
                    need(pe, nm.y_sb, i)
                    for c in range(KC):
                        pe.matmul(ps_h[:, 0:F1], xT[:, c, :], w1[:, expert, c, :], start=c == 0, stop=False)
                    pe.matmul(ps_h[:, 0:F1], ones[:, :], b1[:, expert, :], start=False, stop=True).then_inc(s["h_ps"], 1)
                if pre:
                    need(pe, x_landed[1 - par], landed(half + par))
                    need(pe, s["xT_sb"], i + 1)
                    for c in range(KC):
                        done = pe.transpose(ps_x[:, c * P:(c + 1) * P], x[1 - par][:, c * P:(c + 1) * P], ident[:, :])
                    done.then_inc(s["xT_ps"], 1)
                if post:
                    past = pe.value_load(routes.expert[0:1, bass.ds(i - 1, 1)], min_val=0, max_val=E1 - 1)
                    need(pe, s["ha"], i)
                    need(pe, s["hT_sb"], i - 1)
                    for c in range(KC):
                        done = pe.transpose(ps_t[:, c * P:(c + 1) * P], ha[:, c * P:(c + 1) * P], ident[:, :])
                    done.then_inc(s["hT_ps"], 1)
                    need(pe, s["hT_sb"], i)
                    need(pe, s["y_sb"], i - 1)
                    for c in range(KC):
                        pe.matmul(ps_y[:, 0:D], hT[:, c, :], w2[:, past, c, :], start=c == 0, stop=False)
                    pe.matmul(ps_y[:, 0:D], ones[:, :], b2[:, past, :], start=False, stop=True).then_inc(s["y_ps"], 1)
            tile_steps(pe, routes.tiles, body)

        @block.scalar
        def _(act):
            def body(i, half, par, pre, main, post):
                if main:
                    need(act, s["h_ps"], i + 1)
                    need(act, nm.normed, i)
                    act.activation(nm.y[:, :], ps_h[:, 0:F1], ACT.Copy).then_inc(nm.y_sb, 1)
                if pre:
                    need(act, s["xT_ps"], i + 2)
                    need(act, s["h_ps"], i + 1)
                    act.activation(xT[:, :, :], ps_x[:, 0:D].rearrange("p (c n) -> p c n", c=KC), ACT.Copy).then_inc(s["xT_sb"], 1)
                if post:
                    need(act, s["hT_ps"], i)
                    need(act, s["y_ps"], i - 1)
                    act.activation(hT[:, :, :], ps_t[:, 0:F1].rearrange("p (c n) -> p c n", c=KC), ACT.Copy).then_inc(s["hT_sb"], 1)
                if main:
                    need(act, s["hb"], i + 1)
                    need(act, s["hT_ps"], i)
                    act.activation(ha[:, :], hb[:, :], ACT.Gelu).then_inc(s["ha"], 1)
            tile_steps(act, routes.tiles, body)

        @block.vector
        def _(dve):
            dve.wait_ge(s["w_in"], 96)

            def body(i, half, par, pre, main, post):
                if main:
                    expert = dve.value_load(routes.expert[0:1, bass.ds(i, 1)], min_val=0, max_val=E1 - 1)
                    nm.vector_stats(dve, i + 1)
                if post:
                    need(dve, s["y_ps"], i)
                    need(dve, stored[1 - par], landed(half + par - 2))
                    dve.tensor_copy(y[1 - par][:, :], ps_y[:, 0:D]).then_inc(s["y_sb"], 1)
                if main:
                    need(dve, s["hg"], i)
                    nm.vector_scale(dve, i + 1, hn[:, :])
                    need(dve, nm.normed, i + 1)
                    need(dve, s["hb"], i)
                    dve.tensor_tensor(hg[:, :], hn[:, :], gb[:, 0, expert, :], ALU.mult).then_inc(s["hg"], 1)
                    need(dve, s["hg"], i + 1)
                    need(dve, s["ha"], i)
                    dve.tensor_tensor(hb[:, :], hg[:, :], gb[:, 1, expert, :], ALU.add).then_inc(s["hb"], 1)
            tile_steps(dve, routes.tiles, body)
    st.end()


def combine(nc, routes, x_in, ys, out):
    st = Stage(nc, "fin")
    both = (0, 1)
    x = [st.sb(f"x{k}", [ROWS, D]) for k in both]
    pick = [[st.sb(f"pick{n}_{k}", [ROWS, D]) for k in both] for n in both]
    part = st.sb("part", [ROWS, D])
    minus_half = st.sb("minus_half", [P, 1])
    tick = st.sb("tick", [ROWS, 1])
    xo = [st.sb(f"xo{k}", [ROWS, D]) for k in both]
    nm = Norm(st, "nm")
    half_set, part_done = st.sem("half"), st.sem("part")
    x_landed, stored = ([st.sem(f"{n}{k}") for k in both] for n in ("x_landed", "stored"))
    pick_landed = [[st.sem(f"pick_landed{n}_{k}") for k in both] for n in both]

    with st.block() as block:
        @block.sync
        def _(sp):
            def body(i, half, par, pre, main, post):
                if pre:
                    need(sp, part_done, i)
                    sp.dma_start(x[1 - par][:, :], x_in[i + 1]).then_inc(x_landed[1 - par], 16)
                if post:
                    need(sp, nm.normed, i)
                    sp.dma_start(out[i - 1], xo[1 - par][:, :]).then_inc(stored[1 - par], 16)
            steps(sp, body)
            for k in both:
                sp.wait_ge(stored[k], landed(SEQS // 2 - 1))

        @block.gpsimd
        def _(pool):
            pool.memset(minus_half[:, :], -0.5).then_inc(half_set, 1)
            pool.wait_ge(half_set, 1)

            def fetch(b):
                if b >= 2:
                    pool.wait_ge(nm.y_sb, b - 1)
                for n in both:
                    pool.indirect_dma_start(pick[n][b % 2][:, :], None, ys, bass.IndirectOffsetOnAxis(ap=routes.slot[:, n, b:b + 1], axis=0)).then_inc(pick_landed[n][b % 2], 16)
            fetch(0)
            for b in range(SEQS):
                if b + 1 < SEQS:
                    fetch(b + 1)
                nm.pool_rstd(pool, b + 1, minus_half[0:ROWS, :])

        @block.vector
        def _(dve):
            def body(i, half, par, pre, main, post):
                if main:
                    need(dve, x_landed[par], landed(half))
                    need(dve, pick_landed[0][par], landed(half))
                    dve.memset(tick[:, :], 0.0)
                    dve.scalar_tensor_tensor(part[:, :], pick[0][par][:, :], routes.weight[:, 0, bass.ds(i, 1)], x[par][:, :], ALU.mult, ALU.add).then_inc(part_done, 1)
                    need(dve, part_done, i + 1)
                    need(dve, pick_landed[1][par], landed(half))
                    dve.memset(tick[:, :], 0.0)
                    dve.scalar_tensor_tensor(nm.y[:, :], pick[1][par][:, :], routes.weight[:, 1, bass.ds(i, 1)], part[:, :], ALU.mult, ALU.add).then_inc(nm.y_sb, 1)
                    nm.vector_stats(dve, i + 1)
                    need(dve, stored[par], landed(half - 1))
                    nm.vector_scale(dve, i + 1, xo[par][:, :])
            steps(dve, body)
    st.end()


def clear(nc, xs):
    st = Stage(nc, "clear")
    zeros = st.sb("zeros", [P, D])
    zeroed, stored = st.sem("zeroed"), st.sem("stored")
    with st.block() as block:
        @block.gpsimd
        def _(pool):
            pool.memset(zeros[:, :], 0.0).then_inc(zeroed, 1)

        @block.sync
        def _(sp):
            sp.wait_ge(zeroed, 1)
            for t in range(FFN1_TILES):
                sp.dma_start(xs[t], zeros[:, :]).then_inc(stored, 16)
            sp.wait_ge(stored, 16 * FFN1_TILES)
    st.end()


def decoder(nc, dram, out):
    def scratch(name, shape):
        return nc.dram_tensor(name, shape, F32, kind="Internal").ap()

    x1, x2, x4, x5 = (scratch(f"x{n}", [SEQS, ROWS, D]) for n in (1, 2, 4, 5))
    xs, ys = (scratch(n, [FFN1_TILES, P, D]) for n in ("xs", "ys"))
    xs_rows, ys0_rows, ys_rows = (t.rearrange("t p d -> (t p) d") for t in (xs, ys[0:FFN0_TILES], ys))

    clear(nc, xs)
    self_attention(nc, dram, dram["x"], x1)
    cross_attention(nc, dram, "xa0", x1, x2)
    with ExitStack() as stack:
        routes = Routes(nc, stack, "r0", E0, FFN0_TILES)
        router(nc, dram, routes, x2, xs_rows, F32_EPS, 0.0, False)
        relu_experts(nc, dram, routes, xs, ys)
        recurrence(nc, dram, routes, x2, ys0_rows, x4)
    cross_attention(nc, dram, "xa1", x4, x5, dram["mask"])
    with ExitStack() as stack:
        routes = Routes(nc, stack, "r1", E1, FFN1_TILES)
        router(nc, dram, routes, x5, xs_rows, 0.0, 1e-9, True)
        gelu_experts(nc, dram, routes, xs, ys)
        combine(nc, routes, x5, ys_rows, out)


def layout(inputs):
    f32 = np.float32
    a = {k: np.asarray(v) for k, v in inputs.items()}

    def chunked(w):
        return w.reshape(-1, P, w.shape[-1]).transpose(1, 0, 2)

    def columns(b):
        return b.reshape(-1, P).T

    def every(b):
        return np.broadcast_to(b[None, :], (P, b.shape[0]))

    split = np.concatenate([np.arange(0, D, 2), np.arange(1, D, 2)])
    ipw, ipb = a["L0_attn_in_proj_w"], a["L0_attn_in_proj_b"]
    i = np.arange(D // 2, dtype=f32)
    theta = (f32(10000.0) ** (f32(-2.0) * (i - f32(1.0)) / f32(D))).astype(f32)
    angle = (theta[:, None] * np.arange(ROWS, dtype=f32)[None, :]).astype(f32)
    t = {
        "x": a["x"],
        "sa_w1": np.stack([chunked(a[f"L0_attn_w{c}"][split].T) for c in "qkv"], axis=1),
        "sa_w2": np.stack([chunked(ipw[n * D:(n + 1) * D][:, split].T) for n in range(3)], axis=1),
        "sa_wo": chunked(a["L0_attn_out_w"].T),
        "sa_bqk": np.stack([columns(ipb[0:D]), columns(ipb[D:2 * D])], axis=1),
        "sa_bv": every(ipb[2 * D:]),
        "sa_bo": every(a["L0_attn_out_b"]),
        "ident": np.eye(P, dtype=f32),
        "causal": np.where(np.tril(np.ones((ROWS, ROWS), bool)), f32(0), f32(MASKED)),
        "rope": np.stack([np.cos(angle), np.sin(angle)], axis=1).astype(f32),
        "head_mask": (np.arange(P)[:, None] // HD == np.arange(HPC)[None, :]).astype(f32),
    }
    t["ctxT"] = a["ctx_1024"].reshape(SEQS, KEYS, KC, P).transpose(0, 3, 2, 1)
    t["mask"] = a["mask_Bx1xSxS2_ik1"].reshape(SEQS, ROWS, KEYS)
    for n, w, b, turn in (("xa0", "L0_xattn_w{}_w", "L0_xattn_w{}_b", True), ("xa1", "L1_xattn_w{}", "L1_xattn_b{}", False)):
        for c in "qkvo":
            wn, bn = (("L0_xattn_dense_w", "L0_xattn_dense_b") if turn and c == "o" else (w.format(c), b.format(c)))
            t[f"{n}_w{c}"] = chunked(a[wn].T if turn else a[wn])
            t[f"{n}_b{c}"] = a[bn]
        t[f"{n}_bqk"] = np.stack([columns(t.pop(f"{n}_bq")), columns(t.pop(f"{n}_bk"))], axis=1)
        for c in "vo":
            t[f"{n}_b{c}"] = every(t[f"{n}_b{c}"])
    t["before"] = np.triu(np.ones((ROWS, ROWS), f32), 1)
    t["iota"] = np.broadcast_to(np.arange(P, dtype=f32)[None, :], (P, P))
    for n, e in (("r0", E0), ("r1", E1)):
        t[f"{n}_chain"] = np.broadcast_to((np.arange(SEQS) > 0).astype(f32)[None, None, :], (P, e, SEQS))
    t["r0_wr"] = chunked(a["L0_ffn_Wr"].T)
    t["r0_br"] = np.zeros((P, E0), f32)
    t["r1_wr"] = chunked(a["L1_ffn_Wr"])
    t["r1_br"] = every(a["L1_ffn_br"])
    t["ff0_w"] = np.concatenate([a[f"L0_ffn_W{c}"].transpose(0, 2, 1).reshape(E0, KC, P, F0).transpose(0, 2, 1, 3).reshape(E0, P, KC * F0) for c in "gu"]
                                + [a["L0_ffn_Wd"].transpose(0, 2, 1).reshape(E0, F0 // P, P, D).transpose(0, 2, 1, 3).reshape(E0, P, F0 // P * D)], axis=2)
    t["rec_win"] = np.stack([chunked(a[f"L1_attn_W_{n}"].T) for n in ("delta", "in", "select", "gate")], axis=1)
    t["rec_wout"] = chunked(a["L1_attn_W_out"].T)
    t["rec_la"] = columns(a["L1_attn_log_a"])
    for n in (1, 2):
        t[f"ff1_w{n}"] = a[f"L1_ffn_W{n}"].reshape(E1, KC, P, -1).transpose(2, 0, 1, 3)
        t[f"ff1_b{n}"] = a[f"L1_ffn_b{n}"][None]
    t["ff1_gb"] = np.broadcast_to(np.stack([a["L1_ffn_g1"], a["L1_ffn_be1"]])[None], (P, 2, E1, F1))
    return {k: np.ascontiguousarray(v) for k, v in t.items()}


def kernel(**inputs):
    import concourse.bacc as bacc
    from concourse.bass_utils import run_bass_kernel_spmd

    nc = bacc.Bacc("TRN2", target_bir_lowering=False, num_devices=1)
    arrays = {f"in_{k}": v for k, v in layout(inputs).items()}
    dram = {k[3:]: nc.dram_tensor(k, v.shape, mybir.dt.from_np(v.dtype), kind="ExternalInput").ap() for k, v in arrays.items()}
    out = nc.dram_tensor("out", (SEQS, ROWS, D), F32, kind="ExternalOutput").ap()
    decoder(nc, dram, out)
    r = run_bass_kernel_spmd(nc, [arrays], core_ids=[0])
    return r.results[0]["out"]
```

```python
from contextlib import ExitStack

import numpy as np

import concourse.bass as bass
from concourse import mybir

F32 = mybir.dt.float32
BF16 = mybir.dt.bfloat16
I32 = mybir.dt.int32
U32 = mybir.dt.uint32
ALU = mybir.AluOpType
ACT = mybir.ActivationFunctionType
AX = mybir.AxisListType

P = 128
SEQS = 16
ROWS = 100
D = 256
KC = D // P
HEADS = 16
HD = D // HEADS
HPC = P // HD
KEYS = 361
KT = [(0, 121), (121, 120), (241, 120)]
KTW = 121
BANK = 512
VW = 32
MASKED = -1e30
LN_EPS = 1e-5
E0, F0 = 8, 1024
E1, F1 = 16, 256
PAIRS = SEQS * ROWS * 2
FFN0_TILES = (PAIRS + E0 * (P - 1)) // P
FFN1_TILES = (PAIRS + E1 * (P - 1)) // P
F32_EPS = float(np.finfo(np.float32).eps)


def need(eng, sem, count):
    if isinstance(count, int) and count <= 0:
        return
    eng.wait_ge(sem, count)


def landed(half):
    return 16 * (half + 1)


class At:

    def __init__(self, i, turn, place, n, ring):
        self.i, self.turn, self.place, self.n, self.ring = i, turn, place, n, ring

    def on(self, k):
        return not isinstance(self.i, int) or 0 <= self.i + k < self.n

    def slot(self, k, ring=None):
        return (self.place + k) % (ring or self.ring)

    def nth(self, k, ring=None):
        ring = ring or self.ring
        return self.ring // ring * self.turn + (self.place + k) // ring

    def landed(self, k, ring=None):
        return 16 * (self.nth(k, ring) + 1)


def pipeline(eng, n, ahead, behind, first, body, ring=2):
    turns = (n - ahead - first) // ring
    for i in range(-ahead, first):
        body(At(i, i // ring, i % ring, n, ring))
    with eng.Fori(0, turns) as t:
        for k in range(ring):
            i = first + k
            body(At(t * ring + i, t + i // ring, i % ring, n, ring))
    for i in range(first + turns * ring, n + behind):
        body(At(i, i // ring, i % ring, n, ring))


def steps(eng, body, n=SEQS):
    def one(at):
        body(at.i, at.turn, at.place, at.on(1), at.on(0), at.on(-1))
    pipeline(eng, n, 1, 1, 3, one)


class Stage:

    def __init__(self, nc, name):
        self.nc, self.name, self.stack, self.sems = nc, name, ExitStack(), []

    def sb(self, name, shape, dt=F32):
        return self.stack.enter_context(self.nc.sbuf_tensor(f"{self.name}_{name}", shape, dt))

    def ps(self, name, shape, dt=F32):
        return self.stack.enter_context(self.nc.psum_tensor(f"{self.name}_{name}", shape, dt))

    def sem(self, name):
        self.sems.append(self.nc.alloc_semaphore(f"{self.name}_{name}"))
        return self.sems[-1]

    def block(self):
        return self.nc.Block()

    def end(self):
        self.nc.clear_and_free_semaphores(self.sems)
        self.nc.all_engine_barrier()
        self.stack.close()


def self_attention(nc, dram, x_in, x_out):
    st = Stage(nc, "sa")
    x = [st.sb(f"x{k}", [ROWS, D]) for k in (0, 1)]
    xb = [st.sb(f"xb{k}", [ROWS, D]) for k in (0, 1)]
    xT = st.sb("xT", [P, KC, ROWS])
    w1 = st.sb("w1", [P, 3, KC, D])
    w2 = st.sb("w2", [P, 3, KC, D])
    wo = st.sb("wo", [P, KC, D])
    bqk = st.sb("bqk", [P, 2, KC])
    bv = st.sb("bv", [P, D])
    bo = st.sb("bo", [P, D])
    ident = st.sb("ident", [P, P])
    identb = st.sb("identb", [P, P], BF16)
    causal = st.sb("causal", [ROWS, ROWS])
    causalb = st.sb("causalb", [ROWS, 4, ROWS], BF16)
    cs = st.sb("cs", [P, 2, ROWS])
    hm = st.sb("hm", [P, HPC])
    pc = st.sb("pc", [P, 3, 2, ROWS])
    psn = st.sb("psn", [P, 3, 2, ROWS])
    rot = st.sb("rot", [P, 3, KC, ROWS])
    qT = st.sb("qT", [P, KC, ROWS])
    kT = st.sb("kT", [P, KC, ROWS])
    qm = st.sb("qm", [P, KC, HPC, ROWS])
    va = [st.sb(f"va{k}", [ROWS, HEADS, VW]) for k in (0, 1)]
    mx = st.sb("mx", [ROWS, HEADS])
    sh = st.sb("sh", [ROWS, HEADS, ROWS])
    pr = st.sb("pr", [ROWS, HEADS, ROWS])
    pT = st.sb("pT", [ROWS, HEADS, ROWS])
    oT = st.sb("oT", [P, 4, ROWS])
    rden = st.sb("rden", [ROWS, HEADS])
    o = st.sb("o", [ROWS, D])
    oT2 = st.sb("oT2", [P, KC, ROWS])
    y = st.sb("y", [ROWS, D])
    stat = st.sb("stat", [ROWS, 6])
    mv = st.sb("mv", [ROWS, 2])
    ve = st.sb("ve", [ROWS, 1])
    rstd = st.sb("rstd", [ROWS, 1])
    tick = st.sb("tick", [ROWS, 1])
    minus_half = st.sb("minus_half", [P, 1])
    xo = [st.sb(f"xo{k}", [ROWS, D]) for k in (0, 1)]

    ps_s = st.ps("ps_s", [P, 4, BANK])
    ps_o = st.ps("ps_o", [P, 2, BANK])
    ps_p = st.ps("ps_p", [P, 2, BANK])
    prj = ps_p[:, :, :].rearrange("p a b -> p (a b)")[:, 0:3 * D].rearrange("p (w n) -> p w n", w=3)[:, :, 0:KC * ROWS]

    s = {n: st.sem(n) for n in (
        "w_in", "const", "zeros", "xT_ps", "xT_sb", "prj1", "rope_mul", "rope", "qk_ps", "v_ps", "q_sb",
        "k_sb", "v_sb", "qm", "xb", "o_ps", "oT_sb", "otr_ps", "rden", "o_sb", "oT2_ps", "oT2_sb", "y_ps", "y_sb",
        "stat", "mv", "ve", "rstd", "xo")}
    scores, maxed, shifted, probs, pt_ps, pt_sb = ([st.sem(f"{n}{j}") for j in range(4)] for n in ("scores", "max", "shifted", "probs", "pt_ps", "pt_sb"))
    x_landed = [st.sem(f"x_landed{k}") for k in (0, 1)]
    stored = [st.sem(f"stored{k}") for k in (0, 1)]

    with st.block() as block:
        @block.sync
        def _(sp):
            def load(t, a):
                sp.dma_start(t, a).then_inc(s["w_in"], 16)
            load(w1[:, :, :, :], dram["sa_w1"])
            load(ident[:, :], dram["ident"])
            load(cs[:, :, :], dram["rope"])
            load(w2[:, :, :, :], dram["sa_w2"])
            load(hm[:, :], dram["head_mask"])
            load(bqk[:, :, :], dram["sa_bqk"])
            load(bv[:, :], dram["sa_bv"])
            load(bo[:, :], dram["sa_bo"])
            load(wo[:, :, :], dram["sa_wo"])
            load(causal[:, :], dram["causal"])

            def body(at):
                i = at.i
                if at.on(2):
                    need(sp, s["xb"], i + 1)
                    need(sp, s["xT_ps"], i + 1)
                    sp.dma_start(x[at.slot(2)][:, :], x_in[i + 2]).then_inc(x_landed[at.slot(2)], 16)
                if at.on(-1):
                    need(sp, s["xo"], i)
                    sp.dma_start(x_out[i - 1], xo[at.slot(-1)][:, :]).then_inc(stored[at.slot(-1)], 16)
            pipeline(sp, SEQS, 2, 1, 2, body)
            for par in (0, 1):
                sp.wait_ge(stored[par], landed(SEQS // 2 - 1))

        @block.gpsimd
        def _(pool):
            pool.memset(minus_half[:, :], -0.5).then_inc(s["zeros"], 1)
            for k in (0, 1):
                pool.memset(va[k][:, :, :], 0.0).then_inc(s["zeros"], 1)
            pool.wait_ge(s["zeros"], 3)
            for k in (0, 1):
                pool.memset(va[k][:, :, HD:HD + 1], 1.0).then_inc(s["zeros"], 1)
            pool.wait_ge(s["w_in"], 160)
            pool.tensor_copy(identb[:, :], ident[:, :]).then_inc(s["const"], 1)
            pool.tensor_copy(causalb[:, :, :], causal[:, :].unsqueeze(1).to_broadcast([ROWS, 4, ROWS])).then_inc(s["const"], 1)
            pool.wait_ge(s["zeros"], 5)

            def body(i, half, par, pre, main, post):
                if main:
                    need(pool, x_landed[par], landed(half))
                    need(pool, s["y_sb"], i - 1)
                    pool.tensor_tensor(xb[par][:, :], x[par][:, :], bo[0:ROWS, :], ALU.add).then_inc(s["xb"], 1)
                if pre:
                    need(pool, s["rope_mul"], i + 2)
                    need(pool, s["v_ps"], i + 1)
                    pool.tensor_tensor(rot[:, :, 0, :], pc[:, :, 0, :], psn[:, :, 1, :], ALU.add)
                    pool.tensor_tensor(rot[:, :, 1, :], pc[:, :, 1, :], psn[:, :, 0, :], ALU.subtract).then_inc(s["rope"], 1)
                    need(pool, s["q_sb"], i + 2)
                    need(pool, scores[3], i + 1)
                    for c in range(KC):
                        done = pool.tensor_tensor(qm[:, c, :, :], qT[:, c, :].unsqueeze(1).to_broadcast([P, HPC, ROWS]),
                                                  hm[:, :].unsqueeze(2).to_broadcast([P, HPC, ROWS]), ALU.mult)
                        done.then_inc(s["qm"], 1)
                if post:
                    need(pool, s["ve"], i)
                    need(pool, s["xo"], i - 1)
                    pool.tensor_tensor(rstd[:, :], ve[:, :], minus_half[0:ROWS, :], ALU.pow).then_inc(s["rstd"], 1)
            steps(pool, body)

        @block.tensor
        def _(pe):
            pe.wait_ge(s["w_in"], 160)
            pe.wait_ge(s["const"], 2)

            def bank_scores(j, i):
                if j % 2 == 0:
                    need(pe, s["qm"], 2 * i + 1 + j // 2)
                need(pe, s["k_sb"], i + 1)
                need(pe, pt_sb[j], i)
                pe.matmul(ps_s[0:ROWS, j, 0:4 * ROWS], identb[0:ROWS, 0:ROWS], causalb[:, :, :], start=True, stop=False)
                for g in range(4):
                    h = 4 * j + g
                    done = pe.matmul(ps_s[0:ROWS, j, g * ROWS:(g + 1) * ROWS], qm[:, h // HPC, h % HPC, :],
                                     kT[:, h // HPC, :], start=False, stop=g == 3)
                done.then_inc(scores[j], 1)

            def bank_transposes(j, i):
                need(pe, shifted[j], i + 1)
                need(pe, probs[j], i + 1)
                for g in range(4):
                    done = pe.transpose(ps_s[0:ROWS, j, g * ROWS:(g + 1) * ROWS], pr[:, 4 * j + g, :], ident[0:ROWS, 0:ROWS])
                done.then_inc(pt_ps[j], 1)

            def body(i, half, par, pre, main, post):
                if pre:
                    need(pe, x_landed[1 - par], landed(half + par))
                    need(pe, s["q_sb"], i + 1)
                    need(pe, s["k_sb"], i + 1)
                    for c in range(KC):
                        done = pe.transpose(ps_p[:, 0, c * ROWS:(c + 1) * ROWS], x[1 - par][:, c * P:(c + 1) * P], ident[0:ROWS, 0:ROWS])
                    done.then_inc(s["xT_ps"], 1)
                if post:
                    need(pe, s["v_sb"], i)
                    need(pe, s["oT2_sb"], i - 1)
                    for j in range(4):
                        need(pe, pt_sb[j], i)
                        for g in range(4):
                            h = 4 * j + g
                            done = pe.matmul(ps_o[g * VW:(g + 1) * VW, 0, j * ROWS:(j + 1) * ROWS], va[1 - par][:, h, :], pT[:, h, :],
                                             start=True, stop=True, tile_position=(0, g * VW))
                    done.then_inc(s["o_ps"], 1)
                if main:
                    bank_scores(0, i)
                    bank_scores(1, i)
                if post:
                    need(pe, s["oT_sb"], i)
                    need(pe, s["y_sb"], i - 1)
                    for j in range(4):
                        done = pe.transpose(ps_o[0:ROWS, 1, j * P:(j + 1) * P], oT[:, j, :], ident[:, :])
                    done.then_inc(s["otr_ps"], 1)
                if pre:
                    need(pe, s["xT_sb"], i + 2)
                    need(pe, s["v_sb"], i + 1)
                    for w in range(3):
                        for m in range(KC):
                            for c in range(KC):
                                done = pe.matmul(prj[:, w, m * ROWS:(m + 1) * ROWS], w1[:, w, c, m * P:(m + 1) * P], xT[:, c, :],
                                                 start=c == 0, stop=c == KC - 1)
                    done.then_inc(s["prj1"], 1)
                if main:
                    bank_scores(2, i)
                if post:
                    need(pe, s["o_sb"], i)
                    for c in range(KC):
                        done = pe.transpose(ps_o[:, 0, c * ROWS:(c + 1) * ROWS], o[:, c * P:(c + 1) * P], ident[0:ROWS, 0:ROWS])
                    done.then_inc(s["oT2_ps"], 1)
                if main:
                    bank_scores(3, i)
                    bank_transposes(0, i)
                if post:
                    need(pe, s["oT2_sb"], i)
                    for c in range(KC):
                        done = pe.matmul(ps_o[0:ROWS, 1, 0:D], oT2[:, c, :], wo[:, c, :], start=c == 0, stop=c == KC - 1)
                    done.then_inc(s["y_ps"], 1)
                if main:
                    bank_transposes(1, i)
                if pre:
                    need(pe, s["rope"], i + 2)
                    for w in range(2):
                        for m in range(KC):
                            for c in range(KC):
                                done = pe.matmul(ps_p[:, 0, (KC * w + m) * ROWS:(KC * w + m + 1) * ROWS], w2[:, w, c, m * P:(m + 1) * P],
                                                 rot[:, w, c, :], start=c == 0, stop=c == KC - 1)
                    done.then_inc(s["qk_ps"], 1)
                if main:
                    bank_transposes(2, i)
                if pre:
                    for c in range(KC):
                        done = pe.matmul(ps_p[0:ROWS, 1, 0:D], rot[:, 2, c, :], w2[:, 2, c, :], start=c == 0, stop=c == KC - 1)
                    done.then_inc(s["v_ps"], 1)
                if main:
                    bank_transposes(3, i)
            steps(pe, body)

        @block.scalar
        def _(act):
            act.wait_ge(s["w_in"], 160)

            def exponentials(j, i):
                need(act, shifted[j], i + 1)
                need(act, pt_ps[j], i)
                act.activation(pr[:, 4 * j:4 * j + 4, :], sh[:, 4 * j:4 * j + 4, :], ACT.Exp).then_inc(probs[j], 1)

            def copy_transposed(j, i):
                need(act, pt_ps[j], i + 1)
                if j == 0:
                    need(act, s["o_ps"], i)
                act.activation(pT[:, 4 * j:4 * j + 4, :], ps_s[0:ROWS, j, 0:4 * ROWS].rearrange("p (g n) -> p g n", g=4), ACT.Copy).then_inc(pt_sb[j], 1)

            def body(i, half, par, pre, main, post):
                if pre:
                    need(act, s["xT_ps"], i + 2)
                    need(act, s["prj1"], i + 1)
                    act.activation(xT[:, :, :], ps_p[:, 0, 0:KC * ROWS].rearrange("p (c n) -> p c n", c=KC), ACT.Copy).then_inc(s["xT_sb"], 1)
                if post:
                    need(act, s["o_ps"], i)
                    need(act, s["otr_ps"], i - 1)
                    act.activation(oT[:, :, :], ps_o[:, 0, 0:4 * ROWS].rearrange("p (g n) -> p g n", g=4), ACT.Copy).then_inc(s["oT_sb"], 1)
                if main:
                    exponentials(0, i)
                    exponentials(1, i)
                if post:
                    need(act, s["oT2_ps"], i)
                    need(act, s["y_ps"], i - 1)
                    act.activation(oT2[:, :, :], ps_o[:, 0, 0:KC * ROWS].rearrange("p (g n) -> p g n", g=KC), ACT.Copy).then_inc(s["oT2_sb"], 1)
                if main:
                    exponentials(2, i)
                    copy_transposed(0, i)
                    exponentials(3, i)
                    copy_transposed(1, i)
                if pre:
                    need(act, s["q_sb"], i + 2)
                    need(act, scores[3], i + 1)
                    for c in range(KC):
                        done = act.activation(kT[:, c, :], ps_p[:, 0, (KC + c) * ROWS:(KC + c + 1) * ROWS], ACT.Identity, bias=bqk[:, 1, c:c + 1])
                    done.then_inc(s["k_sb"], 1)
                if main:
                    copy_transposed(2, i)
                    copy_transposed(3, i)
            steps(act, body)

        @block.vector
        def _(dve):
            dve.wait_ge(s["w_in"], 160)
            dve.wait_ge(s["zeros"], 5)

            def shift(banks, i):
                for j in banks:
                    need(dve, scores[j], i + 1)
                    dve.tensor_reduce(mx[:, 4 * j:4 * j + 4], ps_s[0:ROWS, j, 0:4 * ROWS].rearrange("p (g n) -> p g n", g=4), AX.X, ALU.max).then_inc(maxed[j], 1)
                for j in banks:
                    need(dve, maxed[j], i + 1)
                    need(dve, probs[j], i)
                    dve.tensor_tensor(sh[:, 4 * j:4 * j + 4, :], ps_s[0:ROWS, j, 0:4 * ROWS].rearrange("p (g n) -> p g n", g=4),
                                      mx[:, 4 * j:4 * j + 4].unsqueeze(2).to_broadcast([ROWS, 4, ROWS]), ALU.subtract).then_inc(shifted[j], 1)

            def body(i, half, par, pre, main, post):
                if main:
                    shift((0, 1), i)
                if post:
                    need(dve, s["otr_ps"], i)
                    heads = ps_o[0:ROWS, 1, :].rearrange("p (h w) -> p h w", w=VW)
                    dve.reciprocal(rden[:, :], heads[:, :, HD]).then_inc(s["rden"], 1)
                    need(dve, s["rden"], i)
                    need(dve, s["oT2_ps"], i - 1)
                    dve.tensor_tensor(o[:, :].rearrange("p (h d) -> p h d", h=HEADS), heads[:, :, 0:HD],
                                      rden[:, :].unsqueeze(2).to_broadcast([ROWS, HEADS, HD]), ALU.mult).then_inc(s["o_sb"], 1)
                if pre:
                    need(dve, s["prj1"], i + 2)
                    need(dve, s["rope"], i + 1)
                    for t, n in ((pc, 0), (psn, 1)):
                        for w in range(3):
                            done = dve.tensor_tensor(t[:, w, :, :], prj[:, w, :].rearrange("p (c n) -> p c n", c=KC),
                                                     cs[:, n, :].unsqueeze(1).to_broadcast([P, KC, ROWS]), ALU.mult)
                    done.then_inc(s["rope_mul"], 1)
                if main:
                    shift((2, 3), i)
                if post:
                    need(dve, s["y_ps"], i)
                    need(dve, s["xb"], i)
                    dve.tensor_tensor(y[:, :], ps_o[0:ROWS, 1, 0:D], xb[1 - par][:, :], ALU.add).then_inc(s["y_sb"], 1)
                if pre:
                    need(dve, s["qk_ps"], i + 2)
                    need(dve, s["qm"], 2 * i + 2)
                    for c in range(KC):
                        done = dve.tensor_scalar(qT[:, c, :], ps_p[:, 0, c * ROWS:(c + 1) * ROWS], bqk[:, 0, c:c + 1], HD ** -0.5, ALU.add, ALU.mult)
                    done.then_inc(s["q_sb"], 1)
                if post:
                    need(dve, s["y_sb"], i)
                    dve.bn_stats(stat[:, :], y[:, :]).then_inc(s["stat"], 1)
                    need(dve, s["stat"], i)
                    dve.memset(tick[:, :], 0.0)
                    dve.bn_aggr(mv[:, :], stat[:, :]).then_inc(s["mv"], 1)
                    need(dve, s["mv"], i)
                    dve.tensor_scalar(ve[:, :], mv[:, 1:2], LN_EPS, None, ALU.add).then_inc(s["ve"], 1)
                if pre:
                    need(dve, s["v_ps"], i + 2)
                    need(dve, s["o_ps"], i)
                    dve.tensor_tensor(va[1 - par][:, :, 0:HD], ps_p[0:ROWS, 1, 0:D].rearrange("p (h d) -> p h d", h=HEADS),
                                      bv[0:ROWS, :].rearrange("p (h d) -> p h d", h=HEADS), ALU.add).then_inc(s["v_sb"], 1)
                if post:
                    need(dve, s["rstd"], i)
                    need(dve, stored[1 - par], landed(half + par - 2))
                    dve.tensor_scalar(xo[1 - par][:, :], y[:, :], mv[:, 0:1], rstd[:, 0:1], ALU.subtract, ALU.mult).then_inc(s["xo"], 1)
            steps(dve, body)
    st.end()


def cross_attention(nc, dram, name, x_in, x_out, mask=None):
    st = Stage(nc, name)
    NPAIR = HEADS // 2
    ready = 8 if mask is not None else 7
    both = (0, 1)
    x = [st.sb(f"x{k}", [ROWS, D]) for k in both]
    ctx = [st.sb(f"ctx{k}", [P, KC, KEYS]) for k in both]
    wq, wk, wv, wo = (st.sb(n, [P, KC, D]) for n in ("wq", "wk", "wv", "wo"))
    bqk = st.sb("bqk", [P, 2, KC])
    bv = st.sb("bv", [P, D])
    bo = st.sb("bo", [P, D])
    ident = st.sb("ident", [P, P])
    hm = st.sb("hm", [P, HPC])
    xb = st.sb("xb", [ROWS, D])
    xT = st.sb("xT", [P, KC, ROWS])
    qT = st.sb("qT", [P, KC, ROWS])
    qm = [st.sb(f"qm{k}", [P, KC, HPC, ROWS]) for k in both]
    kT = [st.sb(f"kT{k}", [P, KC, KEYS]) for k in both]
    va = [st.sb(f"va{k}", [KTW, 3, HEADS, VW]) for k in both]
    nmx = [st.sb(f"nmx{k}", [ROWS, HEADS]) for k in both]
    pr = [st.sb(f"pr{k}", [ROWS, 2, 3 * KTW]) for k in both]
    pT = [st.sb(f"pT{k}", [KTW, HEADS, 3, ROWS]) for k in both]
    oT = st.sb("oT", [P, 4, ROWS])
    rden = st.sb("rden", [ROWS, HEADS])
    o = st.sb("o", [ROWS, D])
    oT2 = st.sb("oT2", [P, KC, ROWS])
    y = st.sb("y", [ROWS, D])
    stat = st.sb("stat", [ROWS, 6])
    mv = st.sb("mv", [ROWS, 2])
    ve = st.sb("ve", [ROWS, 1])
    rstd = st.sb("rstd", [ROWS, 1])
    tick = st.sb("tick", [ROWS, 1])
    minus_half = st.sb("minus_half", [P, 1])
    xo = [st.sb(f"xo{k}", [ROWS, D]) for k in both]
    if mask is not None:
        maskid = st.sb("maskid", [P, P], BF16)
        mk = [st.sb(f"mk{k}", [ROWS, KEYS], I32) for k in both]
        mb = [st.sb(f"mb{k}", [ROWS, KEYS], BF16) for k in both]

    ps_s = st.ps("ps_s", [P, 4, BANK])
    ps_t = st.ps("ps_t", [P, 2, BANK])
    ps_p = st.ps("ps_p", [P, BANK])
    ps_o = st.ps("ps_o", [P, BANK])

    s = {n: st.sem(n) for n in (
        "w_in", "zeros", "xT_ps", "xT_sb", "q_ps", "q_sb", "qm", "xb", "mb",
        "o_ps", "oT_sb", "otr_ps", "rden", "o_sb", "oT2_ps", "oT2_sb", "y_ps", "y_sb", "stat", "mv", "ve", "rstd", "xo")}
    k_ps, k_sb = ([st.sem(f"{n}{m}") for m in range(KC)] for n in ("k_ps", "k_sb"))
    v_ps, v_sb = ([st.sem(f"{n}{m}") for m in range(3)] for n in ("v_ps", "v_sb"))
    scores, nmax, probs = ([st.sem(f"{n}{p}") for p in range(NPAIR)] for n in ("scores", "nmax", "probs"))
    pt, pt_sb = ([[st.sem(f"{n}{p}_{g}") for g in both] for p in range(NPAIR)] for n in ("pt", "pt_sb"))
    x_landed, c_landed, m_landed, stored = ([st.sem(f"{n}{k}") for k in both] for n in ("x_landed", "c_landed", "m_landed", "stored"))

    with st.block() as block:
        @block.sync
        def _(sp):
            weights = [(wq, "wq"), (ident, "ident"), (hm, "head_mask"), (bqk, "bqk"), (wk, "wk"), (wv, "wv"), (bv, "bv"), (bo, "bo"), (wo, "wo")]
            for t, n in weights:
                key = n if n in ("ident", "head_mask") else f"{name}_{n}"
                sp.dma_start(t.ap(), dram[key]).then_inc(s["w_in"], 16)

            def body(i, half, par, pre, main, post):
                if pre:
                    nxt, nhalf = 1 - par, half + par
                    need(sp, s["xb"], i)
                    sp.dma_start(x[nxt][:, :], x_in[i + 1]).then_inc(x_landed[nxt], 16)
                    need(sp, v_ps[2], i)
                    sp.dma_start(ctx[nxt][:, :, :], dram["ctxT"][i + 1]).then_inc(c_landed[nxt], 16)
                    if mask is not None:
                        need(sp, s["mb"], i)
                        sp.dma_start(mk[nxt][:, :], mask[i + 1]).then_inc(m_landed[nxt], 16)
                if post:
                    need(sp, s["xo"], i)
                    sp.dma_start(x_out[i - 1], xo[1 - par][:, :]).then_inc(stored[1 - par], 16)
            steps(sp, body)
            for k in both:
                sp.wait_ge(stored[k], landed(SEQS // 2 - 1))

        @block.gpsimd
        def _(pool):
            pool.memset(minus_half[:, :], -0.5).then_inc(s["zeros"], 1)
            for k in both:
                pool.memset(va[k][:, :, :, :], 0.0).then_inc(s["zeros"], 1)
                pool.memset(pr[k][:, :, :], 0.0).then_inc(s["zeros"], 1)
            pool.wait_ge(s["zeros"], 5)
            for k in both:
                pool.memset(va[k][:, :, :, HD:HD + 1], 1.0).then_inc(s["zeros"], 1)
            pool.wait_ge(s["w_in"], 144)
            if mask is not None:
                pool.tensor_scalar(maskid[:, :], ident[:, :], MASKED, None, ALU.mult).then_inc(s["zeros"], 1)
            pool.wait_ge(s["zeros"], ready)

            def body(i, half, par, pre, main, post):
                if pre:
                    nxt = 1 - par
                    need(pool, s["q_sb"], i + 2)
                    need(pool, scores[NPAIR - 1], i)
                    for c in range(KC):
                        done = pool.tensor_tensor(qm[nxt][:, c, :, :], qT[:, c, :].unsqueeze(1).to_broadcast([P, HPC, ROWS]),
                                                  hm[:, :].unsqueeze(2).to_broadcast([P, HPC, ROWS]), ALU.mult)
                    done.then_inc(s["qm"], 1)
                if post:
                    need(pool, s["ve"], i)
                    need(pool, s["xo"], i - 1)
                    pool.tensor_tensor(rstd[:, :], ve[:, :], minus_half[0:ROWS, :], ALU.pow).then_inc(s["rstd"], 1)
                if main:
                    need(pool, x_landed[par], landed(half))
                    need(pool, s["y_sb"], i)
                    pool.tensor_tensor(xb[:, :], x[par][:, :], bo[0:ROWS, :], ALU.add).then_inc(s["xb"], 1)
            steps(pool, body)

        @block.tensor
        def _(pe):
            pe.wait_ge(s["w_in"], 144)
            pe.wait_ge(s["zeros"], ready)

            def pair_scores(p, i, par):
                if p == 0:
                    need(pe, s["qm"], i + 1)
                    for c in range(KC):
                        need(pe, k_sb[c], i + 1)
                    if mask is not None:
                        need(pe, s["mb"], i + 1)
                need(pe, probs[(p - 2) % NPAIR], i + 1 if p >= 2 else i)
                for g in both:
                    h = 2 * p + g
                    bank = ps_s[0:ROWS, 2 * (p % 2) + g, 0:KEYS]
                    if mask is not None:
                        pe.matmul(bank, maskid[0:ROWS, 0:ROWS], mb[par][:, :], start=True, stop=False)
                    done = pe.matmul(bank, qm[par][:, h // HPC, h % HPC, :], kT[par][:, h // HPC, :], start=mask is None, stop=True)
                done.then_inc(scores[p], 1)

            def pair_transposes(p, i):
                need(pe, probs[p], i + 1)
                for g in both:
                    need(pe, pt_sb[(p - 1) % NPAIR][g], i + 1 if p >= 1 else i)
                    for k in range(3):
                        done = pe.transpose(ps_t[0:KTW, g, k * ROWS:(k + 1) * ROWS], pr[p % 2][:, g, k * KTW:(k + 1) * KTW], ident[0:ROWS, 0:ROWS])
                    done.then_inc(pt[p][g], 1)

            def pre_step(p, i, half, par):
                nxt, nhalf = 1 - par, half + par
                if p == 0:
                    need(pe, x_landed[nxt], landed(nhalf))
                    need(pe, v_sb[2], i + 1)
                    for c in range(KC):
                        done = pe.transpose(ps_p[:, c * ROWS:(c + 1) * ROWS], x[nxt][:, c * P:(c + 1) * P], ident[0:ROWS, 0:ROWS])
                    done.then_inc(s["xT_ps"], 1)
                if p == 1:
                    need(pe, s["xT_sb"], i + 2)
                    for m in range(KC):
                        for c in range(KC):
                            done = pe.matmul(ps_p[:, m * ROWS:(m + 1) * ROWS], wq[:, c, m * P:(m + 1) * P], xT[:, c, :], start=c == 0, stop=c == KC - 1)
                    done.then_inc(s["q_ps"], 1)
                if p in (2, 3):
                    m = p - 2
                    if m == 0:
                        need(pe, c_landed[nxt], landed(nhalf))
                        need(pe, s["q_sb"], i + 2)
                    else:
                        need(pe, k_sb[0], i + 2)
                    for c in range(KC):
                        done = pe.matmul(ps_p[:, 0:KEYS], wk[:, c, m * P:(m + 1) * P], ctx[nxt][:, c, :], start=c == 0, stop=c == KC - 1)
                    done.then_inc(k_ps[m], 1)
                if p in (4, 5, 6):
                    k = p - 4
                    k0, kn = k * KTW, min(KTW, KEYS - k * KTW)
                    need(pe, k_sb[1] if k == 0 else v_sb[k - 1], i + 2)
                    for c in range(KC):
                        done = pe.matmul(ps_p[0:kn, 0:D], ctx[nxt][:, c, k0:k0 + kn], wv[:, c, :], start=c == 0, stop=c == KC - 1)
                    done.then_inc(v_ps[k], 1)

            def post_step(p, i, par):
                prv = 1 - par
                if p == 1:
                    for g in both:
                        need(pe, pt_sb[NPAIR - 1][g], i)
                    need(pe, s["y_sb"], i - 1)
                    for j in range(4):
                        for k in range(3):
                            for g in range(4):
                                h = 4 * j + g
                                done = pe.matmul(ps_o[g * VW:(g + 1) * VW, j * ROWS:(j + 1) * ROWS], va[prv][:, k, h, :], pT[prv][:, h, k, :],
                                                 start=k == 0, stop=k == 2, tile_position=(0, g * VW))
                    done.then_inc(s["o_ps"], 1)
                if p == 2:
                    need(pe, s["oT_sb"], i)
                    for j in range(4):
                        done = pe.transpose(ps_o[0:ROWS, j * P:(j + 1) * P], oT[:, j, :], ident[:, :])
                    done.then_inc(s["otr_ps"], 1)
                if p == 3:
                    need(pe, s["o_sb"], i)
                    for c in range(KC):
                        done = pe.transpose(ps_o[:, c * ROWS:(c + 1) * ROWS], o[:, c * P:(c + 1) * P], ident[0:ROWS, 0:ROWS])
                    done.then_inc(s["oT2_ps"], 1)
                if p == 4:
                    need(pe, s["oT2_sb"], i)
                    for c in range(KC):
                        done = pe.matmul(ps_o[0:ROWS, 0:D], oT2[:, c, :], wo[:, c, :], start=c == 0, stop=c == KC - 1)
                    done.then_inc(s["y_ps"], 1)

            def body(i, half, par, pre, main, post):
                for p in range(NPAIR):
                    if main:
                        pair_scores(p, i, par)
                    if pre:
                        pre_step(p, i, half, par)
                    if p == 0 and post:
                        pair_transposes(NPAIR - 1, i - 1)
                    if post:
                        post_step(p, i, par)
                    if p >= 1 and main:
                        pair_transposes(p - 1, i)
            steps(pe, body)

        @block.scalar
        def _(act):
            act.wait_ge(s["w_in"], 144)
            act.wait_ge(s["zeros"], 7)

            def copy_odd(p, i, par):
                need(act, pt[p][1], i + 1)
                if p == 0:
                    need(act, s["o_ps"], i - 1)
                act.activation(pT[par][:, 2 * p + 1, :, :], ps_t[0:KTW, 1, 0:3 * ROWS].rearrange("p (k n) -> p k n", k=3), ACT.Copy).then_inc(pt_sb[p][1], 1)

            def body(i, half, par, pre, main, post):
                for p in range(NPAIR):
                    if main:
                        need(act, nmax[p], i + 1)
                        need(act, pt[(p - 2) % NPAIR][1], i + 1 if p >= 2 else i)
                        for g in both:
                            h = 2 * p + g
                            done = act.activation(pr[p % 2][:, g, 0:KEYS], ps_s[0:ROWS, 2 * (p % 2) + g, 0:KEYS], ACT.Exp, bias=nmx[par][:, h:h + 1])
                        done.then_inc(probs[p], 1)
                    if pre and p in (2, 3):
                        m = p - 2
                        need(act, k_ps[m], i + 2)
                        need(act, scores[NPAIR - 1], i)
                        act.activation(kT[1 - par][:, m, :], ps_p[:, 0:KEYS], ACT.Identity, bias=bqk[:, 1, m:m + 1]).then_inc(k_sb[m], 1)
                    if p == 0 and post:
                        copy_odd(NPAIR - 1, i - 1, 1 - par)
                    if p >= 1 and main:
                        copy_odd(p - 1, i, par)
                    if p == 1 and post:
                        need(act, s["o_ps"], i)
                        need(act, s["otr_ps"], i - 1)
                        act.activation(oT[:, :, :], ps_o[:, 0:4 * ROWS].rearrange("p (g n) -> p g n", g=4), ACT.Copy).then_inc(s["oT_sb"], 1)
                    if p == 3 and post:
                        need(act, s["oT2_ps"], i)
                        need(act, s["y_ps"], i - 1)
                        act.activation(oT2[:, :, :], ps_o[:, 0:KC * ROWS].rearrange("p (g n) -> p g n", g=KC), ACT.Copy).then_inc(s["oT2_sb"], 1)
            steps(act, body)

        @block.vector
        def _(dve):
            dve.wait_ge(s["w_in"], 144)
            dve.wait_ge(s["zeros"], 7)

            def copy_even(p, i, par):
                need(dve, pt[p][0], i + 1)
                if p == 0:
                    need(dve, s["o_ps"], i - 1)
                dve.tensor_copy(pT[par][:, 2 * p, :, :], ps_t[0:KTW, 0, 0:3 * ROWS].rearrange("p (k n) -> p k n", k=3)).then_inc(pt_sb[p][0], 1)

            def pre_step(p, i, half, par):
                if p == 7 and mask is not None:
                    need(dve, m_landed[1 - par], landed(half + par))
                    need(dve, scores[NPAIR - 1], i)
                    dve.tensor_scalar(mb[1 - par][:, :], mk[1 - par][:, :], 0.0, None, ALU.is_equal).then_inc(s["mb"], 1)
                if p == 0:
                    need(dve, s["xT_ps"], i + 2)
                    dve.tensor_copy(xT[:, :, :], ps_p[:, 0:KC * ROWS].rearrange("p (c n) -> p c n", c=KC)).then_inc(s["xT_sb"], 1)
                if p == 1:
                    need(dve, s["q_ps"], i + 2)
                    need(dve, s["qm"], i + 1)
                    for c in range(KC):
                        done = dve.tensor_scalar(qT[:, c, :], ps_p[:, c * ROWS:(c + 1) * ROWS], bqk[:, 0, c:c + 1], HD ** -0.5, ALU.add, ALU.mult)
                    done.then_inc(s["q_sb"], 1)
                if p in (4, 5, 6):
                    k = p - 4
                    kn = min(KTW, KEYS - k * KTW)
                    need(dve, v_ps[k], i + 2)
                    need(dve, s["o_ps"], i)
                    dve.tensor_tensor(va[1 - par][0:kn, k, :, 0:HD], ps_p[0:kn, 0:D].rearrange("p (h d) -> p h d", h=HEADS),
                                      bv[0:kn, :].rearrange("p (h d) -> p h d", h=HEADS), ALU.add).then_inc(v_sb[k], 1)

            def post_step(p, i, half, par):
                prv, phalf = 1 - par, half + par - 1
                if p == 2:
                    need(dve, s["otr_ps"], i)
                    heads = ps_o[0:ROWS, :].rearrange("p (h w) -> p h w", w=VW)
                    dve.reciprocal(rden[:, :], heads[:, :, HD]).then_inc(s["rden"], 1)
                    need(dve, s["rden"], i)
                    dve.tensor_tensor(o[:, :].rearrange("p (h d) -> p h d", h=HEADS), heads[:, :, 0:HD],
                                      rden[:, :].unsqueeze(2).to_broadcast([ROWS, HEADS, HD]), ALU.mult).then_inc(s["o_sb"], 1)
                if p == 4:
                    need(dve, s["y_ps"], i)
                    need(dve, s["xb"], i)
                    dve.tensor_tensor(y[:, :], ps_o[0:ROWS, 0:D], xb[:, :], ALU.add).then_inc(s["y_sb"], 1)
                if p == 5:
                    need(dve, s["y_sb"], i)
                    dve.bn_stats(stat[:, :], y[:, :]).then_inc(s["stat"], 1)
                    need(dve, s["stat"], i)
                    dve.memset(tick[:, :], 0.0)
                    dve.bn_aggr(mv[:, :], stat[:, :]).then_inc(s["mv"], 1)
                    need(dve, s["mv"], i)
                    dve.tensor_scalar(ve[:, :], mv[:, 1:2], LN_EPS, None, ALU.add).then_inc(s["ve"], 1)
                if p == 6:
                    need(dve, s["rstd"], i)
                    need(dve, stored[prv], landed(phalf - 1))
                    dve.tensor_scalar(xo[prv][:, :], y[:, :], mv[:, 0:1], rstd[:, 0:1], ALU.subtract, ALU.mult).then_inc(s["xo"], 1)

            def body(i, half, par, pre, main, post):
                for p in range(NPAIR):
                    if main:
                        need(dve, scores[p], i + 1)
                        if p == 0:
                            need(dve, probs[NPAIR - 1], i - 1)
                        dve.tensor_reduce(nmx[par][:, 2 * p:2 * p + 2], ps_s[0:ROWS, 2 * (p % 2):2 * (p % 2) + 2, 0:KEYS], AX.X, ALU.max,
                                          negate=True).then_inc(nmax[p], 1)
                    if p == 0 and post:
                        copy_even(NPAIR - 1, i - 1, 1 - par)
                    if pre:
                        pre_step(p, i, half, par)
                    if p >= 1 and main:
                        copy_even(p - 1, i, par)
                    if post:
                        post_step(p, i, half, par)
            steps(dve, body)
    st.end()


class Routes:

    def __init__(self, nc, stack, name, experts, tiles):
        def sb(n, shape, dt):
            return stack.enter_context(nc.sbuf_tensor(f"{name}_{n}", shape, dt))
        self.name, self.experts, self.tiles = name, experts, tiles
        self.slot = sb("slot", [ROWS, 2, SEQS], I32)
        self.weight = sb("weight", [ROWS, 2, SEQS], F32)
        self.expert = sb("expert", [P, tiles], I32)
        self.ring = sb("ring", [P, tiles], I32)
        self.end = sb("end", [P, experts], I32)


RING = 3


def router(nc, dram, routes, x_in, xs, norm_eps, norm_min, bias):
    E, T = routes.experts, routes.tiles
    st = Stage(nc, routes.name)
    xa = st.sb("xa", [ROWS, SEQS, D])
    wr = st.sb("wr", [P, KC, E])
    br = st.sb("br", [P, E])
    ident = st.sb("ident", [P, P])
    before = st.sb("before", [ROWS, ROWS])
    ones = st.sb("ones", [ROWS, ROWS])
    iota = st.sb("iota", [P, P])
    chain = st.sb("chain", [P, E, SEQS])
    xT = [st.sb(f"xT{k}", [P, KC, ROWS]) for k in (0, 1)]
    lg = st.sb("lg", [ROWS, SEQS, E])
    top = st.sb("top", [ROWS, SEQS, 8])
    idx = st.sb("idx", [ROWS, SEQS, 8], U32)
    idf = st.sb("idf", [ROWS, SEQS, 8])
    hot = [st.sb(f"hot{k}", [ROWS, SEQS, E]) for k in (0, 1)]
    hots = st.sb("hots", [ROWS, SEQS, E])
    less = st.sb("less", [ROWS, SEQS, E])
    ex = st.sb("ex", [ROWS, SEQS, E])
    less2 = st.sb("less2", [ROWS, SEQS])
    sc = st.sb("sc", [ROWS, 2, SEQS])
    ex2 = st.sb("ex2", [ROWS, SEQS])
    z = st.sb("z", [ROWS, SEQS])
    rz = st.sb("rz", [ROWS, SEQS])
    sm = st.sb("sm", [ROWS, SEQS])
    sm2 = st.sb("sm2", [ROWS, SEQS])
    rs = st.sb("rs", [ROWS, SEQS])
    tot = st.sb("tot", [ROWS, E, SEQS])
    upto = st.sb("upto", [ROWS, E, SEQS])
    prior = st.sb("prior", [ROWS, E, SEQS])
    nt = st.sb("nt", [ROWS, E], I32)
    nt2 = st.sb("nt2", [ROWS, E], I32)
    ntf = st.sb("ntf", [ROWS, E])
    endf = st.sb("endf", [ROWS, E])
    base = st.sb("base", [ROWS, E])
    base2 = st.sb("base2", [ROWS, E])
    pos = st.sb("pos", [ROWS, SEQS, E])
    pos2 = st.sb("pos2", [ROWS, SEQS, E])
    pk = [st.sb(f"pk{k}", [ROWS, SEQS, E]) for k in (0, 1)]
    slotf = st.sb("slotf", [ROWS, 2, SEQS])
    past = st.sb("past", [ROWS, T, E])
    ef = st.sb("ef", [ROWS, T])
    ef2 = st.sb("ef2", [ROWS, T])
    wrap = [st.sb(f"wrap{k}", [ROWS, T]) for k in range(E // RING)]
    ringf = [st.sb(f"ringf{k}", [ROWS, T]) for k in range(E // RING)]
    ps_x = [st.ps(f"ps_x{k}", [P, BANK]) for k in (0, 1)]
    ps_l = st.ps("ps_l", [P, BANK])
    ps_r = st.ps("ps_r", [P, BANK])
    ps_c = st.ps("ps_c", [P, BANK])
    s = {n: st.sem(n) for n in ("w_in", "x_in", "xT_ps", "xT_sb", "lg_ps", "hots", "rank_ps", "ones", "less", "ex", "slot", "dve", "sent")}

    with st.block() as block:
        @block.sync
        def _(sp):
            for t, n in ((wr.ap(), f"{routes.name}_wr"), (br.ap(), f"{routes.name}_br"), (ident.ap(), "ident"), (before.ap(), "before"),
                         (iota.ap(), "iota"), (chain.ap(), f"{routes.name}_chain")):
                sp.dma_start(t, dram[n]).then_inc(s["w_in"], 16)
            sp.dma_start(xa[:, :, :], x_in.rearrange("s r d -> r s d")).then_inc(s["x_in"], 16)

        @block.gpsimd
        def _(pool):
            pool.memset(ones[:, :], 1.0).then_inc(s["ones"], 1)
            pool.wait_ge(s["x_in"], 16)
            pool.wait_ge(s["slot"], 1)
            for b in range(SEQS):
                for k in (0, 1):
                    pool.indirect_dma_start(xs, bass.IndirectOffsetOnAxis(ap=routes.slot[:, k, b:b + 1], axis=0), xa[:, b, :], None).then_inc(s["sent"], 16)
            pool.wait_ge(s["sent"], 16 * 2 * SEQS)

        @block.tensor
        def _(pe):
            pe.wait_ge(s["w_in"], 96)
            pe.wait_ge(s["x_in"], 16)

            def logits(b):
                pe.wait_ge(s["xT_sb"], b + 1)
                for c in range(KC):
                    done = pe.matmul(ps_l[0:ROWS, b * E:(b + 1) * E], xT[b % 2][:, c, :], wr[:, c, :], start=c == 0, stop=c == KC - 1)
                done.then_inc(s["lg_ps"], 1)

            for b in range(SEQS):
                if b >= 2:
                    pe.wait_ge(s["xT_sb"], b - 1)
                for c in range(KC):
                    done = pe.transpose(ps_x[b % 2][:, c * ROWS:(c + 1) * ROWS], xa[:, b, c * P:(c + 1) * P], ident[0:ROWS, 0:ROWS])
                done.then_inc(s["xT_ps"], 1)
                if b >= 1:
                    logits(b - 1)
            logits(SEQS - 1)
            pe.wait_ge(s["hots"], 1)
            pe.wait_ge(s["ones"], 1)
            flat = hots[:, :, :].rearrange("p s e -> p (s e)")
            pe.matmul(ps_r[0:ROWS, 0:SEQS * E], before[:, :], flat, start=True, stop=True)
            pe.matmul(ps_c[0:ROWS, 0:SEQS * E], ones[:, :], flat, start=True, stop=True).then_inc(s["rank_ps"], 1)

        @block.scalar
        def _(act):
            for b in range(SEQS):
                act.wait_ge(s["xT_ps"], b + 1)
                if b >= 2:
                    act.wait_ge(s["lg_ps"], b - 1)
                act.activation(xT[b % 2][:, :, :], ps_x[b % 2][:, 0:KC * ROWS].rearrange("p (c n) -> p c n", c=KC), ACT.Copy).then_inc(s["xT_sb"], 1)
            act.wait_ge(s["less"], 2)
            act.activation(ex[:, :, :], less[:, :, :], ACT.Exp).then_inc(s["ex"], 1)
            act.activation(ex2[:, :], less2[:, :], ACT.Exp).then_inc(s["ex"], 1)

        @block.vector
        def _(dve):
            count = [0]

            def then(ins):
                count[0] += 1
                ins.then_inc(s["dve"], 1)
                dve.wait_ge(s["dve"], count[0])

            def over(a, n):
                return a.unsqueeze(2).to_broadcast([ROWS, a.shape[1], n])

            def by_seq(a):
                return a.unsqueeze(1).to_broadcast([ROWS, SEQS, E])

            dve.wait_ge(s["w_in"], 96)
            dve.wait_ge(s["ones"], 1)
            dve.wait_ge(s["lg_ps"], SEQS)
            logits = ps_l[0:ROWS, 0:SEQS * E].rearrange("p (s e) -> p s e", s=SEQS)
            if bias:
                then(dve.tensor_tensor(lg[:, :, :], logits, by_seq(br[0:ROWS, :]), ALU.add))
            else:
                then(dve.tensor_copy(lg[:, :, :], logits))
            for b in range(SEQS):
                last = dve.max(top[:, b, :], lg[:, b, :])
            then(last)
            for b in range(SEQS):
                last = dve.max_index(idx[:, b, :], top[:, b, :], lg[:, b, :])
            then(last)
            then(dve.tensor_copy(idf[:, :, :], idx[:, :, :]))
            row = iota[0:ROWS, 0:E].unsqueeze(1).to_broadcast([ROWS, SEQS, E])
            for k in (0, 1):
                last = dve.tensor_tensor(hot[k][:, :, :], row, over(idf[:, :, k], E), ALU.is_equal)
            then(last)
            dve.tensor_tensor(hots[:, :, :], hot[0][:, :, :], hot[1][:, :, :], ALU.add).then_inc(s["hots"], 1)
            dve.tensor_tensor(less[:, :, :], lg[:, :, :], over(top[:, :, 0], E), ALU.subtract).then_inc(s["less"], 1)
            dve.tensor_tensor(less2[:, :], top[:, :, 1], top[:, :, 0], ALU.subtract).then_inc(s["less"], 1)
            dve.wait_ge(s["ex"], 2)
            then(dve.tensor_reduce(z[:, :], ex[:, :, :], AX.X, ALU.add))
            then(dve.reciprocal(rz[:, :], z[:, :]))
            dve.tensor_copy(sc[:, 0, :], rz[:, :])
            then(dve.tensor_tensor(sc[:, 1, :], ex2[:, :], rz[:, :], ALU.mult))
            then(dve.tensor_tensor(sm[:, :], sc[:, 0, :], sc[:, 1, :], ALU.add))
            then(dve.tensor_scalar(sm2[:, :], sm[:, :], norm_eps, norm_min, ALU.add, ALU.max))
            then(dve.reciprocal(rs[:, :], sm2[:, :]))
            for k in (0, 1):
                dve.tensor_tensor(routes.weight[:, k, :], sc[:, k, :], rs[:, :], ALU.mult)
            dve.wait_ge(s["rank_ps"], 1)
            then(dve.tensor_copy(tot[:, :, :], ps_c[0:ROWS, 0:SEQS * E].rearrange("p (s e) -> p e s", s=SEQS)))
            flat = "p e s -> p (e s)"
            then(dve.tensor_tensor_scan(upto[:, :, :].rearrange(flat), chain[0:ROWS, :, :].rearrange(flat), tot[:, :, :].rearrange(flat), 0.0, ALU.mult, ALU.add))
            dve.tensor_tensor(prior[:, :, :], upto[:, :, :], tot[:, :, :], ALU.subtract)
            then(dve.tensor_scalar(nt[:, :], upto[:, :, SEQS - 1], float(P - 1), None, ALU.add))
            then(dve.tensor_scalar(nt2[:, :], nt[:, :], P.bit_length() - 1, None, ALU.logical_shift_right))
            then(dve.tensor_copy(ntf[:, :], nt2[:, :]))
            then(dve.tensor_tensor_scan(endf[:, :], ones[:, 0:E], ntf[:, :], 0.0, ALU.mult, ALU.add))
            dve.tensor_copy(routes.end[0:ROWS, :], endf[:, :])
            then(dve.tensor_tensor(base[:, :], endf[:, :], ntf[:, :], ALU.subtract))
            then(dve.tensor_scalar(base2[:, :], base[:, :], float(P), None, ALU.mult))
            then(dve.tensor_tensor(pos[:, :, :], ps_r[0:ROWS, 0:SEQS * E].rearrange("p (s e) -> p s e", s=SEQS), prior[:, :, :].rearrange("p e s -> p s e"), ALU.add))
            then(dve.tensor_tensor(pos2[:, :, :], pos[:, :, :], by_seq(base2[:, :]), ALU.add))
            for k in (0, 1):
                last = dve.tensor_tensor(pk[k][:, :, :], hot[k][:, :, :], pos2[:, :, :], ALU.mult)
            then(last)
            for k in (0, 1):
                last = dve.tensor_reduce(slotf[:, k, :], pk[k][:, :, :], AX.X, ALU.add)
            then(last)
            dve.tensor_copy(routes.slot[:, :, :], slotf[:, :, :]).then_inc(s["slot"], 1)
            then(dve.tensor_tensor(past[:, :, :], endf[:, :].unsqueeze(1).to_broadcast([ROWS, T, E]), over(iota[0:ROWS, 0:T], E), ALU.is_le))
            then(dve.tensor_reduce(ef[:, :], past[:, :, :], AX.X, ALU.add))
            then(dve.tensor_scalar(ef2[:, :], ef[:, :], float(E - 1), None, ALU.min))
            dve.tensor_copy(routes.expert[0:ROWS, :], ef2[:, :])
            for k in range(E // RING):
                last = dve.tensor_scalar(wrap[k][:, :], ef2[:, :], float(RING * (k + 1)), float(-RING), ALU.is_ge, ALU.mult)
            then(last)
            for k in range(E // RING):
                then(dve.tensor_tensor(ringf[k][:, :], ringf[k - 1][:, :] if k else ef2[:, :], wrap[k][:, :], ALU.add))
            then(dve.tensor_copy(routes.ring[0:ROWS, :], ringf[-1][:, :]))
    st.end()


def relu_experts(nc, dram, routes, xs, ys):
    st = Stage(nc, "ff0")
    HALF = F0 // 2
    GU = 2 * KC * F0
    FC = F0 // P
    w = st.sb("w", [P, RING, GU + FC * D])
    gu = w[:, :, 0:GU].rearrange("p r (m c f) -> p r m c f", m=2, c=KC)
    down = w[:, :, GU:].rearrange("p r (k d) -> p r k d", k=FC)
    ident = st.sb("ident", [P, P])
    x = [st.sb(f"x{k}", [P, D]) for k in (0, 1)]
    xT = [st.sb(f"xT{k}", [P, KC, P]) for k in (0, 1)]
    rg = st.sb("rg", [P, 2, HALF])
    h = st.sb("h", [P, 2, HALF])
    hT = st.sb("hT", [P, FC, P])
    y = [st.sb(f"y{k}", [P, D]) for k in (0, 1)]
    ps_g = [st.ps(f"ps_g{k}", [P, BANK]) for k in (0, 1)]
    ps_u = [st.ps(f"ps_u{k}", [P, BANK]) for k in (0, 1)]
    ps_h = [st.ps(f"ps_h{k}", [P, BANK]) for k in (0, 1)]
    ps_x = st.ps("ps_x", [P, BANK])
    ps_y = st.ps("ps_y", [P, BANK])
    s = {n: st.sem(n) for n in ("w_in", "w_ready", "freed", "tiles_done", "xT_ps", "xT_sb", "y_ps", "y_sb")}
    g_ps, u_ps, rg_sb, h_sb, hT_ps, hT_sb = ([st.sem(f"{n}{k}") for k in (0, 1)] for n in ("g_ps", "u_ps", "rg_sb", "h_sb", "hT_ps", "hT_sb"))
    x_landed, stored = ([st.sem(f"{n}{k}") for k in (0, 1)] for n in ("x_landed", "stored"))
    w_landed = [st.sem(f"w_landed{k}") for k in range(RING)]

    with st.block() as block:
        @block.sync
        def _(sp):
            sp.dma_start(ident[:, :], dram["ident"]).then_inc(s["w_in"], 16)

            def body(i, half, par, pre, main, post):
                if pre:
                    need(sp, s["xT_ps"], i)
                    sp.dma_start(x[1 - par][:, :], xs[i + 1]).then_inc(x_landed[1 - par], 16)
                if post:
                    need(sp, s["y_sb"], i)
                    sp.dma_start(ys[i - 1], y[1 - par][:, :]).then_inc(stored[1 - par], 16)
            steps(sp, body, routes.tiles)
            for k in (0, 1):
                sp.wait_ge(stored[k], landed(routes.tiles // 2 - 1))

        @block.gpsimd
        def _(pool):
            pool.sem_inc(s["tiles_done"], 1)

            def fetch(e):
                pool.dma_start(w[:, e % RING, :], dram["ff0_w"][e]).then_inc(w_landed[e % RING], 16)
            for e in range(RING):
                fetch(e)
            for e in range(E0):
                pool.wait_ge(w_landed[e % RING], 16 * (e // RING + 1))
                pool.sem_inc(s["w_ready"], 1)
                if e + RING < E0:
                    end = pool.value_load(routes.end[0:1, e:e + 1], min_val=0, max_val=routes.tiles)
                    pool.wait_ge(s["tiles_done"], end + 1)
                    pool.sem_inc(s["freed"], 1)
                    fetch(e + RING)

        @block.tensor
        def _(pe):
            pe.wait_ge(s["w_in"], 16)

            def body(i, half, par, pre, main, post):
                if main:
                    expert = pe.value_load(routes.expert[0:1, bass.ds(i, 1)], min_val=0, max_val=E0 - 1)
                    at = pe.value_load(routes.ring[0:1, bass.ds(i, 1)], min_val=0, max_val=RING - 1)
                    pe.wait_ge(s["w_ready"], expert + 1)
                    need(pe, s["xT_sb"], i + 1)
                    for k in (0, 1):
                        for m, bank, read, sem in ((0, ps_g[k], rg_sb[k], g_ps[k]), (1, ps_u[k], h_sb[k], u_ps[k])):
                            need(pe, read, i)
                            for c in range(KC):
                                done = pe.matmul(bank[:, :], xT[par][:, c, :], gu[:, at, m, c, k * HALF:(k + 1) * HALF], start=c == 0, stop=c == KC - 1)
                            done.then_inc(sem, 1)
                if pre:
                    need(pe, x_landed[1 - par], landed(half + par))
                    need(pe, s["xT_sb"], i + 1)
                    for c in range(KC):
                        done = pe.transpose(ps_x[:, c * P:(c + 1) * P], x[1 - par][:, c * P:(c + 1) * P], ident[:, :])
                    done.then_inc(s["xT_ps"], 1)
                if main:
                    for k in (0, 1):
                        need(pe, h_sb[k], i + 1)
                        need(pe, hT_sb[k], i)
                        for q in range(FC // 2):
                            done = pe.transpose(ps_h[k][:, q * P:(q + 1) * P], h[:, k, q * P:(q + 1) * P], ident[:, :])
                        done.then_inc(hT_ps[k], 1)
                    for k in (0, 1):
                        need(pe, hT_sb[k], i + 1)
                        if k == 0:
                            need(pe, s["y_sb"], i)
                        for q in range(k * FC // 2, (k + 1) * FC // 2):
                            done = pe.matmul(ps_y[:, 0:D], hT[:, q, :], down[:, at, q, :], start=q == 0, stop=q == FC - 1)
                    done.then_inc(s["y_ps"], 1)
            steps(pe, body, routes.tiles)

        @block.scalar
        def _(act):
            def body(i, half, par, pre, main, post):
                if main:
                    for k in (0, 1):
                        need(act, g_ps[k], i + 1)
                        need(act, h_sb[k], i)
                        act.activation(rg[:, k, :], ps_g[k][:, :], ACT.Relu).then_inc(rg_sb[k], 1)
                if pre:
                    need(act, s["xT_ps"], i + 2)
                    need(act, u_ps[1], i)
                    act.activation(xT[1 - par][:, :, :], ps_x[:, 0:D].rearrange("p (c n) -> p c n", c=KC), ACT.Copy).then_inc(s["xT_sb"], 1)
                if main:
                    need(act, hT_ps[0], i + 1)
                    need(act, s["y_ps"], i)
                    act.activation(hT[:, 0:FC // 2, :], ps_h[0][:, :].rearrange("p (q n) -> p q n", n=P), ACT.Copy).then_inc(hT_sb[0], 1)
            steps(act, body, routes.tiles)

        @block.vector
        def _(dve):
            def body(i, half, par, pre, main, post):
                if main:
                    for k in (0, 1):
                        need(dve, rg_sb[k], i + 1)
                        need(dve, u_ps[k], i + 1)
                        need(dve, hT_ps[k], i)
                        dve.tensor_tensor(h[:, k, :], ps_u[k][:, :], rg[:, k, :], ALU.mult).then_inc(h_sb[k], 1)
                    need(dve, hT_ps[1], i + 1)
                    need(dve, s["y_ps"], i)
                    dve.tensor_copy(hT[:, FC // 2:, :], ps_h[1][:, :].rearrange("p (q n) -> p q n", n=P)).then_inc(hT_sb[1], 1)
                    need(dve, s["y_ps"], i + 1)
                    need(dve, stored[par], landed(half - 1))
                    dve.tensor_copy(y[par][:, :], ps_y[:, 0:D]).then_inc(s["y_sb"], 1)
                    dve.sem_inc(s["tiles_done"], 1)
            steps(dve, body, routes.tiles)
    st.end()


class Norm:

    def __init__(self, st, name, rows=ROWS, width=D):
        self.y = st.sb(f"{name}_y", [rows, width])
        self.stat = st.sb(f"{name}_stat", [rows, 6])
        self.mv = st.sb(f"{name}_mv", [rows, 2])
        self.ve = st.sb(f"{name}_ve", [rows, 1])
        self.rstd = st.sb(f"{name}_rstd", [rows, 1])
        self.tick = st.sb(f"{name}_tick", [rows, 1])
        self.y_sb, self.stat_done, self.mv_done, self.ve_done, self.rstd_done, self.normed = (
            st.sem(f"{name}_{n}") for n in ("y_sb", "stat", "mv", "ve", "rstd", "normed"))

    def vector_stats(self, dve, n):
        self.vector_sums(dve, n)
        self.vector_mean(dve, n)
        self.vector_variance(dve, n)

    def vector_sums(self, dve, n):
        need(dve, self.y_sb, n)
        dve.bn_stats(self.stat[:, :], self.y[:, :]).then_inc(self.stat_done, 1)

    def vector_mean(self, dve, n):
        need(dve, self.stat_done, n)
        dve.memset(self.tick[:, :], 0.0)
        dve.bn_aggr(self.mv[:, :], self.stat[:, :]).then_inc(self.mv_done, 1)

    def vector_variance(self, dve, n):
        need(dve, self.mv_done, n)
        need(dve, self.rstd_done, n - 1)
        dve.tensor_scalar(self.ve[:, :], self.mv[:, 1:2], LN_EPS, None, ALU.add).then_inc(self.ve_done, 1)

    def pool_rstd(self, pool, n, minus_half):
        need(pool, self.ve_done, n)
        need(pool, self.normed, n - 1)
        pool.tensor_tensor(self.rstd[:, :], self.ve[:, :], minus_half, ALU.pow).then_inc(self.rstd_done, 1)

    def vector_scale(self, dve, n, out):
        need(dve, self.rstd_done, n)
        dve.tensor_scalar(out, self.y[:, :], self.mv[:, 0:1], self.rstd[:, 0:1], ALU.subtract, ALU.mult).then_inc(self.normed, 1)


def recurrence(nc, dram, routes, x_in, ys, x_out):
    st = Stage(nc, "rec")
    both, ring = (0, 1), range(4)
    x = [st.sb(f"x{k}", [ROWS, D]) for k in both]
    pick = [[st.sb(f"pick{n}_{k}", [ROWS, D]) for k in both] for n in both]
    ident = st.sb("ident", [P, P])
    win = st.sb("win", [P, 4, KC, D])
    wout = st.sb("wout", [P, KC, D])
    la = st.sb("la", [P, KC])
    th = st.sb("th", [P, KC])
    minus_a = st.sb("minus_a", [P, KC])
    minus_half = st.sb("minus_half", [P, 1])
    part = st.sb("part", [ROWS, D])
    x3 = [st.sb(f"x3_{k}", [ROWS, D]) for k in ring]
    x3T = [st.sb(f"x3T{k}", [P, KC, ROWS]) for k in both]
    az, ez, lz, sp_, delta, decay, tin, tsel, upd, state = (
        st.sb(n, [P, KC, ROWS]) for n in ("az", "ez", "lz", "sp", "delta", "decay", "tin", "tsel", "upd", "state"))
    tgate, gated = ([st.sb(f"{n}{k}", [P, KC, ROWS]) for k in both] for n in ("tgate", "gated"))
    xo = [st.sb(f"xo{k}", [ROWS, D]) for k in both]
    n3, n4 = Norm(st, "n3"), Norm(st, "n4")
    ps_x = st.ps("ps_x", [P, BANK])
    ps_d = [st.ps(f"ps_d{k}", [P, BANK]) for k in both]
    ps_z = [None] + [st.ps(f"ps_z{m}", [P, BANK]) for m in (1, 2, 3)]
    ps_y = st.ps("ps_y", [P, BANK])
    s = {n: st.sem(n) for n in ("w_in", "half", "th", "a", "x_read", "part", "x3T_ps", "x3T_sb", "az", "ez", "lz", "sp", "delta", "decay",
                                "tin", "tsel", "tgate", "upd", "state", "gated", "y_ps")}
    z_ps = [st.sem(f"z_ps{m}") for m in range(4)]
    x_landed, stored = ([st.sem(f"{n}{k}") for k in both] for n in ("x_landed", "stored"))
    pick_landed = [[st.sem(f"pick_landed{n}_{k}") for k in both] for n in both]

    def chunks(t):
        return t[:, 0:KC * ROWS].rearrange("p (c n) -> p c n", c=KC)

    def sequences(eng, body, ahead=3):
        pipeline(eng, SEQS, ahead, 1, 3, body, ring=4)

    with st.block() as block:
        @block.sync
        def _(sp):
            for t, n in ((ident, "ident"), (win, "rec_win"), (wout, "rec_wout"), (la, "rec_la")):
                sp.dma_start(t.ap(), dram[n]).then_inc(s["w_in"], 16)

            def body(at):
                i = at.i
                if at.on(5):
                    need(sp, s["part"], i + 4)
                    sp.dma_start(x[at.slot(5, 2)][:, :], x_in[i + 5]).then_inc(x_landed[at.slot(5, 2)], 16)
                if at.on(-1):
                    need(sp, n4.normed, i)
                    sp.dma_start(x_out[i - 1], xo[at.slot(-1, 2)][:, :]).then_inc(stored[at.slot(-1, 2)], 16)
            sequences(sp, body, ahead=5)
            for k in both:
                sp.wait_ge(stored[k], landed(SEQS // 2 - 1))

        @block.gpsimd
        def _(pool):
            pool.memset(minus_half[:, :], -0.5).then_inc(s["half"], 1)
            pool.wait_ge(s["half"], 1)

            def fetch(b):
                if b >= 2:
                    pool.wait_ge(n3.y_sb, b - 1)
                for n in both:
                    pool.indirect_dma_start(pick[n][b % 2][:, :], None, ys, bass.IndirectOffsetOnAxis(ap=routes.slot[:, n, b:b + 1], axis=0)).then_inc(pick_landed[n][b % 2], 16)
            fetch(0)
            fetch(1)
            for i in range(-3, SEQS + 1):
                if i + 3 < SEQS:
                    n3.pool_rstd(pool, i + 4, minus_half[0:ROWS, :])
                if i >= 1:
                    n4.pool_rstd(pool, i, minus_half[0:ROWS, :])
                if i + 5 < SEQS:
                    fetch(i + 5)

        @block.tensor
        def _(pe):
            pe.wait_ge(s["w_in"], 64)

            def body(at):
                i = at.i
                if at.on(-1):
                    need(pe, s["gated"], i)
                    need(pe, n4.y_sb, i - 1)
                    for c in range(KC):
                        done = pe.matmul(ps_y[0:ROWS, 0:D], gated[at.slot(-1, 2)][:, c, :], wout[:, c, :], start=c == 0, stop=c == KC - 1)
                    done.then_inc(s["y_ps"], 1)
                if at.on(2):
                    need(pe, n3.normed, i + 3)
                    need(pe, s["x3T_sb"], i + 2)
                    for c in range(KC):
                        done = pe.transpose(ps_x[:, c * ROWS:(c + 1) * ROWS], x3[at.slot(2)][:, c * P:(c + 1) * P], ident[0:ROWS, 0:ROWS])
                    done.then_inc(s["x3T_ps"], 1)
                if at.on(1):
                    need(pe, s["x3T_sb"], i + 2)
                    for m, read, count in ((0, s["sp"], i), (1, s["tin"], i + 1), (2, s["tsel"], i + 1), (3, s["tgate"], i + 1)):
                        need(pe, read, count)
                        bank = ps_d[at.slot(1, 2)] if m == 0 else ps_z[m]
                        for q in range(KC):
                            for c in range(KC):
                                done = pe.matmul(bank[:, q * ROWS:(q + 1) * ROWS], win[:, m, c, q * P:(q + 1) * P], x3T[at.slot(1, 2)][:, c, :], start=c == 0, stop=c == KC - 1)
                        done.then_inc(z_ps[m], 1)
            sequences(pe, body)

        @block.scalar
        def _(act):
            act.wait_ge(s["w_in"], 64)
            act.activation(th[:, :], la[:, :], ACT.Tanh, scale=0.5).then_inc(s["th"], 1)

            def body(at):
                i = at.i
                if at.on(0):
                    need(act, s["delta"], i + 1)
                    need(act, s["state"], i)
                    for c in range(KC):
                        done = act.activation(decay[:, c, :], delta[:, c, :], ACT.Exp, scale=minus_a[:, c:c + 1])
                    done.then_inc(s["decay"], 1)
                if at.on(2):
                    need(act, s["x3T_ps"], i + 3)
                    need(act, z_ps[3], i + 1)
                    act.activation(x3T[at.slot(2, 2)][:, :, :], chunks(ps_x), ACT.Copy).then_inc(s["x3T_sb"], 1)
                if at.on(1):
                    need(act, z_ps[0], i + 2)
                    need(act, s["ez"], i + 1)
                    act.activation(az[:, :, :], chunks(ps_d[at.slot(1, 2)]), ACT.Abs).then_inc(s["az"], 1)
                    need(act, s["az"], i + 2)
                    need(act, s["lz"], i + 1)
                    act.activation(ez[:, :, :], az[:, :, :], ACT.Exp, scale=-1.0).then_inc(s["ez"], 1)
                    need(act, z_ps[1], i + 2)
                    need(act, s["upd"], i + 1)
                    act.activation(tin[:, :, :], chunks(ps_z[1]), ACT.Tanh).then_inc(s["tin"], 1)
                    need(act, s["ez"], i + 2)
                    need(act, s["sp"], i + 1)
                    act.activation(lz[:, :, :], ez[:, :, :], ACT.Ln, bias=1.0).then_inc(s["lz"], 1)
                    need(act, z_ps[2], i + 2)
                    act.activation(tsel[:, :, :], chunks(ps_z[2]), ACT.Tanh, scale=0.5).then_inc(s["tsel"], 1)
                    need(act, z_ps[3], i + 2)
                    need(act, s["gated"], i)
                    act.activation(tgate[at.slot(1, 2)][:, :, :], chunks(ps_z[3]), ACT.Tanh, scale=0.5).then_inc(s["tgate"], 1)
            sequences(act, body)

        @block.vector
        def _(dve):
            dve.wait_ge(s["th"], 1)
            dve.tensor_scalar(minus_a[:, :], th[:, :], -0.5, -0.5, ALU.mult, ALU.add).then_inc(s["a"], 1)
            dve.wait_ge(s["a"], 1)

            def body(at):
                i = at.i
                if at.on(3):
                    need(dve, x_landed[at.slot(3, 2)], at.landed(3, 2))
                    need(dve, pick_landed[0][at.slot(3, 2)], at.landed(3, 2))
                    need(dve, n3.y_sb, i + 3)
                    dve.memset(n3.tick[:, :], 0.0)
                    dve.scalar_tensor_tensor(part[:, :], pick[0][at.slot(3, 2)][:, :], routes.weight[:, 0, bass.ds(i + 3, 1)], x[at.slot(3, 2)][:, :], ALU.mult, ALU.add).then_inc(s["part"], 1)
                if at.on(0):
                    need(dve, s["decay"], i + 1)
                    need(dve, s["upd"], i + 1)
                    need(dve, s["gated"], i)
                    for c in range(KC):
                        done = dve.tensor_tensor_scan(state[:, c, :], decay[:, c, :], upd[:, c, :], 0.0, ALU.mult, ALU.add)
                    done.then_inc(s["state"], 1)
                if at.on(3):
                    need(dve, s["part"], i + 4)
                    need(dve, pick_landed[1][at.slot(3, 2)], at.landed(3, 2))
                    need(dve, n3.normed, i + 3)
                    dve.memset(n3.tick[:, :], 0.0)
                    dve.scalar_tensor_tensor(n3.y[:, :], pick[1][at.slot(3, 2)][:, :], routes.weight[:, 1, bass.ds(i + 3, 1)], part[:, :], ALU.mult, ALU.add).then_inc(n3.y_sb, 1)
                if at.on(0):
                    need(dve, s["state"], i + 1)
                    need(dve, s["tgate"], i + 1)
                    need(dve, s["y_ps"], i - 1)
                    dve.scalar_tensor_tensor(gated[at.slot(0, 2)][:, :, :], tgate[at.slot(0, 2)][:, :, :], 1.0, state[:, :, :], ALU.add, ALU.mult).then_inc(s["gated"], 1)
                if at.on(3):
                    n3.vector_sums(dve, i + 4)
                if at.on(-1):
                    need(dve, s["y_ps"], i)
                    need(dve, n4.normed, i - 1)
                    dve.scalar_tensor_tensor(n4.y[:, :], ps_y[0:ROWS, 0:D], 0.25, x3[at.slot(-1)][:, :], ALU.mult, ALU.add).then_inc(n4.y_sb, 1)
                if at.on(3):
                    n3.vector_mean(dve, i + 4)
                if at.on(-1):
                    n4.vector_sums(dve, i)
                if at.on(3):
                    n3.vector_variance(dve, i + 4)
                if at.on(-1):
                    n4.vector_mean(dve, i)
                if at.on(1):
                    need(dve, s["lz"], i + 2)
                    need(dve, z_ps[0], i + 2)
                    need(dve, s["delta"], i + 1)
                    dve.scalar_tensor_tensor(sp_[:, :, :], chunks(ps_d[at.slot(1, 2)]), 0.0, lz[:, :, :], ALU.max, ALU.add).then_inc(s["sp"], 1)
                if at.on(-1):
                    n4.vector_variance(dve, i)
                if at.on(3):
                    need(dve, n4.y_sb, i)
                    n3.vector_scale(dve, i + 4, x3[at.slot(3)][:, :])
                if at.on(1):
                    need(dve, s["sp"], i + 2)
                    need(dve, s["decay"], i + 1)
                    dve.tensor_scalar(delta[:, :, :], sp_[:, :, :], 1e-4, None, ALU.max).then_inc(s["delta"], 1)
                if at.on(1):
                    need(dve, s["tsel"], i + 2)
                    need(dve, s["state"], i + 1)
                    dve.scalar_tensor_tensor(upd[:, :, :], tsel[:, :, :], 1.0, tin[:, :, :], ALU.add, ALU.mult).then_inc(s["upd"], 1)
                if at.on(-1):
                    if at.on(-3):
                        need(dve, stored[at.slot(-1, 2)], at.landed(-3, 2))
                    n4.vector_scale(dve, i, xo[at.slot(-1, 2)][:, :])
            sequences(dve, body)
    st.end()


def gelu_experts(nc, dram, routes, xs, ys):
    st = Stage(nc, "ff1")
    T = routes.tiles
    both, ring = (0, 1), range(4)
    w1 = st.sb("w1", [P, E1, KC, F1])
    w2 = st.sb("w2", [P, E1, KC, D])
    b1 = st.sb("b1", [1, E1, F1])
    b2 = st.sb("b2", [1, E1, D])
    gb = st.sb("gb", [P, 2, E1, F1])
    ones = st.sb("ones", [1, P])
    ident = st.sb("ident", [P, P])
    minus_half = st.sb("minus_half", [P, 1])
    x = [st.sb(f"x{k}", [P, D]) for k in ring]
    xT = [st.sb(f"xT{k}", [P, KC, P]) for k in both]
    stat = st.sb("stat", [P, 6])
    mv = [st.sb(f"mv{k}", [P, 2]) for k in both]
    ve = [st.sb(f"ve{k}", [P, 1]) for k in both]
    rstd = [st.sb(f"rstd{k}", [P, 1]) for k in both]
    tick = st.sb("tick", [P, 1])
    hn = st.sb("hn", [P, F1])
    hg = st.sb("hg", [P, F1])
    hb = [st.sb(f"hb{k}", [P, F1]) for k in both]
    ha = [st.sb(f"ha{k}", [P, F1]) for k in both]
    hT = [st.sb(f"hT{k}", [P, KC, P]) for k in both]
    y = [st.sb(f"y{k}", [P, D]) for k in ring]
    ps_x = st.ps("ps_x", [P, BANK])
    ps_h = [st.ps(f"ps_h{k}", [P, BANK]) for k in both]
    ps_t = st.ps("ps_t", [P, BANK])
    ps_y = [st.ps(f"ps_y{k}", [P, BANK]) for k in both]
    s = {n: st.sem(n) for n in ("w_in", "half", "xT_ps", "xT_sb", "h_ps", "stat", "mv", "ve", "rstd", "hn", "hg", "hb", "ha", "hT_ps", "hT_sb", "y_ps", "y_sb")}
    x_landed, stored = ([st.sem(f"{n}{k}") for k in ring] for n in ("x_landed", "stored"))

    def tiles(eng, body, ahead=2):
        pipeline(eng, T, ahead, 2, 6, body, ring=4)

    with st.block() as block:
        @block.sync
        def _(sp):
            for t, n in ((ident, "ident"), (w1, "ff1_w1"), (b1, "ff1_b1"), (gb, "ff1_gb"), (w2, "ff1_w2"), (b2, "ff1_b2")):
                sp.dma_start(t.ap(), dram[n]).then_inc(s["w_in"], 16)

            def body(at):
                i = at.i
                if at.on(4):
                    need(sp, s["xT_ps"], i + 1)
                    sp.dma_start(x[at.slot(4)][:, :], xs[i + 4]).then_inc(x_landed[at.slot(4)], 16)
                if at.on(-2):
                    need(sp, s["y_sb"], i - 1)
                    sp.dma_start(ys[i - 2], y[at.slot(-2)][:, :]).then_inc(stored[at.slot(-2)], 16)
            tiles(sp, body, 4)
            for k in ring:
                sp.wait_ge(stored[k], 16 * (T // 4))

        @block.gpsimd
        def _(pool):
            pool.memset(minus_half[:, :], -0.5).then_inc(s["half"], 1)
            pool.memset(ones[:, :], 1.0).then_inc(s["half"], 1)
            pool.wait_ge(s["half"], 2)

            def body(at):
                i = at.i
                if at.on(1):
                    need(pool, s["ve"], i + 2)
                    need(pool, s["hn"], i)
                    pool.tensor_tensor(rstd[at.slot(1, 2)][:, :], ve[at.slot(1, 2)][:, :], minus_half[:, :], ALU.pow).then_inc(s["rstd"], 1)
            tiles(pool, body)

        @block.tensor
        def _(pe):
            pe.wait_ge(s["w_in"], 96)
            pe.wait_ge(s["half"], 2)

            def body(at):
                i = at.i
                if at.on(1):
                    expert = pe.value_load(routes.expert[0:1, bass.ds(i + 1, 1)], min_val=0, max_val=E1 - 1)
                if at.on(-2):
                    past = pe.value_load(routes.expert[0:1, bass.ds(i - 2, 1)], min_val=0, max_val=E1 - 1)
                if at.on(2):
                    need(pe, x_landed[at.slot(2)], at.landed(2))
                    need(pe, s["xT_sb"], i + 2)
                    for c in range(KC):
                        done = pe.transpose(ps_x[:, c * P:(c + 1) * P], x[at.slot(2)][:, c * P:(c + 1) * P], ident[:, :])
                    done.then_inc(s["xT_ps"], 1)
                if at.on(1):
                    need(pe, s["xT_sb"], i + 2)
                    need(pe, s["hn"], i)
                    for c in range(KC):
                        pe.matmul(ps_h[at.slot(1, 2)][:, 0:F1], xT[at.slot(1, 2)][:, c, :], w1[:, expert, c, :], start=c == 0, stop=False)
                    pe.matmul(ps_h[at.slot(1, 2)][:, 0:F1], ones[:, :], b1[:, expert, :], start=False, stop=True).then_inc(s["h_ps"], 1)
                if at.on(-1):
                    need(pe, s["ha"], i)
                    need(pe, s["hT_sb"], i - 1)
                    for c in range(KC):
                        done = pe.transpose(ps_t[:, c * P:(c + 1) * P], ha[at.slot(-1, 2)][:, c * P:(c + 1) * P], ident[:, :])
                    done.then_inc(s["hT_ps"], 1)
                if at.on(-2):
                    need(pe, s["hT_sb"], i - 1)
                    need(pe, s["y_sb"], i - 3)
                    for c in range(KC):
                        pe.matmul(ps_y[at.slot(-2, 2)][:, 0:D], hT[at.slot(-2, 2)][:, c, :], w2[:, past, c, :], start=c == 0, stop=False)
                    pe.matmul(ps_y[at.slot(-2, 2)][:, 0:D], ones[:, :], b2[:, past, :], start=False, stop=True).then_inc(s["y_ps"], 1)
            tiles(pe, body)

        @block.scalar
        def _(act):
            def body(at):
                i = at.i
                if at.on(2):
                    need(act, s["xT_ps"], i + 3)
                    need(act, s["h_ps"], i + 1)
                    act.activation(xT[at.slot(2, 2)][:, :, :], ps_x[:, 0:D].rearrange("p (c n) -> p c n", c=KC), ACT.Copy).then_inc(s["xT_sb"], 1)
                if at.on(-1):
                    need(act, s["hT_ps"], i)
                    need(act, s["y_ps"], i - 3)
                    act.activation(hT[at.slot(-1, 2)][:, :, :], ps_t[:, 0:F1].rearrange("p (c n) -> p c n", c=KC), ACT.Copy).then_inc(s["hT_sb"], 1)
                if at.on(0):
                    need(act, s["hb"], i + 1)
                    need(act, s["hT_ps"], i - 1)
                    act.activation(ha[at.slot(0, 2)][:, :], hb[at.slot(0, 2)][:, :], ACT.Gelu).then_inc(s["ha"], 1)
                if at.on(-2):
                    need(act, s["y_ps"], i - 1)
                    if at.on(-6):
                        need(act, stored[at.slot(-2)], at.landed(-6))
                    act.activation(y[at.slot(-2)][:, :], ps_y[at.slot(-2, 2)][:, 0:D], ACT.Copy).then_inc(s["y_sb"], 1)
            tiles(act, body)

        @block.vector
        def _(dve):
            dve.wait_ge(s["w_in"], 96)

            def body(at):
                i = at.i
                if at.on(0):
                    expert = dve.value_load(routes.expert[0:1, bass.ds(i, 1)], min_val=0, max_val=E1 - 1)
                if at.on(1):
                    need(dve, s["h_ps"], i + 2)
                    dve.bn_stats(stat[:, :], ps_h[at.slot(1, 2)][:, 0:F1]).then_inc(s["stat"], 1)
                if at.on(0):
                    need(dve, s["rstd"], i + 1)
                    need(dve, s["hg"], i)
                    dve.tensor_scalar(hn[:, :], ps_h[at.slot(0, 2)][:, 0:F1], mv[at.slot(0, 2)][:, 0:1], rstd[at.slot(0, 2)][:, 0:1], ALU.subtract, ALU.mult).then_inc(s["hn"], 1)
                if at.on(1):
                    need(dve, s["stat"], i + 2)
                    dve.memset(tick[:, :], 0.0)
                    dve.bn_aggr(mv[at.slot(1, 2)][:, :], stat[:, :]).then_inc(s["mv"], 1)
                if at.on(0):
                    need(dve, s["hn"], i + 1)
                    need(dve, s["hb"], i)
                    dve.tensor_tensor(hg[:, :], hn[:, :], gb[:, 0, expert, :], ALU.mult).then_inc(s["hg"], 1)
                if at.on(1):
                    need(dve, s["mv"], i + 2)
                    need(dve, s["rstd"], i)
                    dve.tensor_scalar(ve[at.slot(1, 2)][:, :], mv[at.slot(1, 2)][:, 1:2], LN_EPS, None, ALU.add).then_inc(s["ve"], 1)
                if at.on(0):
                    need(dve, s["hg"], i + 1)
                    need(dve, s["ha"], i - 1)
                    dve.tensor_tensor(hb[at.slot(0, 2)][:, :], hg[:, :], gb[:, 1, expert, :], ALU.add).then_inc(s["hb"], 1)
            tiles(dve, body)
    st.end()


def combine(nc, routes, x_in, ys, out):
    st = Stage(nc, "fin")
    both = (0, 1)
    x = [st.sb(f"x{k}", [ROWS, D]) for k in both]
    pick = [[st.sb(f"pick{n}_{k}", [ROWS, D]) for k in both] for n in both]
    part = st.sb("part", [ROWS, D])
    minus_half = st.sb("minus_half", [P, 1])
    tick = st.sb("tick", [ROWS, 1])
    xo = [st.sb(f"xo{k}", [ROWS, D]) for k in both]
    nm = Norm(st, "nm")
    half_set, part_done = st.sem("half"), st.sem("part")
    x_landed, stored = ([st.sem(f"{n}{k}") for k in both] for n in ("x_landed", "stored"))
    pick_landed = [[st.sem(f"pick_landed{n}_{k}") for k in both] for n in both]

    with st.block() as block:
        @block.sync
        def _(sp):
            def body(i, half, par, pre, main, post):
                if pre:
                    need(sp, part_done, i)
                    sp.dma_start(x[1 - par][:, :], x_in[i + 1]).then_inc(x_landed[1 - par], 16)
                if post:
                    need(sp, nm.normed, i)
                    sp.dma_start(out[i - 1], xo[1 - par][:, :]).then_inc(stored[1 - par], 16)
            steps(sp, body)
            for k in both:
                sp.wait_ge(stored[k], landed(SEQS // 2 - 1))

        @block.gpsimd
        def _(pool):
            pool.memset(minus_half[:, :], -0.5).then_inc(half_set, 1)
            pool.wait_ge(half_set, 1)

            def fetch(b):
                if b >= 2:
                    pool.wait_ge(nm.y_sb, b - 1)
                for n in both:
                    pool.indirect_dma_start(pick[n][b % 2][:, :], None, ys, bass.IndirectOffsetOnAxis(ap=routes.slot[:, n, b:b + 1], axis=0)).then_inc(pick_landed[n][b % 2], 16)
            fetch(0)
            for b in range(SEQS):
                if b + 1 < SEQS:
                    fetch(b + 1)
                nm.pool_rstd(pool, b + 1, minus_half[0:ROWS, :])

        @block.vector
        def _(dve):
            def body(i, half, par, pre, main, post):
                if main:
                    need(dve, x_landed[par], landed(half))
                    need(dve, pick_landed[0][par], landed(half))
                    dve.memset(tick[:, :], 0.0)
                    dve.scalar_tensor_tensor(part[:, :], pick[0][par][:, :], routes.weight[:, 0, bass.ds(i, 1)], x[par][:, :], ALU.mult, ALU.add).then_inc(part_done, 1)
                    need(dve, part_done, i + 1)
                    need(dve, pick_landed[1][par], landed(half))
                    dve.memset(tick[:, :], 0.0)
                    dve.scalar_tensor_tensor(nm.y[:, :], pick[1][par][:, :], routes.weight[:, 1, bass.ds(i, 1)], part[:, :], ALU.mult, ALU.add).then_inc(nm.y_sb, 1)
                    nm.vector_stats(dve, i + 1)
                    need(dve, stored[par], landed(half - 1))
                    nm.vector_scale(dve, i + 1, xo[par][:, :])
            steps(dve, body)
    st.end()


def clear(nc, xs):
    st = Stage(nc, "clear")
    zeros = st.sb("zeros", [P, D])
    zeroed, stored = st.sem("zeroed"), st.sem("stored")
    with st.block() as block:
        @block.gpsimd
        def _(pool):
            pool.memset(zeros[:, :], 0.0).then_inc(zeroed, 1)

        @block.sync
        def _(sp):
            sp.wait_ge(zeroed, 1)
            for t in range(FFN1_TILES):
                sp.dma_start(xs[t], zeros[:, :]).then_inc(stored, 16)
            sp.wait_ge(stored, 16 * FFN1_TILES)
    st.end()


def decoder(nc, dram, out):
    def scratch(name, shape):
        return nc.dram_tensor(name, shape, F32, kind="Internal").ap()

    x1, x2, x4, x5 = (scratch(f"x{n}", [SEQS, ROWS, D]) for n in (1, 2, 4, 5))
    xs, ys = (scratch(n, [FFN1_TILES, P, D]) for n in ("xs", "ys"))
    xs_rows, ys0_rows, ys_rows = (t.rearrange("t p d -> (t p) d") for t in (xs, ys[0:FFN0_TILES], ys))

    clear(nc, xs)
    self_attention(nc, dram, dram["x"], x1)
    cross_attention(nc, dram, "xa0", x1, x2)
    with ExitStack() as stack:
        routes = Routes(nc, stack, "r0", E0, FFN0_TILES)
        router(nc, dram, routes, x2, xs_rows, F32_EPS, 0.0, False)
        relu_experts(nc, dram, routes, xs, ys)
        recurrence(nc, dram, routes, x2, ys0_rows, x4)
    cross_attention(nc, dram, "xa1", x4, x5, dram["mask"])
    with ExitStack() as stack:
        routes = Routes(nc, stack, "r1", E1, FFN1_TILES)
        router(nc, dram, routes, x5, xs_rows, 0.0, 1e-9, True)
        gelu_experts(nc, dram, routes, xs, ys)
        combine(nc, routes, x5, ys_rows, out)


def layout(inputs):
    f32 = np.float32
    a = {k: np.asarray(v) for k, v in inputs.items()}

    def chunked(w):
        return w.reshape(-1, P, w.shape[-1]).transpose(1, 0, 2)

    def columns(b):
        return b.reshape(-1, P).T

    def every(b):
        return np.broadcast_to(b[None, :], (P, b.shape[0]))

    split = np.concatenate([np.arange(0, D, 2), np.arange(1, D, 2)])
    ipw, ipb = a["L0_attn_in_proj_w"], a["L0_attn_in_proj_b"]
    i = np.arange(D // 2, dtype=f32)
    theta = (f32(10000.0) ** (f32(-2.0) * (i - f32(1.0)) / f32(D))).astype(f32)
    angle = (theta[:, None] * np.arange(ROWS, dtype=f32)[None, :]).astype(f32)
    t = {
        "x": a["x"],
        "sa_w1": np.stack([chunked(a[f"L0_attn_w{c}"][split].T) for c in "qkv"], axis=1),
        "sa_w2": np.stack([chunked(ipw[n * D:(n + 1) * D][:, split].T) for n in range(3)], axis=1),
        "sa_wo": chunked(a["L0_attn_out_w"].T),
        "sa_bqk": np.stack([columns(ipb[0:D]), columns(ipb[D:2 * D])], axis=1),
        "sa_bv": every(ipb[2 * D:]),
        "sa_bo": every(a["L0_attn_out_b"]),
        "ident": np.eye(P, dtype=f32),
        "causal": np.where(np.tril(np.ones((ROWS, ROWS), bool)), f32(0), f32(MASKED)),
        "rope": np.stack([np.cos(angle), np.sin(angle)], axis=1).astype(f32),
        "head_mask": (np.arange(P)[:, None] // HD == np.arange(HPC)[None, :]).astype(f32),
    }
    t["ctxT"] = a["ctx_1024"].reshape(SEQS, KEYS, KC, P).transpose(0, 3, 2, 1)
    t["mask"] = a["mask_Bx1xSxS2_ik1"].reshape(SEQS, ROWS, KEYS)
    for n, w, b, turn in (("xa0", "L0_xattn_w{}_w", "L0_xattn_w{}_b", True), ("xa1", "L1_xattn_w{}", "L1_xattn_b{}", False)):
        for c in "qkvo":
            wn, bn = (("L0_xattn_dense_w", "L0_xattn_dense_b") if turn and c == "o" else (w.format(c), b.format(c)))
            t[f"{n}_w{c}"] = chunked(a[wn].T if turn else a[wn])
            t[f"{n}_b{c}"] = a[bn]
        t[f"{n}_bqk"] = np.stack([columns(t.pop(f"{n}_bq")), columns(t.pop(f"{n}_bk"))], axis=1)
        for c in "vo":
            t[f"{n}_b{c}"] = every(t[f"{n}_b{c}"])
    t["before"] = np.triu(np.ones((ROWS, ROWS), f32), 1)
    t["iota"] = np.broadcast_to(np.arange(P, dtype=f32)[None, :], (P, P))
    for n, e in (("r0", E0), ("r1", E1)):
        t[f"{n}_chain"] = np.broadcast_to((np.arange(SEQS) > 0).astype(f32)[None, None, :], (P, e, SEQS))
    t["r0_wr"] = chunked(a["L0_ffn_Wr"].T)
    t["r0_br"] = np.zeros((P, E0), f32)
    t["r1_wr"] = chunked(a["L1_ffn_Wr"])
    t["r1_br"] = every(a["L1_ffn_br"])
    t["ff0_w"] = np.concatenate([a[f"L0_ffn_W{c}"].transpose(0, 2, 1).reshape(E0, KC, P, F0).transpose(0, 2, 1, 3).reshape(E0, P, KC * F0) for c in "gu"]
                                + [a["L0_ffn_Wd"].transpose(0, 2, 1).reshape(E0, F0 // P, P, D).transpose(0, 2, 1, 3).reshape(E0, P, F0 // P * D)], axis=2)
    t["rec_win"] = np.stack([chunked(a[f"L1_attn_W_{n}"].T) for n in ("delta", "in", "select", "gate")], axis=1)
    t["rec_wout"] = chunked(a["L1_attn_W_out"].T)
    t["rec_la"] = columns(a["L1_attn_log_a"])
    for n in (1, 2):
        t[f"ff1_w{n}"] = a[f"L1_ffn_W{n}"].reshape(E1, KC, P, -1).transpose(2, 0, 1, 3)
        t[f"ff1_b{n}"] = a[f"L1_ffn_b{n}"][None]
    t["ff1_gb"] = np.broadcast_to(np.stack([a["L1_ffn_g1"], a["L1_ffn_be1"]])[None], (P, 2, E1, F1))
    return {k: np.ascontiguousarray(v) for k, v in t.items()}


def kernel(**inputs):
    import concourse.bacc as bacc
    from concourse.bass_utils import run_bass_kernel_spmd

    nc = bacc.Bacc("TRN2", target_bir_lowering=False, num_devices=1)
    arrays = {f"in_{k}": v for k, v in layout(inputs).items()}
    dram = {k[3:]: nc.dram_tensor(k, v.shape, mybir.dt.from_np(v.dtype), kind="ExternalInput").ap() for k, v in arrays.items()}
    out = nc.dram_tensor("out", (SEQS, ROWS, D), F32, kind="ExternalOutput").ap()
    decoder(nc, dram, out)
    r = run_bass_kernel_spmd(nc, [arrays], core_ids=[0])
    return r.results[0]["out"]
```

```python
from contextlib import ExitStack

import numpy as np

import concourse.bass as bass
from concourse import mybir

F32 = mybir.dt.float32
BF16 = mybir.dt.bfloat16
F32R = mybir.dt.float32r
I32 = mybir.dt.int32
U32 = mybir.dt.uint32
ALU = mybir.AluOpType
ACT = mybir.ActivationFunctionType
AX = mybir.AxisListType

P = 128
SEQS = 16
ROWS = 100
D = 256
KC = D // P
HEADS = 16
HD = D // HEADS
HPC = P // HD
KEYS = 361
KTW = 121
KEYS_EVEN = KEYS + 1
QH = 4
QT = HEADS // QH
BANK = 512
VW = 32
MASKED = -1e30
LN_EPS = 1e-5
E0, F0 = 8, 1024
E1, F1 = 16, 256
PAIRS = SEQS * ROWS * 2
FFN0_TILES = (PAIRS + E0 * (P - 1)) // P
FFN1_TILES = (PAIRS + E1 * (P - 1)) // P
ZERO_ROWS = 64
F32_EPS = float(np.finfo(np.float32).eps)


def need(eng, sem, count):
    if isinstance(count, int) and count <= 0:
        return
    eng.wait_ge(sem, count)


def key_rows(k):
    return min(KTW, KEYS - k * KTW)


def landed(half):
    return 16 * (half + 1)


class At:

    def __init__(self, i, turn, place, n, ring):
        self.i, self.turn, self.place, self.n, self.ring = i, turn, place, n, ring

    def on(self, k):
        return not isinstance(self.i, int) or 0 <= self.i + k < self.n

    def slot(self, k, ring=None):
        return (self.place + k) % (ring or self.ring)

    def nth(self, k, ring=None):
        ring = ring or self.ring
        return self.ring // ring * self.turn + (self.place + k) // ring

    def landed(self, k, ring=None):
        return 16 * (self.nth(k, ring) + 1)


def pipeline(eng, n, ahead, behind, first, body, ring=2):
    turns = (n - ahead - first) // ring
    for i in range(-ahead, first):
        body(At(i, i // ring, i % ring, n, ring))
    with eng.Fori(0, turns) as t:
        for k in range(ring):
            i = first + k
            body(At(t * ring + i, t + i // ring, i % ring, n, ring))
    for i in range(first + turns * ring, n + behind):
        body(At(i, i // ring, i % ring, n, ring))


def steps(eng, body, n=SEQS):
    def one(at):
        body(at.i, at.turn, at.place, at.on(1), at.on(0), at.on(-1))
    pipeline(eng, n, 1, 1, 3, one)


def late_steps(eng, body, n=SEQS):
    def one(at):
        body(at.i, at.turn, at.place, at.on(1), at.on(0), at.on(-1), at.on(-2))
    pipeline(eng, n, 1, 2, 4, one)


class Stage:

    def __init__(self, nc, name):
        self.nc, self.name, self.stack, self.sems = nc, name, ExitStack(), []

    def sb(self, name, shape, dt=F32):
        return self.stack.enter_context(self.nc.sbuf_tensor(f"{self.name}_{name}", shape, dt))

    def ps(self, name, shape, dt=F32):
        return self.stack.enter_context(self.nc.psum_tensor(f"{self.name}_{name}", shape, dt))

    def sem(self, name):
        self.sems.append(self.nc.alloc_semaphore(f"{self.name}_{name}"))
        return self.sems[-1]

    def block(self):
        return self.nc.Block()

    def end(self):
        self.nc.clear_and_free_semaphores(self.sems)
        self.nc.all_engine_barrier()
        self.stack.close()


class Early:

    def __init__(self, nc, stack, name, tensors):
        self.nc, self.keys = nc, {n: key for n, (_, key) in tensors.items()}
        self.t = {n: stack.enter_context(nc.sbuf_tensor(f"{name}_{n}", shape, F32)) for n, (shape, _) in tensors.items()}
        self.landed = nc.alloc_semaphore(f"{name}_landed")

    def fetch(self, eng, dram):
        for n, t in self.t.items():
            eng.dma_start(t.ap(), dram[self.keys[n]]).then_inc(self.landed, 16)

    def wait(self, eng):
        eng.wait_ge(self.landed, 16 * len(self.t))

    def sems(self):
        return [self.landed]

    def end(self):
        self.nc.clear_and_free_semaphores(self.sems())
        self.nc.all_engine_barrier()


def self_attention(nc, dram, x_in, x_out, xs, following):
    st = Stage(nc, "sa")
    zeros = st.sb("zeros", [ZERO_ROWS, D])
    x = [st.sb(f"x{k}", [ROWS, D]) for k in (0, 1)]
    xb = [st.sb(f"xb{k}", [ROWS, D]) for k in (0, 1)]
    xT = st.sb("xT", [P, KC, ROWS])
    w1 = st.sb("w1", [P, 3, KC, D])
    w2 = st.sb("w2", [P, 3, KC, D])
    wo = st.sb("wo", [P, KC, D])
    bqk = st.sb("bqk", [P, 2, KC])
    bv = st.sb("bv", [P, D])
    bo = st.sb("bo", [P, D])
    ident = st.sb("ident", [P, P])
    identb = st.sb("identb", [P, P], BF16)
    causal = st.sb("causal", [ROWS, ROWS])
    causalb = st.sb("causalb", [ROWS, 4, ROWS], BF16)
    cs = st.sb("cs", [P, 2, ROWS])
    hm = st.sb("hm", [P, HPC])
    pc = st.sb("pc", [P, 3, 2, ROWS])
    psn = st.sb("psn", [P, 3, 2, ROWS])
    rot = st.sb("rot", [P, 3, KC, ROWS])
    qT = st.sb("qT", [P, KC, ROWS])
    kT = st.sb("kT", [P, KC, ROWS])
    qm = st.sb("qm", [P, KC, HPC, ROWS])
    va = [st.sb(f"va{k}", [ROWS, HEADS, VW]) for k in (0, 1)]
    mx = st.sb("mx", [ROWS, HEADS])
    sh = st.sb("sh", [ROWS, HEADS, ROWS])
    pr = st.sb("pr", [ROWS, HEADS, ROWS])
    pT = st.sb("pT", [ROWS, HEADS, ROWS])
    oT = st.sb("oT", [P, 4, ROWS])
    rden = st.sb("rden", [ROWS, HEADS])
    o = st.sb("o", [ROWS, D])
    oT2 = st.sb("oT2", [P, KC, ROWS])
    y = st.sb("y", [ROWS, D])
    stat = st.sb("stat", [ROWS, 6])
    mv = st.sb("mv", [ROWS, 2])
    ve = st.sb("ve", [ROWS, 1])
    rstd = st.sb("rstd", [ROWS, 1])
    tick = st.sb("tick", [ROWS, 1])
    minus_half = st.sb("minus_half", [P, 1])
    xo = [st.sb(f"xo{k}", [ROWS, D]) for k in (0, 1)]

    ps_s = st.ps("ps_s", [P, 4, BANK])
    ps_o = st.ps("ps_o", [P, 2, BANK])
    ps_p = st.ps("ps_p", [P, 2, BANK])
    prj = ps_p[:, :, :].rearrange("p a b -> p (a b)")[:, 0:3 * D].rearrange("p (w n) -> p w n", w=3)[:, :, 0:KC * ROWS]

    s = {n: st.sem(n) for n in (
        "first_in", "w_in", "const", "zeros", "xT_ps", "xT_sb", "prj1", "rope_mul", "rope", "qk_ps", "v_ps", "q_sb",
        "k_sb", "v_sb", "qm", "xb", "o_ps", "oT_sb", "otr_ps", "rden", "o_sb", "oT2_ps", "oT2_sb", "y_ps", "y_sb",
        "stat", "mv", "ve", "rstd", "xo")}
    scores, maxed, shifted, probs, pt_ps, pt_sb = ([st.sem(f"{n}{j}") for j in range(4)] for n in ("scores", "max", "shifted", "probs", "pt_ps", "pt_sb"))
    x_landed = [st.sem(f"x_landed{k}") for k in (0, 1)]
    stored = [st.sem(f"stored{k}") for k in (0, 1)]
    cleared = st.sem("cleared")
    xs_part = xs.rearrange("t p d -> (t p) d").rearrange("(s r k) d -> s r k d", s=SEQS, r=ZERO_ROWS)

    with st.block() as block:
        @block.sync
        def _(sp):
            def load(t, a):
                sp.dma_start(t, a).then_inc(s["w_in"], 16)
            for t, a in ((ident[:, :], "ident"), (w1[:, :, :, :], "sa_w1"), (cs[:, :, :], "rope")):
                sp.dma_start(t, dram[a]).then_inc(s["first_in"], 16)

            def body(at):
                i = at.i
                if isinstance(i, int) and i == -1:
                    load(w2[:, :, :, :], dram["sa_w2"])
                    load(hm[:, :], dram["head_mask"])
                    load(bqk[:, :, :], dram["sa_bqk"])
                    load(bv[:, :], dram["sa_bv"])
                    load(causal[:, :], dram["causal"])
                    load(bo[:, :], dram["sa_bo"])
                    load(wo[:, :, :], dram["sa_wo"])
                if at.on(2):
                    need(sp, s["xb"], i + 1)
                    need(sp, s["xT_ps"], i + 1)
                    sp.dma_start(x[at.slot(2)][:, :], x_in[i + 2]).then_inc(x_landed[at.slot(2)], 16)
                if at.on(-1):
                    need(sp, s["xo"], i)
                    sp.dma_start(x_out[i - 1], xo[at.slot(-1)][:, :]).then_inc(stored[at.slot(-1)], 16)
                if isinstance(i, int) and i == 0:
                    following.fetch(sp, dram)
                if at.on(0):
                    need(sp, s["zeros"], 1)
                    sp.dma_start(xs_part[i], zeros[:, :].unsqueeze(1).to_broadcast([ZERO_ROWS, FFN1_TILES * P // SEQS // ZERO_ROWS, D])).then_inc(cleared, 16)
            pipeline(sp, SEQS, 2, 1, 2, body)
            for par in (0, 1):
                sp.wait_ge(stored[par], landed(SEQS // 2 - 2))
            following.fetch_x(sp, x_out)
            for par in (0, 1):
                sp.wait_ge(stored[par], landed(SEQS // 2 - 1))
            sp.wait_ge(cleared, 16 * SEQS)

        @block.gpsimd
        def _(pool):
            pool.memset(zeros[:, :], 0.0).then_inc(s["zeros"], 1)
            pool.wait_ge(s["zeros"], 1)
            pool.memset(minus_half[:, :], -0.5).then_inc(s["zeros"], 1)
            for k in (0, 1):
                pool.memset(va[k][:, :, :], 0.0).then_inc(s["zeros"], 1)
            pool.wait_ge(s["zeros"], 4)
            for k in (0, 1):
                pool.memset(va[k][:, :, HD:HD + 1], 1.0).then_inc(s["zeros"], 1)
            pool.wait_ge(s["first_in"], 48)
            pool.wait_ge(s["w_in"], 112)
            pool.tensor_copy(identb[:, :], ident[:, :]).then_inc(s["const"], 1)
            pool.tensor_copy(causalb[:, :, :], causal[:, :].unsqueeze(1).to_broadcast([ROWS, 4, ROWS])).then_inc(s["const"], 1)
            pool.wait_ge(s["zeros"], 6)

            def body(i, half, par, pre, main, post):
                if main:
                    need(pool, x_landed[par], landed(half))
                    need(pool, s["y_sb"], i - 1)
                    pool.tensor_tensor(xb[par][:, :], x[par][:, :], bo[0:ROWS, :], ALU.add).then_inc(s["xb"], 1)
                if pre:
                    need(pool, s["rope_mul"], i + 2)
                    need(pool, s["v_ps"], i + 1)
                    pool.tensor_tensor(rot[:, :, 0, :], pc[:, :, 0, :], psn[:, :, 1, :], ALU.add)
                    pool.tensor_tensor(rot[:, :, 1, :], pc[:, :, 1, :], psn[:, :, 0, :], ALU.subtract).then_inc(s["rope"], 1)
                    need(pool, s["q_sb"], i + 2)
                    need(pool, scores[3], i + 1)
                    for c in range(KC):
                        done = pool.tensor_tensor(qm[:, c, :, :], qT[:, c, :].unsqueeze(1).to_broadcast([P, HPC, ROWS]),
                                                  hm[:, :].unsqueeze(2).to_broadcast([P, HPC, ROWS]), ALU.mult)
                        done.then_inc(s["qm"], 1)
                if post:
                    need(pool, s["ve"], i)
                    need(pool, s["xo"], i - 1)
                    pool.tensor_tensor(rstd[:, :], ve[:, :], minus_half[0:ROWS, :], ALU.pow).then_inc(s["rstd"], 1)
            steps(pool, body)

        @block.tensor
        def _(pe):
            pe.wait_ge(s["first_in"], 48)

            def bank_scores(j, i):
                if j % 2 == 0:
                    need(pe, s["qm"], 2 * i + 1 + j // 2)
                need(pe, s["k_sb"], i + 1)
                need(pe, pt_sb[j], i)
                pe.matmul(ps_s[0:ROWS, j, 0:4 * ROWS], identb[0:ROWS, 0:ROWS], causalb[:, :, :], start=True, stop=False)
                for g in range(4):
                    h = 4 * j + g
                    done = pe.matmul(ps_s[0:ROWS, j, g * ROWS:(g + 1) * ROWS], qm[:, h // HPC, h % HPC, :],
                                     kT[:, h // HPC, :], start=False, stop=g == 3)
                done.then_inc(scores[j], 1)

            def bank_transposes(j, i):
                need(pe, shifted[j], i + 1)
                need(pe, probs[j], i + 1)
                for g in range(4):
                    done = pe.transpose(ps_s[0:ROWS, j, g * ROWS:(g + 1) * ROWS], pr[:, 4 * j + g, :], ident[0:ROWS, 0:ROWS])
                done.then_inc(pt_ps[j], 1)

            def body(i, half, par, pre, main, post):
                if pre:
                    need(pe, x_landed[1 - par], landed(half + par))
                    need(pe, s["q_sb"], i + 1)
                    need(pe, s["k_sb"], i + 1)
                    for c in range(KC):
                        done = pe.transpose(ps_p[:, 0, c * ROWS:(c + 1) * ROWS], x[1 - par][:, c * P:(c + 1) * P], ident[0:ROWS, 0:ROWS])
                    done.then_inc(s["xT_ps"], 1)
                if post:
                    need(pe, s["v_sb"], i)
                    need(pe, s["oT2_sb"], i - 1)
                    for j in range(4):
                        need(pe, pt_sb[j], i)
                        for g in range(4):
                            h = 4 * j + g
                            done = pe.matmul(ps_o[g * VW:(g + 1) * VW, 0, j * ROWS:(j + 1) * ROWS], va[1 - par][:, h, :], pT[:, h, :],
                                             start=True, stop=True, tile_position=(0, g * VW))
                    done.then_inc(s["o_ps"], 1)
                if main:
                    bank_scores(0, i)
                    bank_scores(1, i)
                if post:
                    need(pe, s["oT_sb"], i)
                    need(pe, s["y_sb"], i - 1)
                    for j in range(4):
                        done = pe.transpose(ps_o[0:ROWS, 1, j * P:(j + 1) * P], oT[:, j, :], ident[:, :])
                    done.then_inc(s["otr_ps"], 1)
                if pre:
                    need(pe, s["xT_sb"], i + 2)
                    need(pe, s["v_sb"], i + 1)
                    for w in range(3):
                        for m in range(KC):
                            for c in range(KC):
                                done = pe.matmul(prj[:, w, m * ROWS:(m + 1) * ROWS], w1[:, w, c, m * P:(m + 1) * P], xT[:, c, :],
                                                 start=c == 0, stop=c == KC - 1)
                    done.then_inc(s["prj1"], 1)
                if main:
                    bank_scores(2, i)
                if post:
                    need(pe, s["o_sb"], i)
                    for c in range(KC):
                        done = pe.transpose(ps_o[:, 0, c * ROWS:(c + 1) * ROWS], o[:, c * P:(c + 1) * P], ident[0:ROWS, 0:ROWS])
                    done.then_inc(s["oT2_ps"], 1)
                if main:
                    bank_scores(3, i)
                    bank_transposes(0, i)
                if post:
                    need(pe, s["oT2_sb"], i)
                    for c in range(KC):
                        done = pe.matmul(ps_o[0:ROWS, 1, 0:D], oT2[:, c, :], wo[:, c, :], start=c == 0, stop=c == KC - 1)
                    done.then_inc(s["y_ps"], 1)
                if main:
                    bank_transposes(1, i)
                if pre:
                    if isinstance(i, int) and i == -1:
                        pe.wait_ge(s["w_in"], 112)
                        pe.wait_ge(s["const"], 2)
                    need(pe, s["rope"], i + 2)
                    for w in range(2):
                        for m in range(KC):
                            for c in range(KC):
                                done = pe.matmul(ps_p[:, 0, (KC * w + m) * ROWS:(KC * w + m + 1) * ROWS], w2[:, w, c, m * P:(m + 1) * P],
                                                 rot[:, w, c, :], start=c == 0, stop=c == KC - 1)
                    done.then_inc(s["qk_ps"], 1)
                if main:
                    bank_transposes(2, i)
                if pre:
                    for c in range(KC):
                        done = pe.matmul(ps_p[0:ROWS, 1, 0:D], rot[:, 2, c, :], w2[:, 2, c, :], start=c == 0, stop=c == KC - 1)
                    done.then_inc(s["v_ps"], 1)
                if main:
                    bank_transposes(3, i)
            steps(pe, body)

        @block.scalar
        def _(act):

            def exponentials(j, i):
                need(act, shifted[j], i + 1)
                need(act, pt_ps[j], i)
                act.activation(pr[:, 4 * j:4 * j + 4, :], sh[:, 4 * j:4 * j + 4, :], ACT.Exp).then_inc(probs[j], 1)

            def copy_transposed(j, i):
                need(act, pt_ps[j], i + 1)
                if j == 0:
                    need(act, s["o_ps"], i)
                act.activation(pT[:, 4 * j:4 * j + 4, :], ps_s[0:ROWS, j, 0:4 * ROWS].rearrange("p (g n) -> p g n", g=4), ACT.Copy).then_inc(pt_sb[j], 1)

            def body(i, half, par, pre, main, post):
                if pre:
                    need(act, s["xT_ps"], i + 2)
                    need(act, s["prj1"], i + 1)
                    act.activation(xT[:, :, :], ps_p[:, 0, 0:KC * ROWS].rearrange("p (c n) -> p c n", c=KC), ACT.Copy).then_inc(s["xT_sb"], 1)
                if post:
                    need(act, s["o_ps"], i)
                    need(act, s["otr_ps"], i - 1)
                    act.activation(oT[:, :, :], ps_o[:, 0, 0:4 * ROWS].rearrange("p (g n) -> p g n", g=4), ACT.Copy).then_inc(s["oT_sb"], 1)
                if main:
                    exponentials(0, i)
                    exponentials(1, i)
                if post:
                    need(act, s["oT2_ps"], i)
                    need(act, s["y_ps"], i - 1)
                    act.activation(oT2[:, :, :], ps_o[:, 0, 0:KC * ROWS].rearrange("p (g n) -> p g n", g=KC), ACT.Copy).then_inc(s["oT2_sb"], 1)
                if main:
                    exponentials(2, i)
                    copy_transposed(0, i)
                    exponentials(3, i)
                    copy_transposed(1, i)
                if pre:
                    if isinstance(i, int) and i == -1:
                        act.wait_ge(s["w_in"], 112)
                    need(act, s["q_sb"], i + 2)
                    need(act, scores[3], i + 1)
                    for c in range(KC):
                        done = act.activation(kT[:, c, :], ps_p[:, 0, (KC + c) * ROWS:(KC + c + 1) * ROWS], ACT.Identity, bias=bqk[:, 1, c:c + 1])
                    done.then_inc(s["k_sb"], 1)
                if main:
                    copy_transposed(2, i)
                    copy_transposed(3, i)
            steps(act, body)

        @block.vector
        def _(dve):
            dve.wait_ge(s["first_in"], 48)
            dve.wait_ge(s["zeros"], 6)

            def shift(banks, i):
                for j in banks:
                    need(dve, scores[j], i + 1)
                    dve.tensor_reduce(mx[:, 4 * j:4 * j + 4], ps_s[0:ROWS, j, 0:4 * ROWS].rearrange("p (g n) -> p g n", g=4), AX.X, ALU.max).then_inc(maxed[j], 1)
                for j in banks:
                    need(dve, maxed[j], i + 1)
                    need(dve, probs[j], i)
                    dve.tensor_tensor(sh[:, 4 * j:4 * j + 4, :], ps_s[0:ROWS, j, 0:4 * ROWS].rearrange("p (g n) -> p g n", g=4),
                                      mx[:, 4 * j:4 * j + 4].unsqueeze(2).to_broadcast([ROWS, 4, ROWS]), ALU.subtract).then_inc(shifted[j], 1)

            def body(i, half, par, pre, main, post):
                if main:
                    shift((0, 1), i)
                if post:
                    need(dve, s["otr_ps"], i)
                    heads = ps_o[0:ROWS, 1, :].rearrange("p (h w) -> p h w", w=VW)
                    dve.reciprocal(rden[:, :], heads[:, :, HD]).then_inc(s["rden"], 1)
                    need(dve, s["rden"], i)
                    need(dve, s["oT2_ps"], i - 1)
                    dve.tensor_tensor(o[:, :].rearrange("p (h d) -> p h d", h=HEADS), heads[:, :, 0:HD],
                                      rden[:, :].unsqueeze(2).to_broadcast([ROWS, HEADS, HD]), ALU.mult).then_inc(s["o_sb"], 1)
                if pre:
                    need(dve, s["prj1"], i + 2)
                    need(dve, s["rope"], i + 1)
                    for t, n in ((pc, 0), (psn, 1)):
                        for w in range(3):
                            done = dve.tensor_tensor(t[:, w, :, :], prj[:, w, :].rearrange("p (c n) -> p c n", c=KC),
                                                     cs[:, n, :].unsqueeze(1).to_broadcast([P, KC, ROWS]), ALU.mult)
                    done.then_inc(s["rope_mul"], 1)
                if main:
                    shift((2, 3), i)
                if post:
                    need(dve, s["y_ps"], i)
                    need(dve, s["xb"], i)
                    dve.tensor_tensor(y[:, :], ps_o[0:ROWS, 1, 0:D], xb[1 - par][:, :], ALU.add).then_inc(s["y_sb"], 1)
                if pre:
                    if isinstance(i, int) and i == -1:
                        dve.wait_ge(s["w_in"], 112)
                    need(dve, s["qk_ps"], i + 2)
                    need(dve, s["qm"], 2 * i + 2)
                    for c in range(KC):
                        done = dve.tensor_scalar(qT[:, c, :], ps_p[:, 0, c * ROWS:(c + 1) * ROWS], bqk[:, 0, c:c + 1], HD ** -0.5, ALU.add, ALU.mult)
                    done.then_inc(s["q_sb"], 1)
                if post:
                    need(dve, s["y_sb"], i)
                    dve.bn_stats(stat[:, :], y[:, :]).then_inc(s["stat"], 1)
                    need(dve, s["stat"], i)
                    dve.memset(tick[:, :], 0.0)
                    dve.bn_aggr(mv[:, :], stat[:, :]).then_inc(s["mv"], 1)
                    need(dve, s["mv"], i)
                    dve.tensor_scalar(ve[:, :], mv[:, 1:2], LN_EPS, None, ALU.add).then_inc(s["ve"], 1)
                if pre:
                    need(dve, s["v_ps"], i + 2)
                    need(dve, s["o_ps"], i)
                    dve.tensor_tensor(va[1 - par][:, :, 0:HD], ps_p[0:ROWS, 1, 0:D].rearrange("p (h d) -> p h d", h=HEADS),
                                      bv[0:ROWS, :].rearrange("p (h d) -> p h d", h=HEADS), ALU.add).then_inc(s["v_sb"], 1)
                if post:
                    need(dve, s["rstd"], i)
                    need(dve, stored[1 - par], landed(half + par - 2))
                    dve.tensor_scalar(xo[1 - par][:, :], y[:, :], mv[:, 0:1], rstd[:, 0:1], ALU.subtract, ALU.mult).then_inc(s["xo"], 1)
            steps(dve, body)
    st.end()


class CrossAttentionEarly(Early):

    def __init__(self, nc, stack, name):
        super().__init__(nc, stack, f"{name}_w", {
            "ident": ([P, P], "ident"), "hm": ([P, QH], "tile_head_mask"),
            "wq": ([P, KC, QT, P], f"{name}_wq"), "bq": ([P, QT], f"{name}_bq"),
            "wk": ([P, KC, D], f"{name}_wk"), "bk": ([P, KC], f"{name}_bk"),
            "wv": ([P, KC, D], f"{name}_wv"), "bv": ([P, D], f"{name}_bv"),
            "wo": ([P, KC, D], f"{name}_wo"), "bo": ([P, D], f"{name}_bo")})
        both = (0, 1)
        self.x = [stack.enter_context(nc.sbuf_tensor(f"{name}_x{k}", [ROWS, D], F32)) for k in both]
        self.ctx = [stack.enter_context(nc.sbuf_tensor(f"{name}_ctx{k}", [P, KC, KEYS_EVEN], F32)) for k in both]
        self.x_landed, self.c_landed = ([nc.alloc_semaphore(f"{name}_{n}{k}") for k in both] for n in ("x_landed", "c_landed"))

    def fetch(self, eng, dram):
        super().fetch(eng, dram)
        for k, t in enumerate(self.ctx):
            eng.dma_start(t[:, :, 0:KEYS], dram["ctxT"][k]).then_inc(self.c_landed[k], 16)

    def fetch_x(self, eng, x_in):
        for k, t in enumerate(self.x):
            eng.dma_start(t[:, :], x_in[k]).then_inc(self.x_landed[k], 16)

    def sems(self):
        return super().sems() + self.x_landed + self.c_landed


def cross_attention(nc, dram, name, early, x_in, x_out, mask=None):
    st = Stage(nc, name)
    NPAIR = HEADS // 2
    V_TILES = {6: (0, 1), 7: (2,)}
    ready = 7 if mask is not None else 4
    both = (0, 1)
    x, ctx = early.x, early.ctx
    ident, hm, wq, bq, wk, bk, wv, bv, wo, bo = early.t.values()
    cr = [[st.sb(f"cr_{n}{k}", [P, KC, KEYS_EVEN], F32R) for k in both] for n in ("hi", "lo")]
    wkr, wvr = ([st.sb(f"{w}_{n}", [P, KC, D], F32R) for n in ("hi", "lo")] for w in ("wkr", "wvr"))
    zero = st.sb("zero", [P, 1])
    PARTS = ((0, 0), (0, 1), (1, 0))
    xb = [st.sb(f"xb{k}", [ROWS, D]) for k in both]
    xT = st.sb("xT", [P, KC, ROWS])
    q = st.sb("q", [P, QT, ROWS])
    qhi = st.sb("qhi", [P, QT, ROWS], F32R)
    qlo = st.sb("qlo", [P, QT, ROWS])
    qm = [[st.sb(f"qm_{n}{k}", [P, QT, QH, ROWS], F32R) for k in both] for n in ("hi", "lo")]
    kr = [st.sb(f"kr{k}", [P, QT, KEYS_EVEN], F32R) for k in both]
    va = [st.sb(f"va{k}", [KTW, 3, HEADS, VW]) for k in both]
    nmx = [st.sb(f"nmx{k}", [ROWS, HEADS]) for k in both]
    pr = [st.sb(f"pr{k}", [ROWS, 2, 3 * KTW]) for k in range(4)]
    pT = [st.sb(f"pT{k}", [KTW, HEADS, 3, ROWS]) for k in both]
    oT = st.sb("oT", [P, 4, ROWS])
    rden = st.sb("rden", [ROWS, HEADS])
    o = st.sb("o", [ROWS, D])
    oT2 = st.sb("oT2", [P, KC, ROWS])
    y = st.sb("y", [ROWS, D])
    stat = st.sb("stat", [ROWS, 6])
    mv = st.sb("mv", [ROWS, 2])
    ve = st.sb("ve", [ROWS, 1])
    rstd = st.sb("rstd", [ROWS, 1])
    tick = st.sb("tick", [ROWS, 1])
    minus_half = st.sb("minus_half", [P, 1])
    xo = [st.sb(f"xo{k}", [ROWS, D]) for k in both]
    if mask is not None:
        maskid = st.sb("maskid", [P, P], BF16)
        mk = [st.sb(f"mk{k}", [ROWS, KEYS], I32) for k in both]
        mb = [st.sb(f"mb{k}", [ROWS, KEYS_EVEN], BF16) for k in both]

    ps_s = st.ps("ps_s", [P, 4, BANK])
    ps_t = st.ps("ps_t", [P, 2, BANK])
    ps_p = st.ps("ps_p", [P, BANK])
    ps_o = st.ps("ps_o", [P, BANK])
    first_bank = {"x": ps_s[:, 0, :], "q": ps_s[:, 1, :], "k0": ps_s[:, 2, :], "k1": ps_s[:, 3, :], "v01": ps_t[:, 0, :], "v2": ps_t[:, 1, :]}

    def room(part, i):
        return first_bank[part] if isinstance(i, int) and i == -1 else ps_p[:, :]

    def turn(pe, sem, i):
        if not (isinstance(i, int) and i == -1):
            need(pe, sem, i + 2)

    s = {n: st.sem(n) for n in (
        "w_hi", "w_lo", "cr_hi", "cr_lo", "zeros", "pr_zeros", "va_zeros", "xT_ps", "xT_sb", "q_ps", "q_sb", "qhi", "qlo", "qm", "xb", "mb",
        "o_ps", "oT_sb", "otr_ps", "rden", "o_sb", "oT2_ps", "oT2_sb", "y_ps", "y_sb", "stat", "mv", "ve", "rstd", "xo")}
    k_ps, k_hi, k_sb = ([st.sem(f"{n}{m}") for m in range(KC)] for n in ("k_ps", "k_hi", "k_sb"))
    v_ps, v_sb = ([st.sem(f"{n}{m}") for m in range(3)] for n in ("v_ps", "v_sb"))
    scores, nmax, probs = ([st.sem(f"{n}{p}") for p in range(NPAIR)] for n in ("scores", "nmax", "probs"))
    pt, pt_sb = ([[st.sem(f"{n}{p}_{g}") for g in both] for p in range(NPAIR)] for n in ("pt", "pt_sb"))
    x_landed, c_landed = early.x_landed, early.c_landed
    m_landed, stored = ([st.sem(f"{n}{k}") for k in both] for n in ("m_landed", "stored"))

    def value_tile(eng, k, i, par):
        kn = key_rows(k)
        eng.tensor_tensor(va[par][0:kn, k, :, 0:HD], room("v2" if k == 2 else "v01", i)[0:kn, k % 2 * D:(k % 2 + 1) * D].rearrange("p (h d) -> p h d", h=HEADS),
                          bv[0:kn, :].rearrange("p (h d) -> p h d", h=HEADS), ALU.add).then_inc(v_sb[k], 1)

    with st.block() as block:
        @block.sync
        def _(sp):
            def body(at):
                i, k = at.i, at.slot(2)
                if at.on(2) and not (isinstance(i, int) and i < 0):
                    need(sp, s["xT_ps"], i + 1)
                    need(sp, s["xb"], i + 1)
                    sp.dma_start(x[k][:, :], x_in[i + 2]).then_inc(x_landed[k], 16)
                    need(sp, s["cr_lo"], i + 1)
                    sp.dma_start(ctx[k][:, :, 0:KEYS], dram["ctxT"][i + 2]).then_inc(c_landed[k], 16)
                if at.on(2) and mask is not None:
                    need(sp, s["mb"], i + 1)
                    sp.dma_start(mk[k][:, :], mask[i + 2]).then_inc(m_landed[k], 16)
                if at.on(-2):
                    need(sp, s["xo"], i - 1)
                    sp.dma_start(x_out[i - 2], xo[k][:, :]).then_inc(stored[k], 16)
            pipeline(sp, SEQS, 2, 2, 2, body)
            for k in both:
                sp.wait_ge(stored[k], landed(SEQS // 2 - 1))

        @block.gpsimd
        def _(pool):
            pool.memset(minus_half[:, :], -0.5).then_inc(s["zeros"], 1)
            pool.memset(zero[:, :], 0.0).then_inc(s["zeros"], 1)
            for k in both:
                pool.memset(ctx[k][:, :, KEYS:], 0.0).then_inc(s["zeros"], 1)
                if mask is not None:
                    pool.memset(mb[k][:, KEYS:], 0.0).then_inc(s["zeros"], 1)
            early.wait(pool)
            if mask is not None:
                pool.tensor_scalar(maskid[:, :], ident[:, :], MASKED, None, ALU.mult).then_inc(s["zeros"], 1)
            pool.wait_ge(s["zeros"], ready)

            def body(at):
                i, half, par = at.i, at.turn, at.place
                if at.on(-2):
                    need(pool, s["ve"], i - 1)
                    need(pool, s["xo"], i - 2)
                    pool.tensor_tensor(rstd[:, :], ve[:, :], minus_half[0:ROWS, :], ALU.pow).then_inc(s["rstd"], 1)
                if at.on(0):
                    need(pool, x_landed[par], landed(half))
                    need(pool, s["y_sb"], i - 1)
                    pool.tensor_tensor(xb[par][:, :], x[par][:, :], bo[0:ROWS, :], ALU.add).then_inc(s["xb"], 1)
                if at.on(1):
                    nxt = 1 - par
                    need(pool, s["qhi"], i + 2)
                    pool.tensor_tensor(qlo[:, :, :], q[:, :, :], qhi[:, :, :], ALU.subtract).then_inc(s["qlo"], 1)
                    need(pool, s["qlo"], i + 2)
                    need(pool, scores[NPAIR - 1], i)
                    for t in range(QT):
                        for n, part in enumerate((qhi, qlo)):
                            done = pool.tensor_tensor(qm[n][nxt][:, t, :, :], part[:, t, :].unsqueeze(1).to_broadcast([P, QH, ROWS]),
                                                      hm[:, :].unsqueeze(2).to_broadcast([P, QH, ROWS]), ALU.mult)
                        done.then_inc(s["qm"], 1)
                if at.on(2):
                    need(pool, c_landed[at.slot(2)], at.landed(2))
                    need(pool, v_ps[2], i + 1)
                    hi, lo = (cr[n][at.slot(2)][:, :, :] for n in both)
                    pool.tensor_tensor(hi, ctx[at.slot(2)][:, :, :], zero[:, :].unsqueeze(2).to_broadcast([P, KC, KEYS_EVEN]), ALU.add).then_inc(s["cr_hi"], 1)
                    need(pool, s["cr_hi"], i + 3)
                    pool.tensor_tensor(lo, ctx[at.slot(2)][:, :, :], hi, ALU.subtract).then_inc(s["cr_lo"], 1)
                if isinstance(i, int) and i == -2:
                    for t in pr:
                        pool.memset(t[:, :, :], 0.0).then_inc(s["pr_zeros"], 1)
            pipeline(pool, SEQS, 2, 2, 4, body)

        @block.tensor
        def _(pe):
            early.wait(pe)

            def pair_scores(p, i, par):
                if p % 2 == 0:
                    need(pe, s["qm"], QT * i + p // 2 + 1)
                if p == 0:
                    for c in range(KC):
                        need(pe, k_sb[c], i + 1)
                    if mask is not None:
                        need(pe, s["mb"], i + 1)
                need(pe, probs[(p - 2) % NPAIR], i + 1 if p >= 2 else i)
                for g in both:
                    h = 2 * p + g
                    bank = ps_s[0:ROWS, 2 * (p % 2) + g, 0:KEYS_EVEN]
                    if mask is not None:
                        pe.matmul(bank, maskid[0:ROWS, 0:ROWS], mb[par][:, :], start=True, stop=False)
                    pe.matmul(bank, qm[0][par][:, h // QH, h % QH, :], kr[par][:, h // QH, :], start=mask is None, stop=False)
                    done = pe.matmul(bank, qm[1][par][:, h // QH, h % QH, :], kr[par][:, h // QH, :], start=False, stop=True)
                done.then_inc(scores[p], 1)

            def pair_transposes(p, i):
                need(pe, probs[p], i + 1)
                for g in both:
                    need(pe, pt_sb[(p - 1) % NPAIR][g], i + 1 if p >= 1 else i)
                    for k in range(3):
                        done = pe.transpose(ps_t[0:KTW, g, k * ROWS:(k + 1) * ROWS], pr[p % 4][:, g, k * KTW:(k + 1) * KTW], ident[0:ROWS, 0:ROWS])
                    done.then_inc(pt[p][g], 1)

            def pre_step(p, i, half, par):
                nxt, nhalf = 1 - par, half + par
                if p == 0:
                    need(pe, x_landed[nxt], landed(nhalf))
                    need(pe, v_sb[2], i + 1)
                    for c in range(KC):
                        done = pe.transpose(room("x", i)[:, c * ROWS:(c + 1) * ROWS], x[nxt][:, c * P:(c + 1) * P], ident[0:ROWS, 0:ROWS])
                    done.then_inc(s["xT_ps"], 1)
                if p == 1:
                    need(pe, s["xT_sb"], i + 2)
                    for t in range(QT):
                        for c in range(KC):
                            done = pe.matmul(room("q", i)[:, t * ROWS:(t + 1) * ROWS], wq[:, c, t, :], xT[:, c, :], start=c == 0, stop=c == KC - 1)
                    done.then_inc(s["q_ps"], 1)
                if p in (2, 4):
                    m = (p - 2) // 2
                    if m == 0:
                        need(pe, s["cr_lo"], i + 2)
                        if isinstance(i, int) and i == -1:
                            pe.wait_ge(s["w_lo"], 1)
                        turn(pe, s["q_sb"], i)
                    else:
                        turn(pe, k_sb[0], i)
                    for c in range(KC):
                        for nw, nx in PARTS:
                            done = pe.matmul(room(f"k{m}", i)[:, 0:KEYS_EVEN], wkr[nw][:, c, m * P:(m + 1) * P], cr[nx][nxt][:, c, :],
                                             start=c == 0 and nw == nx, stop=c == KC - 1 and nw == 1)
                    done.then_inc(k_ps[m], 1)
                for k in V_TILES.get(p, ()):
                    k0, kn = k * KTW, key_rows(k)
                    turn(pe, v_sb[1] if k == 2 else k_sb[1], i)
                    if isinstance(i, int) and i == -1 and k == 0:
                        pe.wait_ge(s["w_lo"], 2)
                    for c in range(KC):
                        for nw, nx in PARTS:
                            done = pe.matmul(room("v2" if k == 2 else "v01", i)[0:kn, k % 2 * D:(k % 2 + 1) * D], cr[nx][nxt][:, c, k0:k0 + kn], wvr[nw][:, c, :],
                                             start=c == 0 and nw == nx, stop=c == KC - 1 and nw == 1)
                    done.then_inc(v_ps[k], 1)

            def post_step(p, i, par):
                prv = 1 - par
                if p == 3:
                    for g in both:
                        need(pe, pt_sb[NPAIR - 1][g], i)
                    need(pe, s["y_sb"], i - 1)
                    for j in range(4):
                        for k in range(3):
                            for g in range(4):
                                h = 4 * j + g
                                done = pe.matmul(ps_o[g * VW:(g + 1) * VW, j * ROWS:(j + 1) * ROWS], va[prv][:, k, h, :], pT[prv][:, h, k, :],
                                                 start=k == 0, stop=k == 2, tile_position=(0, g * VW))
                    done.then_inc(s["o_ps"], 1)
                if p == 5:
                    need(pe, s["oT_sb"], i)
                    for j in range(4):
                        done = pe.transpose(ps_o[0:ROWS, j * P:(j + 1) * P], oT[:, j, :], ident[:, :])
                    done.then_inc(s["otr_ps"], 1)
                if p == 6:
                    need(pe, s["o_sb"], i)
                    for c in range(KC):
                        done = pe.transpose(ps_o[:, c * ROWS:(c + 1) * ROWS], o[:, c * P:(c + 1) * P], ident[0:ROWS, 0:ROWS])
                    done.then_inc(s["oT2_ps"], 1)
                if p == 7:
                    need(pe, s["oT2_sb"], i)
                    for c in range(KC):
                        done = pe.matmul(ps_o[0:ROWS, 0:D], oT2[:, c, :], wo[:, c, :], start=c == 0, stop=c == KC - 1)
                    done.then_inc(s["y_ps"], 1)

            def body(i, half, par, pre, main, post):
                for p in range(NPAIR):
                    if main:
                        pair_scores(p, i, par)
                    if pre:
                        pre_step(p, i, half, par)
                    if p < 2 and post:
                        pair_transposes(NPAIR - 2 + p, i - 1)
                    if post:
                        post_step(p, i, par)
                    if p >= 2 and main:
                        pair_transposes(p - 2, i)
            steps(pe, body)

        @block.scalar
        def _(act):
            early.wait(act)

            def copy_odd(p, i, par):
                need(act, pt[p][1], i + 1)
                if p == 0:
                    need(act, s["o_ps"], i - 1)
                act.activation(pT[par][:, 2 * p + 1, :, :], ps_t[0:KTW, 1, 0:3 * ROWS].rearrange("p (k n) -> p k n", k=3), ACT.Copy).then_inc(pt_sb[p][1], 1)

            def body(i, half, par, pre, main, post):
                for p in range(NPAIR):
                    if pre and p == 0:
                        need(act, s["xT_ps"], i + 2)
                        need(act, s["q_ps"], i + 1)
                        act.activation(xT[:, :, :], room("x", i)[:, 0:KC * ROWS].rearrange("p (c n) -> p c n", c=KC), ACT.Copy).then_inc(s["xT_sb"], 1)
                    if p == 4 and post:
                        need(act, s["o_ps"], i)
                        need(act, s["otr_ps"], i - 1)
                        act.activation(oT[:, :, :], ps_o[:, 0:4 * ROWS].rearrange("p (g n) -> p g n", g=4), ACT.Copy).then_inc(s["oT_sb"], 1)
                    if pre and p in (2, 4):
                        m = (p - 2) // 2
                        need(act, k_ps[m], i + 2)
                        need(act, scores[NPAIR - 1], i)
                        for t, rows in ((2 * m, slice(0, 64)), (2 * m + 1, slice(64, P))):
                            act.activation(kr[1 - par][rows, t, :], room(f"k{m}", i)[rows, 0:KEYS_EVEN], ACT.Identity, bias=bk[rows, m:m + 1]).then_inc(k_hi[m], 1)
                    if main:
                        if isinstance(i, int) and i == 0 and p == 0:
                            act.wait_ge(s["pr_zeros"], 4)
                        need(act, nmax[p], i + 1)
                        need(act, pt[(p - 4) % NPAIR][1], i + 1 if p >= 4 else i)
                        for g in both:
                            h = 2 * p + g
                            done = act.activation(pr[p % 4][:, g, 0:KEYS], ps_s[0:ROWS, 2 * (p % 2) + g, 0:KEYS], ACT.Exp, bias=nmx[par][:, h:h + 1])
                        done.then_inc(probs[p], 1)
                    if pre and p == 1:
                        need(act, s["q_sb"], i + 2)
                        need(act, s["qm"], QT * (i + 1))
                        act.activation(qhi[:, :, :], q[:, :, :], ACT.Copy).then_inc(s["qhi"], 1)
                    if p == 6 and post:
                        need(act, s["oT2_ps"], i)
                        need(act, s["y_ps"], i - 1)
                        act.activation(oT2[:, :, :], ps_o[:, 0:KC * ROWS].rearrange("p (g n) -> p g n", g=KC), ACT.Copy).then_inc(s["oT2_sb"], 1)
                    if p < 2 and post:
                        copy_odd(NPAIR - 2 + p, i - 1, 1 - par)
                    if p >= 2 and main:
                        copy_odd(p - 2, i, par)
            steps(act, body)

        @block.vector
        def _(dve):
            early.wait(dve)
            for n, (w, parts) in enumerate(((wk, wkr), (wv, wvr))):
                dve.tensor_copy(parts[0][:, :, :], w[:, :, :]).then_inc(s["w_hi"], 1)
                dve.wait_ge(s["w_hi"], n + 1)
                dve.tensor_tensor(parts[1][:, :, :], w[:, :, :], parts[0][:, :, :], ALU.subtract).then_inc(s["w_lo"], 1)
            for t in va:
                dve.memset(t[:, :, :, :], 0.0).then_inc(s["va_zeros"], 1)
            dve.wait_ge(s["va_zeros"], 2)
            for t in va:
                dve.memset(t[:, :, :, HD:HD + 1], 1.0).then_inc(s["va_zeros"], 1)
            dve.wait_ge(s["va_zeros"], 4)

            def copy_even(p, i, par):
                need(dve, pt[p][0], i + 1)
                if p == 0:
                    need(dve, s["o_ps"], i - 1)
                dve.tensor_copy(pT[par][:, 2 * p, :, :], ps_t[0:KTW, 0, 0:3 * ROWS].rearrange("p (k n) -> p k n", k=3)).then_inc(pt_sb[p][0], 1)

            def pre_step(p, i, half, par):
                if p == 7 and mask is not None:
                    need(dve, m_landed[1 - par], landed(half + par))
                    need(dve, scores[NPAIR - 1], i)
                    dve.tensor_scalar(mb[1 - par][:, 0:KEYS], mk[1 - par][:, :], 0.0, None, ALU.is_equal).then_inc(s["mb"], 1)
                if p == 1:
                    need(dve, s["q_ps"], i + 2)
                    need(dve, s["qm"], QT * (i + 1))
                    dve.tensor_tensor(q[:, :, :], room("q", i)[:, 0:QT * ROWS].rearrange("p (t n) -> p t n", t=QT),
                                      bq[:, :].unsqueeze(2).to_broadcast([P, QT, ROWS]), ALU.add).then_inc(s["q_sb"], 1)
                for k in V_TILES.get(p, ()):
                    need(dve, v_ps[V_TILES[p][-1]], i + 2)
                    need(dve, s["o_ps"], i)
                    value_tile(dve, k, i, 1 - par)

            def post_step(p, i, par):
                if p == 5:
                    need(dve, s["otr_ps"], i)
                    heads = ps_o[0:ROWS, :].rearrange("p (h w) -> p h w", w=VW)
                    dve.reciprocal(rden[:, :], heads[:, :, HD]).then_inc(s["rden"], 1)
                    need(dve, s["rden"], i)
                    dve.tensor_tensor(o[:, :].rearrange("p (h d) -> p h d", h=HEADS), heads[:, :, 0:HD],
                                      rden[:, :].unsqueeze(2).to_broadcast([ROWS, HEADS, HD]), ALU.mult).then_inc(s["o_sb"], 1)
                if p == 7:
                    need(dve, s["y_ps"], i)
                    need(dve, s["xb"], i)
                    dve.tensor_tensor(y[:, :], ps_o[0:ROWS, 0:D], xb[1 - par][:, :], ALU.add).then_inc(s["y_sb"], 1)

            def late_step(p, i, half, par):
                if p == 0:
                    need(dve, s["y_sb"], i - 1)
                    dve.bn_stats(stat[:, :], y[:, :]).then_inc(s["stat"], 1)
                    need(dve, s["stat"], i - 1)
                    dve.memset(tick[:, :], 0.0)
                    dve.bn_aggr(mv[:, :], stat[:, :]).then_inc(s["mv"], 1)
                    need(dve, s["mv"], i - 1)
                    dve.tensor_scalar(ve[:, :], mv[:, 1:2], LN_EPS, None, ALU.add).then_inc(s["ve"], 1)
                if p == 1:
                    need(dve, s["rstd"], i - 1)
                    need(dve, stored[par], landed(half - 2))
                    dve.tensor_scalar(xo[par][:, :], y[:, :], mv[:, 0:1], rstd[:, 0:1], ALU.subtract, ALU.mult).then_inc(s["xo"], 1)

            def body(i, half, par, pre, main, post, late):
                for p in range(NPAIR):
                    if pre and p in (3, 5):
                        m = (p - 3) // 2
                        for n, (t, rows, to) in enumerate(((2 * m, slice(0, 64), slice(64, P)), (2 * m + 1, slice(64, P), slice(0, 64)))):
                            need(dve, k_hi[m], 2 * (i + 1) + n + 1)
                            done = dve.scalar_tensor_tensor(kr[1 - par][to, t, :], room(f"k{m}", i)[rows, 0:KEYS_EVEN], bk[rows, m:m + 1], kr[1 - par][rows, t, :], ALU.add, ALU.subtract)
                        done.then_inc(k_sb[m], 1)

                    if main:
                        need(dve, scores[p], i + 1)
                        if p == 0:
                            need(dve, probs[NPAIR - 1], i - 1)
                        dve.tensor_reduce(nmx[par][:, 2 * p:2 * p + 2], ps_s[0:ROWS, 2 * (p % 2):2 * (p % 2) + 2, 0:KEYS], AX.X, ALU.max,
                                          negate=True).then_inc(nmax[p], 1)
                    if pre:
                        pre_step(p, i, half, par)
                    if post:
                        post_step(p, i, par)
                    if late:
                        late_step(p, i, half, par)
                    if p < 2 and post:
                        copy_even(NPAIR - 2 + p, i - 1, 1 - par)
                    if p >= 2 and main:
                        copy_even(p - 2, i, par)
            late_steps(dve, body)
    st.end()


class Routes:

    def __init__(self, nc, stack, name, experts, tiles):
        def sb(n, shape, dt):
            return stack.enter_context(nc.sbuf_tensor(f"{name}_{n}", shape, dt))
        self.name, self.experts, self.tiles = name, experts, tiles
        self.slot = sb("slot", [ROWS, 2, SEQS], I32)
        self.weight = sb("weight", [ROWS, 2, SEQS], F32)
        self.expert = sb("expert", [P, tiles], I32)
        self.end = sb("end", [P, experts], I32)


RING = 2


class Weights:

    def __init__(self, nc, stack, name, tensors, sems):
        self.nc = nc
        self.t = {n: stack.enter_context(nc.sbuf_tensor(f"{name}_{n}", shape, F32)) for n, shape in tensors.items()}
        self.landed = [nc.alloc_semaphore(f"{name}_landed{k}") for k in range(sems)]

    def end(self):
        self.nc.clear_and_free_semaphores(self.landed)
        self.nc.all_engine_barrier()


class ReluWeights(Weights):

    def __init__(self, nc, stack):
        self.width = width = 2 * KC * F0 + F0 // P * D
        super().__init__(nc, stack, "w0", {"raw": [P, RING, width]}, RING)
        self.split = stack.enter_context(nc.sbuf_tensor("w0_split", [P, RING, 2, width], F32R))
        self.zero = stack.enter_context(nc.sbuf_tensor("w0_zero", [P, 1], F32))
        self.zeroed = nc.alloc_semaphore("w0_zeroed")
        self.first_hi, self.first_split, self.hi_done = (nc.alloc_semaphore(f"w0_{n}") for n in ("first_hi", "first_split", "hi_done"))

    def fetch_first(self, eng, dram):
        for e in range(RING):
            eng.dma_start(self.t["raw"][:, e, :], dram["ff0_w"][e]).then_inc(self.landed[e], 16)

    def prepare_zeros(self, pool):
        pool.memset(self.zero[:, :], 0.0).then_inc(self.zeroed, 1)

    def parts(self, e):
        return self.t["raw"][:, e % RING, :], self.split[:, e % RING, 0, :], self.split[:, e % RING, 1, :]

    def prepare_hi(self, act):
        raw, hi, _ = self.parts(0)
        act.wait_ge(self.landed[0], 16)
        act.activation(hi, raw, ACT.Copy).then_inc(self.first_hi, 1)

    def prepare_lo(self, dve):
        raw, hi, lo = self.parts(0)
        dve.wait_ge(self.first_hi, 1)
        dve.tensor_tensor(lo, raw, hi, ALU.subtract).then_inc(self.first_split, 1)

    def split_expert(self, pool, e, ready):
        raw, hi, lo = self.parts(e)
        pool.tensor_tensor(hi, raw, self.zero[:, :].to_broadcast([P, self.width]), ALU.add).then_inc(self.hi_done, 1)
        pool.wait_ge(self.hi_done, e)
        pool.tensor_tensor(lo, raw, hi, ALU.subtract).then_inc(ready, 1)

    def end(self):
        self.landed += [self.zeroed, self.first_hi, self.first_split, self.hi_done]
        super().end()


class GeluWeights(Weights):
    BIAS_ROWS = 33

    def __init__(self, nc, stack):
        super().__init__(nc, stack, "w1", {"w1": [P, E1, KC, F1], "gb": [P, 2, E1, F1], "w2": [P, E1, KC, D]}, 1)
        self.raw = [stack.enter_context(nc.sbuf_tensor(f"w1_b{n}", [self.BIAS_ROWS, E1, F1], F32)) for n in (1, 2)]
        self.bias = [stack.enter_context(nc.sbuf_tensor(f"w1_b{n}r", [self.BIAS_ROWS, E1, F1], F32R)) for n in (1, 2)]
        self.zeroed, self.b_landed, self.b_hi, self.b_split = (nc.alloc_semaphore(f"w1_{n}") for n in ("zeroed", "b_landed", "b_hi", "b_split"))

    def prepare_zeros(self, pool):
        for raw in self.raw:
            pool.memset(raw[:, :, :], 0.0).then_inc(self.zeroed, 1)

    def fetch_first(self, eng, dram):
        for n, t in self.t.items():
            eng.dma_start(t.ap(), dram[f"ff1_{n}"]).then_inc(self.landed[0], 16)
        eng.wait_ge(self.zeroed, 2)
        for n, raw in enumerate(self.raw):
            for row in (0, 32):
                eng.dma_start(raw[row:row + 1, :, :], dram[f"ff1_b{n + 1}"]).then_inc(self.b_landed, 16)

    def prepare_hi(self, act):
        act.wait_ge(self.b_landed, 64)
        for raw, bias in zip(self.raw, self.bias):
            act.activation(bias[:, :, :], raw[:, :, :], ACT.Copy).then_inc(self.b_hi, 1)

    def prepare_lo(self, dve):
        dve.wait_ge(self.b_hi, 2)
        for raw, bias in zip(self.raw, self.bias):
            dve.tensor_tensor(bias[32:33, :, :], raw[32:33, :, :], bias[32:33, :, :], ALU.subtract).then_inc(self.b_split, 1)

    def end(self):
        self.landed += [self.zeroed, self.b_landed, self.b_hi, self.b_split]
        super().end()


def router(nc, dram, routes, weights, x_in, xs, norm_eps, norm_min, bias):
    E, T = routes.experts, routes.tiles
    st = Stage(nc, routes.name)
    xa = st.sb("xa", [ROWS, SEQS, D])
    wr = st.sb("wr", [P, KC, E])
    br = st.sb("br", [P, E])
    ident = st.sb("ident", [P, P])
    before = st.sb("before", [ROWS, ROWS])
    ones = st.sb("ones", [ROWS, ROWS])
    iota = st.sb("iota", [P, P])
    chain = st.sb("chain", [P, E, SEQS])
    xT = [st.sb(f"xT{k}", [P, KC, ROWS]) for k in range(4)]
    lg = st.sb("lg", [ROWS, SEQS, E])
    top = st.sb("top", [ROWS, SEQS, 8])
    idx = st.sb("idx", [ROWS, SEQS, 8], U32)
    idf = st.sb("idf", [ROWS, SEQS, 8])
    hot = [st.sb(f"hot{k}", [ROWS, SEQS, E]) for k in (0, 1)]
    hots = st.sb("hots", [ROWS, SEQS, E])
    less = st.sb("less", [ROWS, SEQS, E])
    ex = st.sb("ex", [ROWS, SEQS, E])
    less2 = st.sb("less2", [ROWS, SEQS])
    sc = st.sb("sc", [ROWS, 2, SEQS])
    ex2 = st.sb("ex2", [ROWS, SEQS])
    z = st.sb("z", [ROWS, SEQS])
    rz = st.sb("rz", [ROWS, SEQS])
    sm = st.sb("sm", [ROWS, SEQS])
    sm2 = st.sb("sm2", [ROWS, SEQS])
    rs = st.sb("rs", [ROWS, SEQS])
    tot = st.sb("tot", [ROWS, E, SEQS])
    upto = st.sb("upto", [ROWS, E, SEQS])
    prior = st.sb("prior", [ROWS, E, SEQS])
    nt = st.sb("nt", [ROWS, E], I32)
    nt2 = st.sb("nt2", [ROWS, E], I32)
    ntf = st.sb("ntf", [ROWS, E])
    endf = st.sb("endf", [ROWS, E])
    base = st.sb("base", [ROWS, E])
    base2 = st.sb("base2", [ROWS, E])
    pos = st.sb("pos", [ROWS, SEQS, E])
    pos2 = st.sb("pos2", [ROWS, SEQS, E])
    pk = [st.sb(f"pk{k}", [ROWS, SEQS, E]) for k in (0, 1)]
    slotf = st.sb("slotf", [ROWS, 2, SEQS])
    past = st.sb("past", [ROWS, T, E])
    ef = st.sb("ef", [ROWS, T])
    ef2 = st.sb("ef2", [ROWS, T])
    ps_x = [st.ps(f"ps_x{k}", [P, BANK]) for k in range(4)]
    ps_l = st.ps("ps_l", [P, BANK])
    ps_r = st.ps("ps_r", [P, BANK])
    ps_c = st.ps("ps_c", [P, BANK])
    s = {n: st.sem(n) for n in ("w_in", "more_in", "xT_ps", "xT_sb", "lg_ps", "hots", "rank_ps", "ones", "less", "ex", "slot", "dve", "sent")}
    x_in_done = [st.sem(f"x_in{k}") for k in range(4)]

    with st.block() as block:
        @block.sync
        def _(sp):
            for t, n in ((ident, "ident"), (wr, f"{routes.name}_wr")):
                sp.dma_start(t.ap(), dram[n]).then_inc(s["w_in"], 16)
            for k in range(4):
                group = slice(4 * k, 4 * k + 4)
                sp.dma_start(xa[:, group, :], x_in[group].rearrange("s r d -> r s d")).then_inc(x_in_done[k], 16)
            for t, n in ((br, f"{routes.name}_br"), (before, "before"), (iota, "iota"), (chain, f"{routes.name}_chain")):
                sp.dma_start(t.ap(), dram[n]).then_inc(s["more_in"], 16)
            weights.fetch_first(sp, dram)

        @block.gpsimd
        def _(pool):
            pool.memset(ones[:, :], 1.0).then_inc(s["ones"], 1)
            weights.prepare_zeros(pool)
            for k in range(4):
                pool.wait_ge(x_in_done[k], 16)
            pool.wait_ge(s["slot"], 1)
            for b in range(SEQS):
                for k in (0, 1):
                    pool.indirect_dma_start(xs, bass.IndirectOffsetOnAxis(ap=routes.slot[:, k, b:b + 1], axis=0), xa[:, b, :], None).then_inc(s["sent"], 16)
            pool.wait_ge(s["sent"], 16 * 2 * SEQS)

        @block.tensor
        def _(pe):
            pe.wait_ge(s["w_in"], 32)

            def logits(b):
                pe.wait_ge(s["xT_sb"], b + 1)
                for c in range(KC):
                    done = pe.matmul(ps_l[0:ROWS, b * E:(b + 1) * E], xT[b % 4][:, c, :], wr[:, c, :], start=c == 0, stop=c == KC - 1)
                done.then_inc(s["lg_ps"], 1)

            for b in range(SEQS):
                if b % 4 == 0:
                    pe.wait_ge(x_in_done[b // 4], 16)
                if b >= 4:
                    pe.wait_ge(s["xT_sb"], b - 3)
                for c in range(KC):
                    done = pe.transpose(ps_x[b % 4][:, c * ROWS:(c + 1) * ROWS], xa[:, b, c * P:(c + 1) * P], ident[0:ROWS, 0:ROWS])
                done.then_inc(s["xT_ps"], 1)
                if b >= 3:
                    logits(b - 3)
            for b in range(SEQS - 3, SEQS):
                logits(b)
            pe.wait_ge(s["more_in"], 64)
            pe.wait_ge(s["hots"], 1)
            pe.wait_ge(s["ones"], 1)
            flat = hots[:, :, :].rearrange("p s e -> p (s e)")
            pe.matmul(ps_r[0:ROWS, 0:SEQS * E], before[:, :], flat, start=True, stop=True)
            pe.matmul(ps_c[0:ROWS, 0:SEQS * E], ones[:, :], flat, start=True, stop=True).then_inc(s["rank_ps"], 1)

        @block.scalar
        def _(act):
            for b in range(SEQS):
                act.wait_ge(s["xT_ps"], b + 1)
                if b >= 4:
                    act.wait_ge(s["lg_ps"], b - 3)
                act.activation(xT[b % 4][:, :, :], ps_x[b % 4][:, 0:KC * ROWS].rearrange("p (c n) -> p c n", c=KC), ACT.Copy).then_inc(s["xT_sb"], 1)
            weights.prepare_hi(act)
            act.wait_ge(s["less"], 2)
            act.activation(ex[:, :, :], less[:, :, :], ACT.Exp).then_inc(s["ex"], 1)
            act.activation(ex2[:, :], less2[:, :], ACT.Exp).then_inc(s["ex"], 1)

        @block.vector
        def _(dve):
            count = [0]

            def then(ins):
                count[0] += 1
                ins.then_inc(s["dve"], 1)
                dve.wait_ge(s["dve"], count[0])

            def over(a, n):
                return a.unsqueeze(2).to_broadcast([ROWS, a.shape[1], n])

            def by_seq(a):
                return a.unsqueeze(1).to_broadcast([ROWS, SEQS, E])

            dve.wait_ge(s["more_in"], 64)
            dve.wait_ge(s["ones"], 1)
            dve.wait_ge(s["lg_ps"], SEQS)
            logits = ps_l[0:ROWS, 0:SEQS * E].rearrange("p (s e) -> p s e", s=SEQS)
            if bias:
                then(dve.tensor_tensor(lg[:, :, :], logits, by_seq(br[0:ROWS, :]), ALU.add))
            else:
                then(dve.tensor_copy(lg[:, :, :], logits))
            for b in range(SEQS):
                last = dve.max(top[:, b, :], lg[:, b, :])
            then(last)
            for b in range(SEQS):
                last = dve.max_index(idx[:, b, :], top[:, b, :], lg[:, b, :])
            then(last)
            then(dve.tensor_copy(idf[:, :, :], idx[:, :, :]))
            row = iota[0:ROWS, 0:E].unsqueeze(1).to_broadcast([ROWS, SEQS, E])
            for k in (0, 1):
                last = dve.tensor_tensor(hot[k][:, :, :], row, over(idf[:, :, k], E), ALU.is_equal)
            then(last)
            dve.tensor_tensor(hots[:, :, :], hot[0][:, :, :], hot[1][:, :, :], ALU.add).then_inc(s["hots"], 1)
            dve.wait_ge(s["rank_ps"], 1)
            then(dve.tensor_copy(tot[:, :, :], ps_c[0:ROWS, 0:SEQS * E].rearrange("p (s e) -> p e s", s=SEQS)))
            flat = "p e s -> p (e s)"
            then(dve.tensor_tensor_scan(upto[:, :, :].rearrange(flat), chain[0:ROWS, :, :].rearrange(flat), tot[:, :, :].rearrange(flat), 0.0, ALU.mult, ALU.add))
            dve.tensor_tensor(prior[:, :, :], upto[:, :, :], tot[:, :, :], ALU.subtract)
            then(dve.tensor_scalar(nt[:, :], upto[:, :, SEQS - 1], float(P - 1), None, ALU.add))
            then(dve.tensor_scalar(nt2[:, :], nt[:, :], P.bit_length() - 1, None, ALU.logical_shift_right))
            then(dve.tensor_copy(ntf[:, :], nt2[:, :]))
            then(dve.tensor_tensor_scan(endf[:, :], ones[:, 0:E], ntf[:, :], 0.0, ALU.mult, ALU.add))
            dve.tensor_copy(routes.end[0:ROWS, :], endf[:, :])
            then(dve.tensor_tensor(base[:, :], endf[:, :], ntf[:, :], ALU.subtract))
            then(dve.tensor_scalar(base2[:, :], base[:, :], float(P), None, ALU.mult))
            then(dve.tensor_tensor(pos[:, :, :], ps_r[0:ROWS, 0:SEQS * E].rearrange("p (s e) -> p s e", s=SEQS), prior[:, :, :].rearrange("p e s -> p s e"), ALU.add))
            then(dve.tensor_tensor(pos2[:, :, :], pos[:, :, :], by_seq(base2[:, :]), ALU.add))
            for k in (0, 1):
                last = dve.tensor_tensor(pk[k][:, :, :], hot[k][:, :, :], pos2[:, :, :], ALU.mult)
            then(last)
            for k in (0, 1):
                last = dve.tensor_reduce(slotf[:, k, :], pk[k][:, :, :], AX.X, ALU.add)
            then(last)
            dve.tensor_copy(routes.slot[:, :, :], slotf[:, :, :]).then_inc(s["slot"], 1)
            dve.tensor_tensor(less[:, :, :], lg[:, :, :], over(top[:, :, 0], E), ALU.subtract).then_inc(s["less"], 1)
            dve.tensor_tensor(less2[:, :], top[:, :, 1], top[:, :, 0], ALU.subtract).then_inc(s["less"], 1)
            dve.wait_ge(s["ex"], 2)
            then(dve.tensor_reduce(z[:, :], ex[:, :, :], AX.X, ALU.add))
            then(dve.reciprocal(rz[:, :], z[:, :]))
            dve.tensor_copy(sc[:, 0, :], rz[:, :])
            then(dve.tensor_tensor(sc[:, 1, :], ex2[:, :], rz[:, :], ALU.mult))
            then(dve.tensor_tensor(sm[:, :], sc[:, 0, :], sc[:, 1, :], ALU.add))
            then(dve.tensor_scalar(sm2[:, :], sm[:, :], norm_eps, norm_min, ALU.add, ALU.max))
            then(dve.reciprocal(rs[:, :], sm2[:, :]))
            for k in (0, 1):
                dve.tensor_tensor(routes.weight[:, k, :], sc[:, k, :], rs[:, :], ALU.mult)
            then(dve.tensor_tensor(past[:, :, :], endf[:, :].unsqueeze(1).to_broadcast([ROWS, T, E]), over(iota[0:ROWS, 0:T], E), ALU.is_le))
            then(dve.tensor_reduce(ef[:, :], past[:, :, :], AX.X, ALU.add))
            then(dve.tensor_scalar(ef2[:, :], ef[:, :], float(E - 1), None, ALU.min))
            then(dve.tensor_copy(routes.expert[0:ROWS, :], ef2[:, :]))
            weights.prepare_lo(dve)
    st.end()


def relu_experts(nc, dram, routes, weights, xs, ys, following):
    st = Stage(nc, "ff0")
    HALF = F0 // 2
    GU = 2 * KC * F0
    FC = F0 // P
    both = (0, 1)
    gu = weights.split[:, :, :, 0:GU].rearrange("p r n (m c f) -> p r n m c f", m=2, c=KC)
    down = weights.split[:, :, :, GU:].rearrange("p r n (k d) -> p r n k d", k=FC)
    ident = st.sb("ident", [P, P])
    x = [st.sb(f"x{k}", [P, D]) for k in both]
    xT = [[st.sb(f"xT_{n}{k}", [P, KC, P], F32R) for k in both] for n in ("hi", "lo")]
    rg = st.sb("rg", [P, 2, HALF])
    h = st.sb("h", [P, 2, HALF])
    hT = [st.sb(f"hT_{n}", [P, FC, P], F32R) for n in ("hi", "lo")]
    ylo = st.sb("ylo", [P, D])
    y = [st.sb(f"y{k}", [P, D]) for k in both]
    ps_g = [st.ps(f"ps_g{k}", [P, BANK]) for k in both]
    ps_u = [st.ps(f"ps_u{k}", [P, BANK]) for k in both]
    ps_h = [st.ps(f"ps_h{k}", [P, BANK]) for k in both]
    ps_x = st.ps("ps_x", [P, BANK])
    ps_y = st.ps("ps_y", [P, BANK])
    s = {n: st.sem(n) for n in ("w_in", "w_ready", "freed", "tiles_done", "xT_ps", "xT_hi", "xT_sb", "y_ps", "ylo", "y_sb")}
    g_ps, u_ps, rg_sb, h_sb, hT_ps, hT_hi, hT_sb = ([st.sem(f"{n}{k}") for k in both] for n in ("g_ps", "u_ps", "rg_sb", "h_sb", "hT_ps", "hT_hi", "hT_sb"))
    x_landed, stored = ([st.sem(f"{n}{k}") for k in both] for n in ("x_landed", "stored"))
    w_landed = [st.sem(f"w_landed{k}") for k in range(RING)]
    PARTS = ((0, 0), (0, 1), (1, 0))

    def half_of(k):
        return slice(k * FC // 2, (k + 1) * FC // 2)

    def in_bank(k):
        return ps_h[k][:, :].rearrange("p (q n) -> p q n", n=P)

    with st.block() as block:
        @block.sync
        def _(sp):
            sp.dma_start(ident[:, :], dram["ident"]).then_inc(s["w_in"], 16)

            def body(at):
                i = at.i
                if isinstance(i, int) and i == 0:
                    following.fetch(sp, dram)
                if at.on(2):
                    need(sp, s["xT_ps"], i + 1)
                    sp.dma_start(x[at.slot(2)][:, :], xs[i + 2]).then_inc(x_landed[at.slot(2)], 16)
                if at.on(-1):
                    need(sp, s["y_sb"], i)
                    sp.dma_start(ys[i - 1], y[at.slot(-1)][:, :]).then_inc(stored[at.slot(-1)], 16)
            pipeline(sp, routes.tiles, 2, 1, 2, body)
            for k in both:
                sp.wait_ge(stored[k], landed(routes.tiles // 2 - 1))

        @block.gpsimd
        def _(pool):
            pool.sem_inc(s["tiles_done"], 1)
            pool.wait_ge(weights.zeroed, 1)
            pool.wait_ge(weights.first_split, 1)
            pool.sem_inc(s["w_ready"], 1)
            for e in range(E0):
                if e >= 1:
                    if e < RING:
                        pool.wait_ge(weights.landed[e], 16)
                    else:
                        pool.wait_ge(w_landed[e % RING], 16 * (e // RING))
                        end = pool.value_load(routes.end[0:1, e - RING:e - RING + 1], min_val=0, max_val=routes.tiles)
                        pool.wait_ge(s["tiles_done"], end + 1)
                        pool.sem_inc(s["freed"], 1)
                    weights.split_expert(pool, e, s["w_ready"])
                if e + RING < E0:
                    pool.wait_ge(s["w_ready"], e + 1)
                    pool.dma_start(weights.t["raw"][:, e % RING, :], dram["ff0_w"][e + RING]).then_inc(w_landed[e % RING], 16)

        @block.tensor
        def _(pe):
            pe.wait_ge(s["w_in"], 16)

            def gate_and_up(k, i, par, at):
                for m, bank, read, sem in ((0, ps_g[k], rg_sb[k], g_ps[k]), (1, ps_u[k], h_sb[k], u_ps[k])):
                    need(pe, read, i)
                    for c in range(KC):
                        for nx, nw in PARTS:
                            done = pe.matmul(bank[:, :], xT[nx][par][:, c, :], gu[:, at, nw, m, c, k * HALF:(k + 1) * HALF],
                                             start=c == 0 and nx == nw, stop=c == KC - 1 and nx == 1)
                    done.then_inc(sem, 1)

            def h_transposes(k, i):
                need(pe, h_sb[k], i + 1)
                need(pe, hT_sb[k], i)
                for q in range(FC // 2):
                    done = pe.transpose(ps_h[k][:, q * P:(q + 1) * P], h[:, k, q * P:(q + 1) * P], ident[:, :])
                done.then_inc(hT_ps[k], 1)

            def body(i, half, par, pre, main, post):
                if main:
                    expert = pe.value_load(routes.expert[0:1, bass.ds(i, 1)], min_val=0, max_val=E0 - 1)
                    at = expert & (RING - 1)
                if post:
                    past = pe.value_load(routes.expert[0:1, bass.ds(i - 1, 1)], min_val=0, max_val=E0 - 1)
                    at_post = past & (RING - 1)
                if main:
                    pe.wait_ge(s["w_ready"], expert + 1)
                    need(pe, s["xT_sb"], i + 1)
                    gate_and_up(0, i, par, at)
                if post:
                    h_transposes(1, i - 1)
                    need(pe, s["y_sb"], i - 1)
                    for k in both:
                        need(pe, hT_sb[k], i)
                        for q in range(k * FC // 2, (k + 1) * FC // 2):
                            pe.matmul(ps_y[:, :].rearrange("p (n d) -> p n d", n=2), hT[0][:, q, :], down[:, at_post, :, q, :], start=q == 0, stop=False)
                            done = pe.matmul(ps_y[:, 0:D], hT[1][:, q, :], down[:, at_post, 0, q, :], start=False, stop=q == FC - 1)
                    done.then_inc(s["y_ps"], 1)
                if main:
                    h_transposes(0, i)
                if pre:
                    need(pe, x_landed[1 - par], landed(half + par))
                    need(pe, s["xT_sb"], i + 1)
                    for c in range(KC):
                        done = pe.transpose(ps_x[:, c * P:(c + 1) * P], x[1 - par][:, c * P:(c + 1) * P], ident[:, :])
                    done.then_inc(s["xT_ps"], 1)
                if main:
                    gate_and_up(1, i, par, at)
            steps(pe, body, routes.tiles)

        @block.scalar
        def _(act):
            def relu(k, i):
                need(act, g_ps[k], i + 1)
                need(act, h_sb[k], i)
                act.activation(rg[:, k, :], ps_g[k][:, :], ACT.Relu).then_inc(rg_sb[k], 1)

            def h_hi(k, i):
                need(act, hT_ps[k], i + 1)
                need(act, s["y_ps"], i)
                act.activation(hT[0][:, half_of(k), :], in_bank(k), ACT.Copy).then_inc(hT_hi[k], 1)

            def body(i, half, par, pre, main, post):
                if main:
                    relu(0, i)
                if post:
                    h_hi(1, i - 1)
                if main:
                    h_hi(0, i)
                if pre:
                    need(act, s["xT_ps"], i + 2)
                    need(act, u_ps[1], i)
                    act.activation(xT[0][1 - par][:, :, :], ps_x[:, 0:D].rearrange("p (c n) -> p c n", c=KC), ACT.Copy).then_inc(s["xT_hi"], 1)
                if main:
                    relu(1, i)
            steps(act, body, routes.tiles)

        @block.vector
        def _(dve):
            def gated(k, i):
                need(dve, rg_sb[k], i + 1)
                need(dve, u_ps[k], i + 1)
                need(dve, hT_ps[k], i)
                dve.tensor_tensor(h[:, k, :], ps_u[k][:, :], rg[:, k, :], ALU.mult).then_inc(h_sb[k], 1)

            def h_lo(k, i):
                need(dve, hT_hi[k], i + 1)
                dve.tensor_tensor(hT[1][:, half_of(k), :], in_bank(k), hT[0][:, half_of(k), :], ALU.subtract).then_inc(hT_sb[k], 1)

            def body(i, half, par, pre, main, post):
                if main:
                    gated(0, i)
                if post:
                    h_lo(1, i - 1)
                    need(dve, s["y_ps"], i)
                    need(dve, stored[1 - par], landed(half + par - 2))
                    dve.tensor_copy(ylo[:, :], ps_y[:, D:2 * D]).then_inc(s["ylo"], 1)
                    need(dve, s["ylo"], i)
                    dve.tensor_tensor(y[1 - par][:, :], ps_y[:, 0:D], ylo[:, :], ALU.add).then_inc(s["y_sb"], 1)
                    dve.sem_inc(s["tiles_done"], 1)
                if main:
                    h_lo(0, i)
                if pre:
                    need(dve, s["xT_hi"], i + 2)
                    dve.tensor_tensor(xT[1][1 - par][:, :, :], ps_x[:, 0:D].rearrange("p (c n) -> p c n", c=KC), xT[0][1 - par][:, :, :], ALU.subtract).then_inc(s["xT_sb"], 1)
                if main:
                    gated(1, i)
            steps(dve, body, routes.tiles)
    st.end()


class Norm:

    def __init__(self, st, name, rows=ROWS, width=D):
        self.y = st.sb(f"{name}_y", [rows, width])
        self.stat = st.sb(f"{name}_stat", [rows, 6])
        self.mv = st.sb(f"{name}_mv", [rows, 2])
        self.ve = st.sb(f"{name}_ve", [rows, 1])
        self.rstd = st.sb(f"{name}_rstd", [rows, 1])
        self.tick = st.sb(f"{name}_tick", [rows, 1])
        self.y_sb, self.stat_done, self.mv_done, self.ve_done, self.rstd_done, self.normed = (
            st.sem(f"{name}_{n}") for n in ("y_sb", "stat", "mv", "ve", "rstd", "normed"))

    def vector_stats(self, dve, n):
        self.vector_sums(dve, n)
        self.vector_mean(dve, n)
        self.vector_variance(dve, n)

    def vector_sums(self, dve, n):
        need(dve, self.y_sb, n)
        dve.bn_stats(self.stat[:, :], self.y[:, :]).then_inc(self.stat_done, 1)

    def vector_mean(self, dve, n):
        need(dve, self.stat_done, n)
        dve.memset(self.tick[:, :], 0.0)
        dve.bn_aggr(self.mv[:, :], self.stat[:, :]).then_inc(self.mv_done, 1)

    def vector_variance(self, dve, n):
        need(dve, self.mv_done, n)
        need(dve, self.rstd_done, n - 1)
        dve.tensor_scalar(self.ve[:, :], self.mv[:, 1:2], LN_EPS, None, ALU.add).then_inc(self.ve_done, 1)

    def pool_rstd(self, pool, n, minus_half):
        need(pool, self.ve_done, n)
        need(pool, self.normed, n - 1)
        pool.tensor_tensor(self.rstd[:, :], self.ve[:, :], minus_half, ALU.pow).then_inc(self.rstd_done, 1)

    def vector_scale(self, dve, n, out):
        need(dve, self.rstd_done, n)
        dve.tensor_scalar(out, self.y[:, :], self.mv[:, 0:1], self.rstd[:, 0:1], ALU.subtract, ALU.mult).then_inc(self.normed, 1)


def recurrence_early(nc, stack):
    return Early(nc, stack, "rec_w", {
        "ident": ([P, P], "ident"), "win": ([P, 4, KC, D], "rec_win"),
        "wout": ([P, KC, D], "rec_wout"), "la": ([P, KC], "rec_la")})


def recurrence(nc, dram, routes, early, x_in, ys, x_out, following):
    st = Stage(nc, "rec")
    both, ring = (0, 1), range(4)
    x = [st.sb(f"x{k}", [ROWS, D]) for k in both]
    pick = [[st.sb(f"pick{n}_{k}", [ROWS, D]) for k in both] for n in both]
    ident, win, wout, la = early.t.values()
    th = st.sb("th", [P, KC])
    minus_a = st.sb("minus_a", [P, KC])
    minus_half = st.sb("minus_half", [P, 1])
    part = st.sb("part", [ROWS, D])
    x3 = [st.sb(f"x3_{k}", [ROWS, D]) for k in ring]
    x3T = [st.sb(f"x3T{k}", [P, KC, ROWS]) for k in both]
    az, ez, lz, sp_, delta, decay, tin, tsel, upd, state = (
        st.sb(n, [P, KC, ROWS]) for n in ("az", "ez", "lz", "sp", "delta", "decay", "tin", "tsel", "upd", "state"))
    tgate, gated = ([st.sb(f"{n}{k}", [P, KC, ROWS]) for k in both] for n in ("tgate", "gated"))
    xo = [st.sb(f"xo{k}", [ROWS, D]) for k in both]
    n3, n4 = Norm(st, "n3"), Norm(st, "n4")
    ps_x = st.ps("ps_x", [P, BANK])
    ps_d = [st.ps(f"ps_d{k}", [P, BANK]) for k in both]
    ps_z = [None] + [st.ps(f"ps_z{m}", [P, BANK]) for m in (1, 2, 3)]
    ps_y = st.ps("ps_y", [P, BANK])
    s = {n: st.sem(n) for n in ("half", "th", "a", "part", "x3T_ps", "x3T_sb", "az", "ez", "lz", "sp", "delta", "decay",
                                "tin", "tsel", "tgate", "upd", "state", "gated", "y_ps")}
    z_ps = [st.sem(f"z_ps{m}") for m in range(4)]
    x_landed, stored = ([st.sem(f"{n}{k}") for k in both] for n in ("x_landed", "stored"))
    pick_landed = [[st.sem(f"pick_landed{n}_{k}") for k in both] for n in both]

    def chunks(t):
        return t[:, 0:KC * ROWS].rearrange("p (c n) -> p c n", c=KC)

    def sequences(eng, body, ahead=3):
        pipeline(eng, SEQS, ahead, 1, 3, body, ring=4)

    with st.block() as block:
        @block.sync
        def _(sp):
            def body(at):
                i = at.i
                if isinstance(i, int) and i == 0:
                    following.fetch(sp, dram)
                if at.on(5):
                    need(sp, s["part"], i + 4)
                    sp.dma_start(x[at.slot(5, 2)][:, :], x_in[i + 5]).then_inc(x_landed[at.slot(5, 2)], 16)
                if at.on(-1):
                    need(sp, n4.normed, i)
                    sp.dma_start(x_out[i - 1], xo[at.slot(-1, 2)][:, :]).then_inc(stored[at.slot(-1, 2)], 16)
            sequences(sp, body, ahead=5)
            for k in both:
                sp.wait_ge(stored[k], landed(SEQS // 2 - 2))
            following.fetch_x(sp, x_out)
            for k in both:
                sp.wait_ge(stored[k], landed(SEQS // 2 - 1))

        @block.gpsimd
        def _(pool):
            pool.memset(minus_half[:, :], -0.5).then_inc(s["half"], 1)
            pool.wait_ge(s["half"], 1)

            def fetch(b):
                if b >= 2:
                    pool.wait_ge(n3.y_sb, b - 1)
                for n in both:
                    pool.indirect_dma_start(pick[n][b % 2][:, :], None, ys, bass.IndirectOffsetOnAxis(ap=routes.slot[:, n, b:b + 1], axis=0)).then_inc(pick_landed[n][b % 2], 16)
            fetch(0)
            fetch(1)
            for i in range(-3, SEQS + 1):
                if i + 3 < SEQS:
                    n3.pool_rstd(pool, i + 4, minus_half[0:ROWS, :])
                if i >= 1:
                    n4.pool_rstd(pool, i, minus_half[0:ROWS, :])
                if i + 5 < SEQS:
                    fetch(i + 5)

        @block.tensor
        def _(pe):
            early.wait(pe)

            def body(at):
                i = at.i
                if at.on(-1):
                    need(pe, s["gated"], i)
                    need(pe, n4.y_sb, i - 1)
                    for c in range(KC):
                        done = pe.matmul(ps_y[0:ROWS, 0:D], gated[at.slot(-1, 2)][:, c, :], wout[:, c, :], start=c == 0, stop=c == KC - 1)
                    done.then_inc(s["y_ps"], 1)
                if at.on(2):
                    need(pe, n3.normed, i + 3)
                    need(pe, s["x3T_sb"], i + 2)
                    for c in range(KC):
                        done = pe.transpose(ps_x[:, c * ROWS:(c + 1) * ROWS], x3[at.slot(2)][:, c * P:(c + 1) * P], ident[0:ROWS, 0:ROWS])
                    done.then_inc(s["x3T_ps"], 1)
                if at.on(1):
                    need(pe, s["x3T_sb"], i + 2)
                    for m, read, count in ((0, s["sp"], i), (1, s["tin"], i + 1), (2, s["tsel"], i + 1), (3, s["tgate"], i + 1)):
                        need(pe, read, count)
                        bank = ps_d[at.slot(1, 2)] if m == 0 else ps_z[m]
                        for q in range(KC):
                            for c in range(KC):
                                done = pe.matmul(bank[:, q * ROWS:(q + 1) * ROWS], win[:, m, c, q * P:(q + 1) * P], x3T[at.slot(1, 2)][:, c, :], start=c == 0, stop=c == KC - 1)
                        done.then_inc(z_ps[m], 1)
            sequences(pe, body)

        @block.scalar
        def _(act):
            early.wait(act)
            act.activation(th[:, :], la[:, :], ACT.Tanh, scale=0.5).then_inc(s["th"], 1)

            def body(at):
                i = at.i
                if at.on(0):
                    need(act, s["delta"], i + 1)
                    need(act, s["state"], i)
                    for c in range(KC):
                        done = act.activation(decay[:, c, :], delta[:, c, :], ACT.Exp, scale=minus_a[:, c:c + 1])
                    done.then_inc(s["decay"], 1)
                if at.on(2):
                    need(act, s["x3T_ps"], i + 3)
                    need(act, z_ps[3], i + 1)
                    act.activation(x3T[at.slot(2, 2)][:, :, :], chunks(ps_x), ACT.Copy).then_inc(s["x3T_sb"], 1)
                if at.on(1):
                    need(act, z_ps[0], i + 2)
                    need(act, s["ez"], i + 1)
                    act.activation(az[:, :, :], chunks(ps_d[at.slot(1, 2)]), ACT.Abs).then_inc(s["az"], 1)
                    need(act, s["az"], i + 2)
                    need(act, s["lz"], i + 1)
                    act.activation(ez[:, :, :], az[:, :, :], ACT.Exp, scale=-1.0).then_inc(s["ez"], 1)
                    need(act, z_ps[1], i + 2)
                    need(act, s["upd"], i + 1)
                    act.activation(tin[:, :, :], chunks(ps_z[1]), ACT.Tanh).then_inc(s["tin"], 1)
                    need(act, s["ez"], i + 2)
                    need(act, s["sp"], i + 1)
                    act.activation(lz[:, :, :], ez[:, :, :], ACT.Ln, bias=1.0).then_inc(s["lz"], 1)
                    need(act, z_ps[2], i + 2)
                    act.activation(tsel[:, :, :], chunks(ps_z[2]), ACT.Tanh, scale=0.5).then_inc(s["tsel"], 1)
                    need(act, z_ps[3], i + 2)
                    need(act, s["gated"], i)
                    act.activation(tgate[at.slot(1, 2)][:, :, :], chunks(ps_z[3]), ACT.Tanh, scale=0.5).then_inc(s["tgate"], 1)
            sequences(act, body)

        @block.vector
        def _(dve):
            dve.wait_ge(s["th"], 1)
            dve.tensor_scalar(minus_a[:, :], th[:, :], -0.5, -0.5, ALU.mult, ALU.add).then_inc(s["a"], 1)
            dve.wait_ge(s["a"], 1)

            def body(at):
                i = at.i
                if at.on(3):
                    need(dve, x_landed[at.slot(3, 2)], at.landed(3, 2))
                    need(dve, pick_landed[0][at.slot(3, 2)], at.landed(3, 2))
                    need(dve, n3.y_sb, i + 3)
                    dve.memset(n3.tick[:, :], 0.0)
                    dve.scalar_tensor_tensor(part[:, :], pick[0][at.slot(3, 2)][:, :], routes.weight[:, 0, bass.ds(i + 3, 1)], x[at.slot(3, 2)][:, :], ALU.mult, ALU.add).then_inc(s["part"], 1)
                if at.on(0):
                    need(dve, s["decay"], i + 1)
                    need(dve, s["upd"], i + 1)
                    need(dve, s["gated"], i)
                    for c in range(KC):
                        done = dve.tensor_tensor_scan(state[:, c, :], decay[:, c, :], upd[:, c, :], 0.0, ALU.mult, ALU.add)
                    done.then_inc(s["state"], 1)
                if at.on(3):
                    need(dve, s["part"], i + 4)
                    need(dve, pick_landed[1][at.slot(3, 2)], at.landed(3, 2))
                    need(dve, n3.normed, i + 3)
                    dve.memset(n3.tick[:, :], 0.0)
                    dve.scalar_tensor_tensor(n3.y[:, :], pick[1][at.slot(3, 2)][:, :], routes.weight[:, 1, bass.ds(i + 3, 1)], part[:, :], ALU.mult, ALU.add).then_inc(n3.y_sb, 1)
                if at.on(0):
                    need(dve, s["state"], i + 1)
                    need(dve, s["tgate"], i + 1)
                    need(dve, s["y_ps"], i - 1)
                    dve.scalar_tensor_tensor(gated[at.slot(0, 2)][:, :, :], tgate[at.slot(0, 2)][:, :, :], 1.0, state[:, :, :], ALU.add, ALU.mult).then_inc(s["gated"], 1)
                if at.on(3):
                    n3.vector_sums(dve, i + 4)
                if at.on(-1):
                    need(dve, s["y_ps"], i)
                    need(dve, n4.normed, i - 1)
                    dve.scalar_tensor_tensor(n4.y[:, :], ps_y[0:ROWS, 0:D], 0.25, x3[at.slot(-1)][:, :], ALU.mult, ALU.add).then_inc(n4.y_sb, 1)
                if at.on(3):
                    n3.vector_mean(dve, i + 4)
                if at.on(-1):
                    n4.vector_sums(dve, i)
                if at.on(3):
                    n3.vector_variance(dve, i + 4)
                if at.on(-1):
                    n4.vector_mean(dve, i)
                if at.on(1):
                    need(dve, s["lz"], i + 2)
                    need(dve, z_ps[0], i + 2)
                    need(dve, s["delta"], i + 1)
                    dve.scalar_tensor_tensor(sp_[:, :, :], chunks(ps_d[at.slot(1, 2)]), 0.0, lz[:, :, :], ALU.max, ALU.add).then_inc(s["sp"], 1)
                if at.on(-1):
                    n4.vector_variance(dve, i)
                if at.on(3):
                    need(dve, n4.y_sb, i)
                    n3.vector_scale(dve, i + 4, x3[at.slot(3)][:, :])
                if at.on(1):
                    need(dve, s["sp"], i + 2)
                    need(dve, s["decay"], i + 1)
                    dve.tensor_scalar(delta[:, :, :], sp_[:, :, :], 1e-4, None, ALU.max).then_inc(s["delta"], 1)
                if at.on(1):
                    need(dve, s["tsel"], i + 2)
                    need(dve, s["state"], i + 1)
                    dve.scalar_tensor_tensor(upd[:, :, :], tsel[:, :, :], 1.0, tin[:, :, :], ALU.add, ALU.mult).then_inc(s["upd"], 1)
                if at.on(-1):
                    if at.on(-3):
                        need(dve, stored[at.slot(-1, 2)], at.landed(-3, 2))
                    n4.vector_scale(dve, i, xo[at.slot(-1, 2)][:, :])
            sequences(dve, body)
    st.end()


def gelu_experts(nc, dram, routes, weights, xs, ys):
    st = Stage(nc, "ff1")
    T = routes.tiles
    both, ring = (0, 1), range(4)
    w1, w2, gb = (weights.t[n] for n in ("w1", "w2", "gb"))
    b1, b2 = weights.bias
    ones = st.sb("ones", [weights.BIAS_ROWS, P])
    ones_r = st.sb("ones_r", [weights.BIAS_ROWS, P], F32R)
    ident = st.sb("ident", [P, P])
    minus_half = st.sb("minus_half", [P, 1])
    x = [st.sb(f"x{k}", [P, D]) for k in ring]
    xT = [st.sb(f"xT{k}", [P, KC, P]) for k in both]
    stat = st.sb("stat", [P, 6])
    mv = [st.sb(f"mv{k}", [P, 2]) for k in both]
    ve = [st.sb(f"ve{k}", [P, 1]) for k in both]
    rstd = [st.sb(f"rstd{k}", [P, 1]) for k in both]
    tick = st.sb("tick", [P, 1])
    hn = st.sb("hn", [P, F1])
    hg = st.sb("hg", [P, F1])
    hb = [st.sb(f"hb{k}", [P, F1]) for k in both]
    ha = [st.sb(f"ha{k}", [P, F1]) for k in both]
    hT = [st.sb(f"hT{k}", [P, KC, P]) for k in both]
    y = [st.sb(f"y{k}", [P, D]) for k in ring]
    ps_x = st.ps("ps_x", [P, BANK])
    ps_h = [st.ps(f"ps_h{k}", [P, BANK]) for k in both]
    ps_t = st.ps("ps_t", [P, BANK])
    ps_y = [st.ps(f"ps_y{k}", [P, BANK]) for k in both]
    s = {n: st.sem(n) for n in ("w_in", "half", "xT_ps", "xT_sb", "h_ps", "stat", "mv", "ve", "rstd", "hn", "hg", "hb", "ha", "hT_ps", "hT_sb", "y_ps", "y_sb")}
    x_landed, stored = ([st.sem(f"{n}{k}") for k in ring] for n in ("x_landed", "stored"))

    def tiles(eng, body, ahead=2):
        pipeline(eng, T, ahead, 2, 6, body, ring=4)

    with st.block() as block:
        @block.sync
        def _(sp):
            sp.dma_start(ident[:, :], dram["ident"]).then_inc(s["w_in"], 16)

            def body(at):
                i = at.i
                if at.on(4):
                    need(sp, s["xT_ps"], i + 1)
                    sp.dma_start(x[at.slot(4)][:, :], xs[i + 4]).then_inc(x_landed[at.slot(4)], 16)
                if at.on(-2):
                    need(sp, s["y_sb"], i - 1)
                    sp.dma_start(ys[i - 2], y[at.slot(-2)][:, :]).then_inc(stored[at.slot(-2)], 16)
            tiles(sp, body, 4)
            for k in ring:
                sp.wait_ge(stored[k], 16 * (T // 4))

        @block.gpsimd
        def _(pool):
            pool.memset(minus_half[:, :], -0.5).then_inc(s["half"], 1)
            pool.memset(ones[:, :], 1.0).then_inc(s["half"], 1)
            pool.wait_ge(s["half"], 2)
            pool.tensor_copy(ones_r[:, :], ones[:, :]).then_inc(s["half"], 1)

            def body(at):
                i = at.i
                if at.on(1):
                    need(pool, s["ve"], i + 2)
                    need(pool, s["hn"], i)
                    pool.tensor_tensor(rstd[at.slot(1, 2)][:, :], ve[at.slot(1, 2)][:, :], minus_half[:, :], ALU.pow).then_inc(s["rstd"], 1)
            tiles(pool, body)

        @block.tensor
        def _(pe):
            pe.wait_ge(s["w_in"], 16)
            pe.wait_ge(weights.landed[0], 16 * len(weights.t))
            pe.wait_ge(s["half"], 3)
            pe.wait_ge(weights.b_split, 2)

            def body(at):
                i = at.i
                if at.on(1):
                    expert = pe.value_load(routes.expert[0:1, bass.ds(i + 1, 1)], min_val=0, max_val=E1 - 1)
                if at.on(-2):
                    past = pe.value_load(routes.expert[0:1, bass.ds(i - 2, 1)], min_val=0, max_val=E1 - 1)
                if at.on(2):
                    need(pe, x_landed[at.slot(2)], at.landed(2))
                    need(pe, s["xT_sb"], i + 2)
                    for c in range(KC):
                        done = pe.transpose(ps_x[:, c * P:(c + 1) * P], x[at.slot(2)][:, c * P:(c + 1) * P], ident[:, :])
                    done.then_inc(s["xT_ps"], 1)
                if at.on(1):
                    need(pe, s["xT_sb"], i + 2)
                    need(pe, s["hn"], i)
                    for c in range(KC):
                        pe.matmul(ps_h[at.slot(1, 2)][:, 0:F1], xT[at.slot(1, 2)][:, c, :], w1[:, expert, c, :], start=c == 0, stop=False)
                    pe.matmul(ps_h[at.slot(1, 2)][:, 0:F1], ones_r[:, :], b1[:, expert, :], start=False, stop=True).then_inc(s["h_ps"], 1)
                if at.on(-1):
                    need(pe, s["ha"], i)
                    need(pe, s["hT_sb"], i - 1)
                    for c in range(KC):
                        done = pe.transpose(ps_t[:, c * P:(c + 1) * P], ha[at.slot(-1, 2)][:, c * P:(c + 1) * P], ident[:, :])
                    done.then_inc(s["hT_ps"], 1)
                if at.on(-2):
                    need(pe, s["hT_sb"], i - 1)
                    need(pe, s["y_sb"], i - 3)
                    for c in range(KC):
                        pe.matmul(ps_y[at.slot(-2, 2)][:, 0:D], hT[at.slot(-2, 2)][:, c, :], w2[:, past, c, :], start=c == 0, stop=False)
                    pe.matmul(ps_y[at.slot(-2, 2)][:, 0:D], ones_r[:, :], b2[:, past, :], start=False, stop=True).then_inc(s["y_ps"], 1)
            tiles(pe, body)

        @block.scalar
        def _(act):
            def body(at):
                i = at.i
                if at.on(2):
                    need(act, s["xT_ps"], i + 3)
                    need(act, s["h_ps"], i + 1)
                    act.activation(xT[at.slot(2, 2)][:, :, :], ps_x[:, 0:D].rearrange("p (c n) -> p c n", c=KC), ACT.Copy).then_inc(s["xT_sb"], 1)
                if at.on(-1):
                    need(act, s["hT_ps"], i)
                    need(act, s["y_ps"], i - 3)
                    act.activation(hT[at.slot(-1, 2)][:, :, :], ps_t[:, 0:F1].rearrange("p (c n) -> p c n", c=KC), ACT.Copy).then_inc(s["hT_sb"], 1)
                if at.on(0):
                    need(act, s["hb"], i + 1)
                    need(act, s["hT_ps"], i - 1)
                    act.activation(ha[at.slot(0, 2)][:, :], hb[at.slot(0, 2)][:, :], ACT.Gelu).then_inc(s["ha"], 1)
                if at.on(-2):
                    need(act, s["y_ps"], i - 1)
                    if at.on(-6):
                        need(act, stored[at.slot(-2)], at.landed(-6))
                    act.activation(y[at.slot(-2)][:, :], ps_y[at.slot(-2, 2)][:, 0:D], ACT.Copy).then_inc(s["y_sb"], 1)
            tiles(act, body)

        @block.vector
        def _(dve):
            dve.wait_ge(weights.landed[0], 16 * len(weights.t))

            def body(at):
                i = at.i
                if at.on(0):
                    expert = dve.value_load(routes.expert[0:1, bass.ds(i, 1)], min_val=0, max_val=E1 - 1)
                if at.on(1):
                    need(dve, s["h_ps"], i + 2)
                    dve.bn_stats(stat[:, :], ps_h[at.slot(1, 2)][:, 0:F1]).then_inc(s["stat"], 1)
                if at.on(0):
                    need(dve, s["rstd"], i + 1)
                    need(dve, s["hg"], i)
                    dve.tensor_scalar(hn[:, :], ps_h[at.slot(0, 2)][:, 0:F1], mv[at.slot(0, 2)][:, 0:1], rstd[at.slot(0, 2)][:, 0:1], ALU.subtract, ALU.mult).then_inc(s["hn"], 1)
                if at.on(1):
                    need(dve, s["stat"], i + 2)
                    dve.memset(tick[:, :], 0.0)
                    dve.bn_aggr(mv[at.slot(1, 2)][:, :], stat[:, :]).then_inc(s["mv"], 1)
                if at.on(0):
                    need(dve, s["hn"], i + 1)
                    need(dve, s["hb"], i)
                    dve.tensor_tensor(hg[:, :], hn[:, :], gb[:, 0, expert, :], ALU.mult).then_inc(s["hg"], 1)
                if at.on(1):
                    need(dve, s["mv"], i + 2)
                    need(dve, s["rstd"], i)
                    dve.tensor_scalar(ve[at.slot(1, 2)][:, :], mv[at.slot(1, 2)][:, 1:2], LN_EPS, None, ALU.add).then_inc(s["ve"], 1)
                if at.on(0):
                    need(dve, s["hg"], i + 1)
                    need(dve, s["ha"], i - 1)
                    dve.tensor_tensor(hb[at.slot(0, 2)][:, :], hg[:, :], gb[:, 1, expert, :], ALU.add).then_inc(s["hb"], 1)
            tiles(dve, body)
    st.end()


def combine(nc, routes, x_in, ys, out):
    st = Stage(nc, "fin")
    both, ring = (0, 1), range(4)
    x = [st.sb(f"x{k}", [ROWS, D]) for k in both]
    pick = [[st.sb(f"pick{n}_{k}", [ROWS, D]) for k in ring] for n in both]
    part = st.sb("part", [ROWS, D])
    minus_half = st.sb("minus_half", [P, 1])
    tick = st.sb("tick", [ROWS, 1])
    xo = [st.sb(f"xo{k}", [ROWS, D]) for k in both]
    nm = Norm(st, "nm")
    half_set, part_done = st.sem("half"), st.sem("part")
    x_landed, stored = ([st.sem(f"{n}{k}") for k in both] for n in ("x_landed", "stored"))
    pick_landed = [[st.sem(f"pick_landed{n}_{k}") for k in ring] for n in both]

    with st.block() as block:
        @block.sync
        def _(sp):
            def body(at):
                i = at.i
                if at.on(2):
                    need(sp, part_done, i + 1)
                    sp.dma_start(x[at.slot(2, 2)][:, :], x_in[i + 2]).then_inc(x_landed[at.slot(2, 2)], 16)
                if at.on(-1):
                    need(sp, nm.normed, i)
                    sp.dma_start(out[i - 1], xo[at.slot(-1, 2)][:, :]).then_inc(stored[at.slot(-1, 2)], 16)
            pipeline(sp, SEQS, 2, 1, 3, body, ring=4)
            for k in both:
                sp.wait_ge(stored[k], landed(SEQS // 2 - 1))

        @block.gpsimd
        def _(pool):
            pool.memset(minus_half[:, :], -0.5).then_inc(half_set, 1)
            pool.wait_ge(half_set, 1)

            def fetch(b):
                if b >= 4:
                    pool.wait_ge(nm.y_sb, b - 3)
                for n in both:
                    pool.indirect_dma_start(pick[n][b % 4][:, :], None, ys, bass.IndirectOffsetOnAxis(ap=routes.slot[:, n, b:b + 1], axis=0)).then_inc(pick_landed[n][b % 4], 16)
            for b in range(3):
                fetch(b)
            for b in range(SEQS):
                if b + 3 < SEQS:
                    fetch(b + 3)
                nm.pool_rstd(pool, b + 1, minus_half[0:ROWS, :])

        @block.vector
        def _(dve):
            def body(at):
                i, par = at.i, at.slot(0, 2)
                if at.on(0):
                    need(dve, part_done, i + 1)
                    need(dve, pick_landed[1][at.slot(0)], at.landed(0))
                    need(dve, nm.normed, i)
                    dve.memset(tick[:, :], 0.0)
                    dve.scalar_tensor_tensor(nm.y[:, :], pick[1][at.slot(0)][:, :], routes.weight[:, 1, bass.ds(i, 1)], part[:, :], ALU.mult, ALU.add).then_inc(nm.y_sb, 1)
                    nm.vector_stats(dve, i + 1)
                if at.on(1):
                    need(dve, x_landed[1 - par], at.landed(1, 2))
                    need(dve, pick_landed[0][at.slot(1)], at.landed(1))
                    dve.memset(tick[:, :], 0.0)
                    dve.scalar_tensor_tensor(part[:, :], pick[0][at.slot(1)][:, :], routes.weight[:, 0, bass.ds(i + 1, 1)], x[1 - par][:, :], ALU.mult, ALU.add).then_inc(part_done, 1)
                if at.on(0):
                    need(dve, stored[par], at.landed(-2, 2))
                    nm.vector_scale(dve, i + 1, xo[par][:, :])
            pipeline(dve, SEQS, 1, 0, 3, body, ring=4)
    st.end()


def decoder(nc, dram, out):
    def scratch(name, shape):
        return nc.dram_tensor(name, shape, F32, kind="Internal").ap()

    x1, x2, x4, x5 = (scratch(f"x{n}", [SEQS, ROWS, D]) for n in (1, 2, 4, 5))
    xs, ys = (scratch(n, [FFN1_TILES, P, D]) for n in ("xs", "ys"))
    xs_rows, ys0_rows, ys_rows = (t.rearrange("t p d -> (t p) d") for t in (xs, ys[0:FFN0_TILES], ys))

    with ExitStack() as stack:
        early = CrossAttentionEarly(nc, stack, "xa0")
        self_attention(nc, dram, dram["x"], x1, xs, early)
        cross_attention(nc, dram, "xa0", early, x1, x2)
        early.end()
    with ExitStack() as stack:
        early = recurrence_early(nc, stack), CrossAttentionEarly(nc, stack, "xa1")
        with ExitStack() as routed:
            routes = Routes(nc, routed, "r0", E0, FFN0_TILES)
            with ExitStack() as held:
                weights = ReluWeights(nc, held)
                router(nc, dram, routes, weights, x2, xs_rows, F32_EPS, 0.0, False)
                relu_experts(nc, dram, routes, weights, xs, ys, early[0])
                weights.end()
            recurrence(nc, dram, routes, early[0], x2, ys0_rows, x4, early[1])
            early[0].end()
        cross_attention(nc, dram, "xa1", early[1], x4, x5, dram["mask"])
        early[1].end()
    with ExitStack() as stack:
        routes = Routes(nc, stack, "r1", E1, FFN1_TILES)
        with ExitStack() as held:
            weights = GeluWeights(nc, held)
            router(nc, dram, routes, weights, x5, xs_rows, 0.0, 1e-9, True)
            gelu_experts(nc, dram, routes, weights, xs, ys)
            weights.end()
        combine(nc, routes, x5, ys_rows, out)


def layout(inputs):
    f32 = np.float32
    a = {k: np.asarray(v) for k, v in inputs.items()}

    def chunked(w):
        return w.reshape(-1, P, w.shape[-1]).transpose(1, 0, 2)

    def columns(b):
        return b.reshape(-1, P).T

    def every(b):
        return np.broadcast_to(b[None, :], (P, b.shape[0]))

    split = np.concatenate([np.arange(0, D, 2), np.arange(1, D, 2)])
    ipw, ipb = a["L0_attn_in_proj_w"], a["L0_attn_in_proj_b"]
    i = np.arange(D // 2, dtype=f32)
    theta = (f32(10000.0) ** (f32(-2.0) * (i - f32(1.0)) / f32(D))).astype(f32)
    angle = (theta[:, None] * np.arange(ROWS, dtype=f32)[None, :]).astype(f32)
    t = {
        "x": a["x"],
        "sa_w1": np.stack([chunked(a[f"L0_attn_w{c}"][split].T) for c in "qkv"], axis=1),
        "sa_w2": np.stack([chunked(ipw[n * D:(n + 1) * D][:, split].T) for n in range(3)], axis=1),
        "sa_wo": chunked(a["L0_attn_out_w"].T),
        "sa_bqk": np.stack([columns(ipb[0:D]), columns(ipb[D:2 * D])], axis=1),
        "sa_bv": every(ipb[2 * D:]),
        "sa_bo": every(a["L0_attn_out_b"]),
        "ident": np.eye(P, dtype=f32),
        "causal": np.where(np.tril(np.ones((ROWS, ROWS), bool)), f32(0), f32(MASKED)),
        "rope": np.stack([np.cos(angle), np.sin(angle)], axis=1).astype(f32),
        "head_mask": (np.arange(P)[:, None] // HD == np.arange(HPC)[None, :]).astype(f32),
    }
    t["tile_head_mask"] = (np.arange(P)[:, None] % 64 // HD == np.arange(QH)[None, :]).astype(f32) * f32(HD ** -0.5)
    twice = np.arange(D).reshape(QT, 1, 64).repeat(2, axis=1).reshape(-1)
    t["ctxT"] = a["ctx_1024"].reshape(SEQS, KEYS, KC, P).transpose(0, 3, 2, 1)
    t["mask"] = a["mask_Bx1xSxS2_ik1"].reshape(SEQS, ROWS, KEYS)
    for n, w, b, turn in (("xa0", "L0_xattn_w{}_w", "L0_xattn_w{}_b", True), ("xa1", "L1_xattn_w{}", "L1_xattn_b{}", False)):
        for c in "qkvo":
            wn, bn = (("L0_xattn_dense_w", "L0_xattn_dense_b") if turn and c == "o" else (w.format(c), b.format(c)))
            t[f"{n}_w{c}"] = chunked(a[wn].T if turn else a[wn])
            t[f"{n}_b{c}"] = a[bn]
        t[f"{n}_wq"] = t[f"{n}_wq"][:, :, twice].reshape(P, KC, QT, P)
        t[f"{n}_bq"] = t[f"{n}_bq"][twice].reshape(QT, P).T
        t[f"{n}_bk"] = columns(t[f"{n}_bk"])
        for c in "vo":
            t[f"{n}_b{c}"] = every(t[f"{n}_b{c}"])
    t["before"] = np.triu(np.ones((ROWS, ROWS), f32), 1)
    t["iota"] = np.broadcast_to(np.arange(P, dtype=f32)[None, :], (P, P))
    for n, e in (("r0", E0), ("r1", E1)):
        t[f"{n}_chain"] = np.broadcast_to((np.arange(SEQS) > 0).astype(f32)[None, None, :], (P, e, SEQS))
    t["r0_wr"] = chunked(a["L0_ffn_Wr"].T)
    t["r0_br"] = np.zeros((P, E0), f32)
    t["r1_wr"] = chunked(a["L1_ffn_Wr"])
    t["r1_br"] = every(a["L1_ffn_br"])
    t["ff0_w"] = np.concatenate([a[f"L0_ffn_W{c}"].transpose(0, 2, 1).reshape(E0, KC, P, F0).transpose(0, 2, 1, 3).reshape(E0, P, KC * F0) for c in "gu"]
                                + [a["L0_ffn_Wd"].transpose(0, 2, 1).reshape(E0, F0 // P, P, D).transpose(0, 2, 1, 3).reshape(E0, P, F0 // P * D)], axis=2)
    t["rec_win"] = np.stack([chunked(a[f"L1_attn_W_{n}"].T) for n in ("delta", "in", "select", "gate")], axis=1)
    t["rec_wout"] = chunked(a["L1_attn_W_out"].T)
    t["rec_la"] = columns(a["L1_attn_log_a"])
    for n in (1, 2):
        t[f"ff1_w{n}"] = a[f"L1_ffn_W{n}"].reshape(E1, KC, P, -1).transpose(2, 0, 1, 3)
        t[f"ff1_b{n}"] = a[f"L1_ffn_b{n}"][None]
    t["ff1_gb"] = np.broadcast_to(np.stack([a["L1_ffn_g1"], a["L1_ffn_be1"]])[None], (P, 2, E1, F1))
    return {k: np.ascontiguousarray(v) for k, v in t.items()}


def kernel(**inputs):
    import concourse.bacc as bacc
    from concourse.bass_utils import run_bass_kernel_spmd

    nc = bacc.Bacc("TRN2", target_bir_lowering=False, num_devices=1)
    arrays = {f"in_{k}": v for k, v in layout(inputs).items()}
    dram = {k[3:]: nc.dram_tensor(k, v.shape, mybir.dt.from_np(v.dtype), kind="ExternalInput").ap() for k, v in arrays.items()}
    out = nc.dram_tensor("out", (SEQS, ROWS, D), F32, kind="ExternalOutput").ap()
    decoder(nc, dram, out)
    r = run_bass_kernel_spmd(nc, [arrays], core_ids=[0])
    return r.results[0]["out"]
```
